# Optimizing a Trainium2 kernel written in Bass

```python
import numpy as np
import jax
import jax.numpy as jnp

def _softmax(x, axis=-1):
    return jax.nn.softmax(x, axis=axis)

def _gelu(x):
    return jax.nn.gelu(x, approximate=True)

def _silu(x):
    return jax.nn.silu(x)

def _sigmoid(x):
    return jax.nn.sigmoid(x)

def _layernorm(x, axis=-1, eps=1e-05):
    m = jnp.mean(x, axis=axis, keepdims=True)
    v = jnp.var(x, axis=axis, keepdims=True)
    return (x - m) / jnp.sqrt(v + eps)

def _scatter_add(tgt, idx, src, axis=0):
    return tgt.at[idx].add(src)

def _segment_sum(src, seg, n):
    return jax.ops.segment_sum(src, seg, n)
kernel_name = 'mk_vit_tower_postln_d2_tok_img1024_r4_d89858'

def setup_inputs(seed: int=0):
    np.random.seed(seed)
    _w = jnp.asarray

    def _rec_inputs():
        import jax
        import jax.numpy as jnp
        _rk = jax.random.key(seed)
        x = -0.00016672 + 0.999947 * jax.random.normal(jax.random.fold_in(_rk, 1), (16, 96, 96, 3), jnp.float32)
        return x
    x = _rec_inputs()

    def _L0_tok_setup():
        import jax, jax.numpy as jnp
        import numpy as np
        P = 16
        E = 256

        def patchify(images, patch_size):
            B, H, W, C = images.shape
            hp, wp = (H // patch_size, W // patch_size)
            x = images.reshape(B, hp, patch_size, wp, patch_size, C)
            x = x.transpose(0, 1, 3, 2, 4, 5)
            return x.reshape(B, hp * wp, patch_size * patch_size * C)
        key = jax.random.key(seed)
        k_img, k_w, k_b, k_pos = jax.random.split(key, 4)
        B, H, W, C = (64, 96, 96, 3)
        patch_dim = P * P * C
        patch_count = H // P * (W // P)
        images = jax.random.normal(k_img, (B, H, W, C), dtype=jnp.float32)
        W_proj = jax.random.normal(k_w, (E, patch_dim), dtype=jnp.float32) * patch_dim ** (-0.5)
        b_proj = jax.random.normal(k_b, (E,), dtype=jnp.float32) * 0.02
        pos_emb = jax.random.normal(k_pos, (patch_count, E), dtype=jnp.float32) * 0.02
        return {'images': images, 'W_proj': W_proj, 'b_proj': b_proj, 'pos_emb': pos_emb}
    _L0_tok_all = _L0_tok_setup()
    _L0_tok_in = {k: v for k, v in _L0_tok_all.items() if k in ('W_proj', 'b_proj', 'pos_emb')}
    del _L0_tok_all

    def _L0_attn_setup():
        import jax, jax.numpy as jnp
        import numpy as np
        HEADS = 16
        LN_EPS = 1e-05

        def _ln(v, w, b):
            mu = jnp.mean(v, axis=-1, keepdims=True)
            var = jnp.mean(jnp.square(v - mu), axis=-1, keepdims=True)
            return (v - mu) * jax.lax.rsqrt(var + LN_EPS) * w + b
        key = jax.random.key(seed)
        ks = jax.random.split(key, 5)
        b, t, e = (2, 512, 256)
        x = jax.random.normal(ks[0], (b, t, e), dtype=jnp.float32)
        scale = 0.02
        Wk = jax.random.normal(ks[1], (e, e), dtype=jnp.float32) * scale
        Wq = jax.random.normal(ks[2], (e, e), dtype=jnp.float32) * scale
        Wv = jax.random.normal(ks[3], (e, e), dtype=jnp.float32) * scale
        Wu = jax.random.normal(ks[4], (e, e), dtype=jnp.float32) * scale
        s = e // HEADS
        return {'x': x, 'Wk': Wk, 'Wq': Wq, 'Wv': Wv, 'Wu': Wu, 'kln_w': jnp.ones((s,), jnp.float32), 'kln_b': jnp.zeros((s,), jnp.float32), 'qln_w': jnp.ones((s,), jnp.float32), 'qln_b': jnp.zeros((s,), jnp.float32)}
    _L0_attn_all = _L0_attn_setup()
    _L0_attn_in = {k: v for k, v in _L0_attn_all.items() if k in ('Wk', 'Wq', 'Wv', 'Wu', 'kln_w', 'kln_b', 'qln_w', 'qln_b')}
    del _L0_attn_all

    def _L0_ffn_setup():
        import jax, jax.numpy as jnp
        import numpy as np
        B, S, DIM = (4, 1024, 256)
        BASE_COUPLING = 0.1
        NUM_CYCLES = 3

        def _gelu(x):
            return jax.nn.gelu(x, approximate=False)

        def _coupling_net(h, w1, b1, w2, b2, w3, b3, w4, b4):
            h = _gelu(h @ w1 + b1)
            h = _gelu(h @ w2 + b2)
            h = _gelu(h @ w3 + b3)
            return jax.nn.sigmoid(h @ w4 + b4)

        def _global_net(h, w1, b1, w2, b2, w3, b3):
            h = _gelu(h @ w1 + b1)
            h = _gelu(h @ w2 + b2)
            return jax.nn.sigmoid(h @ w3 + b3)

        def _twist(x):
            o_r, o_i, p_r, p_i = jnp.split(x, 4, axis=-1)
            return jnp.concatenate([p_r, -p_i, -o_r, o_i], axis=-1)
        key = jax.random.key(seed)
        ks = jax.random.split(key, 9)
        d = DIM

        def w(k, fan_in, fan_out):
            return jax.random.normal(k, (fan_in, fan_out), dtype=jnp.float32) / np.sqrt(fan_in).astype(np.float32)
        inp = {'x': jax.random.normal(ks[0], (B, S, d), dtype=jnp.float32)}
        cn_dims = [(d, d), (d, d // 2), (d // 2, d // 4), (d // 4, 1)]
        for i, (a, b) in enumerate(cn_dims):
            inp[f'cn_w{i + 1}'] = w(ks[1 + i], a, b)
            inp[f'cn_b{i + 1}'] = jnp.zeros((b,), dtype=jnp.float32)
        gc_dims = [(d, d // 2), (d // 2, d // 4), (d // 4, 1)]
        for i, (a, b) in enumerate(gc_dims):
            inp[f'gc_w{i + 1}'] = w(ks[5 + i], a, b)
            inp[f'gc_b{i + 1}'] = jnp.zeros((b,), dtype=jnp.float32)
        inp['adaptive_range'] = jnp.full((1,), 0.2, dtype=jnp.float32)
        return inp
    _L0_ffn_all = _L0_ffn_setup()
    _L0_ffn_in = {k: v for k, v in _L0_ffn_all.items() if k in ('cn_w1', 'cn_b1', 'cn_w2', 'cn_b2', 'cn_w3', 'cn_b3', 'cn_w4', 'cn_b4', 'gc_w1', 'gc_b1', 'gc_w2', 'gc_b2', 'gc_w3', 'gc_b3', 'adaptive_range')}
    del _L0_ffn_all

    def _L1_attn_setup():
        import jax, jax.numpy as jnp
        import numpy as np
        D_MODEL = 256
        HEADS = 16
        D_K = D_MODEL // HEADS
        ROPE_BASE = 10000.0

        def _rope(x, pos_offset=0):
            S, d = (x.shape[-2], x.shape[-1])
            inv_freq = 1.0 / ROPE_BASE ** (jnp.arange(0, d, 2, dtype=jnp.float32) / d)
            pos = jnp.arange(S, dtype=jnp.float32) + pos_offset
            ang = pos[:, None] * inv_freq[None, :]
            cos, sin = (jnp.cos(ang), jnp.sin(ang))
            x1, x2 = (x[..., :d // 2], x[..., d // 2:])
            return jnp.concatenate([x1 * cos - x2 * sin, x1 * sin + x2 * cos], axis=-1)
        key = jax.random.key(seed)
        ks = jax.random.split(key, 5)
        B, S = (2, 512)
        x = jax.random.normal(ks[0], (B, S, D_MODEL), dtype=jnp.float32)
        w = lambda k: jax.random.normal(k, (D_MODEL, D_MODEL), dtype=jnp.float32) * 0.02
        z = jnp.zeros((D_MODEL,), dtype=jnp.float32)
        return {'x': x, 'Wq': w(ks[1]), 'bq': z, 'Wk': w(ks[2]), 'bk': z, 'Wv': w(ks[3]), 'bv': z, 'Wo': w(ks[4]), 'bo': z}
    _L1_attn_all = _L1_attn_setup()
    _L1_attn_in = {k: v for k, v in _L1_attn_all.items() if k in ('Wq', 'bq', 'Wk', 'bk', 'Wv', 'bv', 'Wo', 'bo')}
    del _L1_attn_all

    def _L1_ffn_setup():
        import jax, jax.numpy as jnp
        import numpy as np
        B, L, D = (1, 512, 256)
        E, H, G, K = (64, 64, 64, 16)

        def _grouped_routing_scores(router_scores):
            T, En = router_scores.shape
            Tq = T // G
            budget = Tq * K
            order = jnp.argsort(-router_scores, axis=0)
            sorted_vals = jnp.take_along_axis(router_scores, order, axis=0)
            group_score = sorted_vals.reshape(Tq, G, En).sum(axis=1)
            _, top_flat = jax.lax.top_k(group_score.reshape(-1), budget)
            gmask = jnp.zeros((Tq * En,), bool).at[top_flat].set(True).reshape(Tq, En)
            mask_sorted = jnp.broadcast_to(gmask[:, None, :], (Tq, G, En)).reshape(T, En)
            mask = jnp.zeros((T, En), bool).at[order, jnp.arange(En)[None, :]].set(mask_sorted)
            fs = jnp.where(mask, router_scores, 0.0)
            return fs / (fs.sum(axis=-1, keepdims=True) + 1e-06)
        key = jax.random.key(seed)
        ks = jax.random.split(key, 6)
        s = lambda k, shape, scale: jax.random.normal(k, shape, jnp.float32) * scale
        return {'x': jax.random.normal(ks[0], (B, L, D), jnp.float32), 'Wr': s(ks[1], (D, E), D ** (-0.5)), 'br': jnp.zeros((E,), jnp.float32), 'Wup': s(ks[2], (E, D, H), D ** (-0.5)), 'bup': jnp.zeros((E, H), jnp.float32), 'Wgate': s(ks[3], (E, D, H), D ** (-0.5)), 'bgate': jnp.zeros((E, H), jnp.float32), 'Wdown': s(ks[4], (E, H, D), H ** (-0.5)), 'bdown': jnp.zeros((E, D), jnp.float32)}
    _L1_ffn_all = _L1_ffn_setup()
    _L1_ffn_in = {k: v for k, v in _L1_ffn_all.items() if k in ('Wr', 'br', 'Wup', 'bup', 'Wgate', 'bgate', 'Wdown', 'bdown')}
    del _L1_ffn_all
    return {'x': x, 'L0_tok_W_proj': _L0_tok_in['W_proj'], 'L0_tok_b_proj': _L0_tok_in['b_proj'], 'L0_tok_pos_emb': _L0_tok_in['pos_emb'], 'L0_attn_Wk': _L0_attn_in['Wk'], 'L0_attn_Wq': _L0_attn_in['Wq'], 'L0_attn_Wv': _L0_attn_in['Wv'], 'L0_attn_Wu': _L0_attn_in['Wu'], 'L0_attn_kln_w': _L0_attn_in['kln_w'], 'L0_attn_kln_b': _L0_attn_in['kln_b'], 'L0_attn_qln_w': _L0_attn_in['qln_w'], 'L0_attn_qln_b': _L0_attn_in['qln_b'], 'L0_ffn_cn_w1': _L0_ffn_in['cn_w1'], 'L0_ffn_cn_b1': _L0_ffn_in['cn_b1'], 'L0_ffn_cn_w2': _L0_ffn_in['cn_w2'], 'L0_ffn_cn_b2': _L0_ffn_in['cn_b2'], 'L0_ffn_cn_w3': _L0_ffn_in['cn_w3'], 'L0_ffn_cn_b3': _L0_ffn_in['cn_b3'], 'L0_ffn_cn_w4': _L0_ffn_in['cn_w4'], 'L0_ffn_cn_b4': _L0_ffn_in['cn_b4'], 'L0_ffn_gc_w1': _L0_ffn_in['gc_w1'], 'L0_ffn_gc_b1': _L0_ffn_in['gc_b1'], 'L0_ffn_gc_w2': _L0_ffn_in['gc_w2'], 'L0_ffn_gc_b2': _L0_ffn_in['gc_b2'], 'L0_ffn_gc_w3': _L0_ffn_in['gc_w3'], 'L0_ffn_gc_b3': _L0_ffn_in['gc_b3'], 'L0_ffn_adaptive_range': _L0_ffn_in['adaptive_range'], 'L1_attn_Wq': _L1_attn_in['Wq'], 'L1_attn_bq': _L1_attn_in['bq'], 'L1_attn_Wk': _L1_attn_in['Wk'], 'L1_attn_bk': _L1_attn_in['bk'], 'L1_attn_Wv': _L1_attn_in['Wv'], 'L1_attn_bv': _L1_attn_in['bv'], 'L1_attn_Wo': _L1_attn_in['Wo'], 'L1_attn_bo': _L1_attn_in['bo'], 'L1_ffn_Wr': _L1_ffn_in['Wr'], 'L1_ffn_br': _L1_ffn_in['br'], 'L1_ffn_Wup': _L1_ffn_in['Wup'], 'L1_ffn_bup': _L1_ffn_in['bup'], 'L1_ffn_Wgate': _L1_ffn_in['Wgate'], 'L1_ffn_bgate': _L1_ffn_in['bgate'], 'L1_ffn_Wdown': _L1_ffn_in['Wdown'], 'L1_ffn_bdown': _L1_ffn_in['bdown']}

def reference(x, L0_tok_W_proj, L0_tok_b_proj, L0_tok_pos_emb, L0_attn_Wk, L0_attn_Wq, L0_attn_Wv, L0_attn_Wu, L0_attn_kln_w, L0_attn_kln_b, L0_attn_qln_w, L0_attn_qln_b, L0_ffn_cn_w1, L0_ffn_cn_b1, L0_ffn_cn_w2, L0_ffn_cn_b2, L0_ffn_cn_w3, L0_ffn_cn_b3, L0_ffn_cn_w4, L0_ffn_cn_b4, L0_ffn_gc_w1, L0_ffn_gc_b1, L0_ffn_gc_w2, L0_ffn_gc_b2, L0_ffn_gc_w3, L0_ffn_gc_b3, L0_ffn_adaptive_range, L1_attn_Wq, L1_attn_bq, L1_attn_Wk, L1_attn_bk, L1_attn_Wv, L1_attn_bv, L1_attn_Wo, L1_attn_bo, L1_ffn_Wr, L1_ffn_br, L1_ffn_Wup, L1_ffn_bup, L1_ffn_Wgate, L1_ffn_bgate, L1_ffn_Wdown, L1_ffn_bdown):
    import jax
    import jax.numpy as jnp

    def _L0_tok_ref(images, W_proj, b_proj, pos_emb):
        import jax, jax.numpy as jnp
        import numpy as np
        P = 16
        E = 256

        def patchify(images, patch_size):
            B, H, W, C = images.shape
            hp, wp = (H // patch_size, W // patch_size)
            x = images.reshape(B, hp, patch_size, wp, patch_size, C)
            x = x.transpose(0, 1, 3, 2, 4, 5)
            return x.reshape(B, hp * wp, patch_size * patch_size * C)
        patches = patchify(images, P)
        out = jnp.einsum('bnd,ed->bne', patches, W_proj) + b_proj + pos_emb[None, :, :]
        return out

    def _L0_attn_ref(x, Wk, Wq, Wv, Wu, kln_w, kln_b, qln_w, qln_b):
        import jax, jax.numpy as jnp
        import numpy as np
        HEADS = 16
        LN_EPS = 1e-05

        def _ln(v, w, b):
            mu = jnp.mean(v, axis=-1, keepdims=True)
            var = jnp.mean(jnp.square(v - mu), axis=-1, keepdims=True)
            return (v - mu) * jax.lax.rsqrt(var + LN_EPS) * w + b
        b, t, e = x.shape
        h = HEADS
        s = e // h
        k = (x @ Wk.T).reshape(b, t, h, s)
        q = (x @ Wq.T).reshape(b, t, h, s)
        v = (x @ Wv.T).reshape(b, t, h, s)
        k = _ln(k, kln_w, kln_b)
        q = _ln(q, qln_w, qln_b)
        scalefactor = 1.0 / np.sqrt(s).astype(np.float32)
        dot = jnp.einsum('bqhs,bkhs->bhqk', q, k) * scalefactor
        causal = jnp.triu(jnp.ones((t, t), dtype=bool), k=1)
        dot = jnp.where(causal, -jnp.inf, dot)
        attn = jax.nn.softmax(dot, axis=-1)
        out = jnp.einsum('bhqk,bkhs->bqhs', attn, v).reshape(b, t, e)
        return out @ Wu.T

    def _L0_ffn_ref(x, cn_w1, cn_b1, cn_w2, cn_b2, cn_w3, cn_b3, cn_w4, cn_b4, gc_w1, gc_b1, gc_w2, gc_b2, gc_w3, gc_b3, adaptive_range):
        import jax, jax.numpy as jnp
        import numpy as np
        B, S, DIM = (4, 1024, 256)
        BASE_COUPLING = 0.1
        NUM_CYCLES = 3

        def _gelu(x):
            return jax.nn.gelu(x, approximate=False)

        def _coupling_net(h, w1, b1, w2, b2, w3, b3, w4, b4):
            h = _gelu(h @ w1 + b1)
            h = _gelu(h @ w2 + b2)
            h = _gelu(h @ w3 + b3)
            return jax.nn.sigmoid(h @ w4 + b4)

        def _global_net(h, w1, b1, w2, b2, w3, b3):
            h = _gelu(h @ w1 + b1)
            h = _gelu(h @ w2 + b2)
            return jax.nn.sigmoid(h @ w3 + b3)

        def _twist(x):
            o_r, o_i, p_r, p_i = jnp.split(x, 4, axis=-1)
            return jnp.concatenate([p_r, -p_i, -o_r, o_i], axis=-1)
        global_context = x.mean(axis=1, keepdims=True)
        gf = _global_net(global_context, gc_w1, gc_b1, gc_w2, gc_b2, gc_w3, gc_b3)
        out = x
        for _ in range(NUM_CYCLES):
            tf = _coupling_net(out, cn_w1, cn_b1, cn_w2, cn_b2, cn_w3, cn_b3, cn_w4, cn_b4)
            combined = 0.7 * gf + 0.3 * tf
            coupling = BASE_COUPLING + adaptive_range * (combined - 0.5) * 2.0
            out = out + coupling * _twist(out)
        return out

    def _L1_attn_ref(x, Wq, bq, Wk, bk, Wv, bv, Wo, bo):
        import jax, jax.numpy as jnp
        import numpy as np
        D_MODEL = 256
        HEADS = 16
        D_K = D_MODEL // HEADS
        ROPE_BASE = 10000.0

        def _rope(x, pos_offset=0):
            S, d = (x.shape[-2], x.shape[-1])
            inv_freq = 1.0 / ROPE_BASE ** (jnp.arange(0, d, 2, dtype=jnp.float32) / d)
            pos = jnp.arange(S, dtype=jnp.float32) + pos_offset
            ang = pos[:, None] * inv_freq[None, :]
            cos, sin = (jnp.cos(ang), jnp.sin(ang))
            x1, x2 = (x[..., :d // 2], x[..., d // 2:])
            return jnp.concatenate([x1 * cos - x2 * sin, x1 * sin + x2 * cos], axis=-1)
        B, S, _ = x.shape

        def split_heads(t):
            return t.reshape(B, S, HEADS, D_K).transpose(0, 2, 1, 3)
        q = split_heads(x @ Wq + bq)
        k = split_heads(x @ Wk + bk)
        v = split_heads(x @ Wv + bv)
        q = _rope(q, pos_offset=0)
        k = _rope(k, pos_offset=0)
        scores = jnp.einsum('bhqd,bhkd->bhqk', q, k) / np.sqrt(D_K).astype(np.float32)
        probs = jax.nn.softmax(scores, axis=-1)
        attn = jnp.einsum('bhqk,bhkd->bhqd', probs, v)
        out = attn.transpose(0, 2, 1, 3).reshape(B, S, D_MODEL)
        return out @ Wo + bo

    def _L1_ffn_ref(x, Wr, br, Wup, bup, Wgate, bgate, Wdown, bdown):
        import jax, jax.numpy as jnp
        import numpy as np
        B, L, D = (1, 512, 256)
        E, H, G, K = (64, 64, 64, 16)

        def _grouped_routing_scores(router_scores):
            T, En = router_scores.shape
            Tq = T // G
            budget = Tq * K
            order = jnp.argsort(-router_scores, axis=0)
            sorted_vals = jnp.take_along_axis(router_scores, order, axis=0)
            group_score = sorted_vals.reshape(Tq, G, En).sum(axis=1)
            _, top_flat = jax.lax.top_k(group_score.reshape(-1), budget)
            gmask = jnp.zeros((Tq * En,), bool).at[top_flat].set(True).reshape(Tq, En)
            mask_sorted = jnp.broadcast_to(gmask[:, None, :], (Tq, G, En)).reshape(T, En)
            mask = jnp.zeros((T, En), bool).at[order, jnp.arange(En)[None, :]].set(mask_sorted)
            fs = jnp.where(mask, router_scores, 0.0)
            return fs / (fs.sum(axis=-1, keepdims=True) + 1e-06)
        Bx, Lx, Dx = x.shape
        xt = x.reshape(-1, Dx)
        router_scores = jax.nn.softmax(xt @ Wr + br, axis=-1)
        fs = _grouped_routing_scores(router_scores)
        up = jnp.einsum('td,edh->teh', xt, Wup) + bup
        gate = jnp.einsum('td,edh->teh', xt, Wgate) + bgate
        h = jax.nn.silu(up) * gate * fs[:, :, None]
        out = jnp.einsum('teh,ehd->td', h, Wdown) + fs @ bdown
        return out.reshape(Bx, Lx, Dx)
    h = _L0_tok_ref(x, L0_tok_W_proj, L0_tok_b_proj, L0_tok_pos_emb)
    h = _layernorm(h + _L0_attn_ref(h, L0_attn_Wk, L0_attn_Wq, L0_attn_Wv, L0_attn_Wu, L0_attn_kln_w, L0_attn_kln_b, L0_attn_qln_w, L0_attn_qln_b), axis=-1)
    h = _layernorm(h + _L0_ffn_ref(h, L0_ffn_cn_w1, L0_ffn_cn_b1, L0_ffn_cn_w2, L0_ffn_cn_b2, L0_ffn_cn_w3, L0_ffn_cn_b3, L0_ffn_cn_w4, L0_ffn_cn_b4, L0_ffn_gc_w1, L0_ffn_gc_b1, L0_ffn_gc_w2, L0_ffn_gc_b2, L0_ffn_gc_w3, L0_ffn_gc_b3, L0_ffn_adaptive_range), axis=-1)
    h = _layernorm(h + _L1_attn_ref(h, L1_attn_Wq, L1_attn_bq, L1_attn_Wk, L1_attn_bk, L1_attn_Wv, L1_attn_bv, L1_attn_Wo, L1_attn_bo), axis=-1)
    h = _layernorm(h + _L1_ffn_ref(h, L1_ffn_Wr, L1_ffn_br, L1_ffn_Wup, L1_ffn_bup, L1_ffn_Wgate, L1_ffn_bgate, L1_ffn_Wdown, L1_ffn_bdown), axis=-1)
    return h

_drawn_inputs = setup_inputs


def setup_inputs(seed=0):
    import zlib

    import numpy as np

    out = dict(_drawn_inputs(seed))
    spreads = {'L0_attn_kln_w': (1.0, 0.6),
     'L0_attn_kln_b': (0.0, 0.8),
     'L0_attn_qln_w': (1.0, 0.6),
     'L0_attn_qln_b': (0.0, 0.8),
     'L0_ffn_cn_b1': (0.0, 0.8),
     'L0_ffn_cn_b2': (0.0, 0.8),
     'L0_ffn_cn_b3': (0.0, 0.8),
     'L0_ffn_gc_b1': (0.0, 0.8),
     'L0_ffn_gc_b2': (0.0, 0.8),
     'L1_attn_bq': (0.0, 0.8),
     'L1_attn_bk': (0.0, 0.8),
     'L1_attn_bv': (0.0, 0.1),
     'L1_attn_bo': (0.0, 0.1),
     'L1_ffn_br': (0.0, 0.1),
     'L1_ffn_bup': (0.0, 0.444),
     'L1_ffn_bgate': (0.0, 0.442),
     'L1_ffn_bdown': (0.0, 0.272)}
    factors = {'L0_ffn_cn_w1': 6.255,
     'L0_ffn_cn_w2': 6.296,
     'L0_ffn_cn_w3': 5.351,
     'L0_ffn_cn_w4': 6.03,
     'L0_ffn_gc_w1': 8.0,
     'L0_ffn_gc_w2': 8.0,
     'L0_ffn_gc_w3': 4.67,
     'L1_attn_Wq': 8.0,
     'L1_attn_Wk': 8.0,
     'L1_attn_Wv': 2.894}
    for name, (base, spread) in spreads.items():
        noise = np.random.default_rng([zlib.crc32(name.encode()), seed]).standard_normal(out[name].shape)
        drawn = base * np.exp(spread * noise) if base else spread * noise
        out[name] = jnp.asarray(drawn.astype(out[name].dtype))
    for name, factor in factors.items():
        out[name] = (out[name] * factor).astype(out[name].dtype)
    return out
```

```python
from contextlib import ExitStack

import numpy as np

import concourse.bass as bass
from concourse import mybir

F32 = mybir.dt.float32
ALU = mybir.AluOpType
ACT = mybir.ActivationFunctionType
AX = mybir.AxisListType

P = 128
B, SEQ, E = 16, 36, 256
NT = B * SEQ
HALF = NT // 2
EC = E // P
KD = 768 // P
HEADS, HD = 16, 16
HPC = P // HD
QP = 64
PAIRS = B // 2
TRI = 3
NTRI = 6
TT, TTN = 96, 6
NX, XH = 64, 64
XP = NX // 2
GROUP = 64
NG = NT // GROUP
BUDGET = NG * 16
EPS = 1e-5
NEG = -1e30
CYCLES = 3
FB = 3

CST = {}


def _constants():
    parts = []
    at = 0

    def put(name, a):
        nonlocal at
        full = np.zeros((P, a.shape[1]), np.float32)
        full[:a.shape[0]] = a
        CST[name] = (at, a.shape[1])
        parts.append(full)
        at += a.shape[1]

    p = np.arange(P)
    same_head = (p[:, None] // HD == p[None, :] // HD).astype(np.float32)
    put("ident", np.eye(P, dtype=np.float32))
    put("center", np.eye(P, dtype=np.float32) - same_head / HD)
    put("head_mean", same_head / HD)
    put("all_mean", np.full((P, P), 1.0 / E, np.float32))
    put("ones", np.ones((P, P), np.float32))
    put("same_half", (p[:, None] // NX == p[None, :] // NX).astype(np.float32))
    put("same_expert", (p[:, None] % NX == p[None, :] % NX).astype(np.float32))
    put("to_both", (p[:, None] == p[None, :] % NX).astype(np.float32))
    put("to_second", ((p[:, None] + NX) == p[None, :]).astype(np.float32))
    h = np.arange(E) // HD
    put("v_mask", (h[None, :] % TRI == (np.arange(TRI * SEQ) // SEQ)[:, None]).astype(np.float32))
    q = p % QP
    causal = np.where((np.arange(SEQ)[None, :] > q[:, None]) & (q[:, None] < SEQ), NEG, 0.0)
    put("causal", causal.astype(np.float32))
    put("head_of", (p[:, None] // HD == np.arange(HPC)[None, :]).astype(np.float32))
    put("sign", np.where(p < 64, 1.0, -1.0).astype(np.float32)[:, None])
    put("minus_sign", np.where(p < 64, -1.0, 1.0).astype(np.float32)[:, None])
    put("eps", np.full((P, 1), EPS, np.float32))
    half = HD // 2
    inv = (np.float32(1.0) / np.float32(10000.0) ** (np.arange(0, HD, 2, dtype=np.float32) / np.float32(HD))).astype(np.float32)
    ang = (np.arange(SEQ, dtype=np.float32)[None, :] * inv[:, None]).astype(np.float32)
    put("cos", np.cos(ang)[p % half])
    put("sin", np.sin(ang)[p % half] * np.where(p % HD < half, -1.0, 1.0)[:, None].astype(np.float32))
    put("before", (np.arange(NX)[None, :] < np.arange(NX)[:, None]).astype(np.float32))
    return np.concatenate(parts, axis=1)


CONST = _constants()

PAR = ["kln_w", "kln_b", "qln_w", "qln_b", "b_proj", "b_proj1", "cn_b1", "cn_b11", "cn_b2", "cn_b3", "cn_b4",
       "gc_b1", "gc_b2", "gc_b3", "ar", "bq", "bq1", "bk", "bk1", "bv", "bv1", "bo", "bo1"]
PCOL = {n: i for i, n in enumerate(PAR)}
NPAR = len(PAR)
SHUFFLE = [p - 8 if p % 16 >= 8 else p + 8 for p in range(32)]


def build(nc, d, out):
    ctx = ExitStack()
    with ctx:
        def sb(name, shape, dt=F32):
            return ctx.enter_context(nc.sbuf_tensor(name, shape, dt))

        def sem(name):
            return ctx.enter_context(nc.semaphore(name))

        ps = ctx.enter_context(nc.psum_tensor("ps", [P, 8, 512], F32))
        cst = sb("cst", [P, CONST.shape[1]])
        par = sb("par", [P, NPAR])
        posb = sb("posb", [P, EC, SEQ])
        wa0 = sb("wa0", [P, 4, EC, E])
        wa1 = wa0
        cw = sb("cw", [P, 2 * E + 2 * P + 64 + P])
        gw = sb("gw", [P, 2 * P + 64 + P])
        wr = sb("wr", [P, EC, NX])
        br = sb("br", [TT, NX])
        bdown = sb("bdown", [P, E])
        bup = sb("bup", [P, XP])
        bgate = sb("bgate", [P, XP])
        wup = sb("wup", [P, EC, NX, XH])
        wgate = sb("wgate", [P, EC, NX, XH])
        wdown = sb("wdown", [P, XP, E])

        ha = sb("ha", [P, EC, NT])
        hb = sb("hb", [P, EC, NT])
        res = sb("res", [P, EC, NT])
        xc = sb("xc", [P, EC, NT])
        qt = sb("qt", [P, EC, NT + QP])
        kc = res
        big = sb("big", [P, EC * HPC * NT])
        tmp = sb("tmp", [P, 4224])

        def part(area, at, *shape, rows=P):
            n = int(np.prod(shape))
            flat = area[0:rows, at:at + n]
            if len(shape) == 1:
                return flat
            axes = "abcd"[:len(shape)]
            return flat.rearrange(f"p ({' '.join(axes)}) -> p {' '.join(axes)}",
                                  **{x: k for x, k in zip(axes[1:], shape[1:])})

        patches = part(big, 0, KD, NT)
        w_proj = part(big, KD * NT, KD, E)
        wkc = part(big, KD * (NT + E), 2, EC, E)
        kb = part(big, 0, EC, HPC, NT)
        sq = part(tmp, 0, EC, NT)
        sd = part(tmp, EC * NT, EC, NT)
        rs = part(tmp, 2 * EC * NT, EC, NT)
        scal = sb("scal", [P, 2, HPC])
        xr = sb("xr", [P, 2, EC, TRI * SEQ])
        vm = part(tmp, 0, 2, 2, E, rows=TRI * SEQ)
        ssb = part(tmp, 1024, 2, HEADS, SEQ)
        pt = part(tmp, 2176, 2, NTRI, P, rows=TRI * SEQ)
        osb = part(tmp, 3712, 2, E)
        psb = sb("psb", [P, 2, NTRI * TRI, SEQ])
        mx = sb("mx", [P, 2, HEADS])
        sm = sb("sm", [P, 2, HEADS])
        rc = sb("rc", [P, 2, HEADS])
        cx = sb("cx", [P, EC, NT])

        g1 = part(big, 0, EC, NT)
        g2 = part(big, 2 * NT, NT)
        g3 = part(big, 3 * NT, NT, rows=64)
        th = part(big, 4 * NT, NT)
        co = part(big, 5 * NT, NT)
        gsum = sb("gsum", [P, EC, B])
        gg1 = sb("gg1", [P, B])
        gg2 = sb("gg2", [64, B])
        gth = sb("gth", [P, B])
        gco = sb("gco", [P, 2])
        cg = sb("cg", [P, B])
        nk = NG - 1
        lg = part(tmp, 0, TTN, NX, rows=TT)
        sc = part(tmp, 384, TTN // 2, 2, NX, rows=TT)
        se = part(tmp, 768, HALF)
        wk = part(tmp, 1056, HALF)
        srt = part(tmp, 1344, HALF)
        junk = part(tmp, 1632, NT)
        junk2 = part(tmp, 2208, NT, rows=NX)
        cum = part(tmp, 2208, HALF)
        ine = part(tmp, 2496, HALF)
        mask = part(tmp, 2784, HALF)
        msc = part(tmp, 3072, HALF)
        rden = part(tmp, 3360, HALF)
        ma = cx[0:NX, 0, :]
        mb = cx[0:NX, 1, :]
        dg = kc[0:NX, 0, :].rearrange("p (g e) -> p g e", e=NX)
        gall = kc[0:NX, 1, :]
        eq = part(big, 0, nk, HALF)
        gt = part(big, nk * HALF, nk, HALF)
        lm = sb("lm", [TT, TTN])
        ls = sb("ls", [TT, TTN])
        lr = sb("lr", [TT, TTN])
        st = sb("st", [NX, 2 * NG])
        st2 = sb("st2", [P, 2 * NG])
        rank = sb("rank", [NX, 2 * NG])
        sel = sb("sel", [NX, NG])
        dsel = sb("dsel", [NX, NG])
        dsel2 = sb("dsel2", [P, NG])
        cnt = sb("cnt", [P, 2 * nk])
        base = sb("base", [P, nk])
        fs_dram = nc.dram_tensor("fs_dram", (NX, NT), F32, kind="Internal").ap()
        fb = part(tmp, 0, FB, NT)
        fst = sb("fst", [P, HALF])
        uu = part(big, 2 * nk * HALF, 2, HALF)
        hh = part(big, 2 * nk * HALF + 2 * HALF, 2, HALF)
        hw = part(big, 2 * nk * HALF + 4 * HALF, 2, NT)
        before = part(big, 2 * nk * HALF + 4 * HALF + 2 * NT, 2 * NT - NX, rows=NX)
        ofin = part(big, 0, TTN, E, rows=TT)
        bn = sb("bn", [TT, TTN, 6])
        ag = sb("ag", [TT, TTN, 2])
        sdf = sb("sdf", [TT, TTN])
        rsf = sb("rsf", [TT, TTN])

        def C(name, rows=P):
            a, n = CST[name]
            return cst[0:rows, a:a + n]

        def par_col(name, rows=P):
            return par[0:rows, PCOL[name]:PCOL[name] + 1]

        ident = C("ident")

        s_ld_cst = sem("s_ld_cst")
        s_ld_par = sem("s_ld_par")
        s_ld_pos = sem("s_ld_pos")
        s_ld_a0k = sem("s_ld_a0k")
        s_ld_a0v = sem("s_ld_a0v")
        s_ld_cn = sem("s_ld_cn")
        s_ld_gc = sem("s_ld_gc")
        s_ld_a1 = sem("s_ld_a1")
        s_ld_wr = sem("s_ld_wr")
        s_ld_misc = sem("s_ld_misc")
        s_ld_up = sem("s_ld_up")
        s_ld_gate = sem("s_ld_gate")
        s_ld_down = sem("s_ld_down")
        s_w_psum = sem("s_w_psum")
        s_w_ready = sem("s_w_ready")
        s_tok_psum = sem("s_tok_psum")
        s_h0_ready = sem("s_h0_ready")
        s_kraw = sem("s_kraw")
        s_qraw = sem("s_qraw")
        s_kcopy = sem("s_kcopy")
        s_sq_k = sem("s_sq_k")
        s_sq_q = sem("s_sq_q")
        s_kvar = sem("s_kvar")
        s_qvar = sem("s_qvar")
        s_sd_k = sem("s_sd_k")
        s_sd_q = sem("s_sd_q")
        s_qk_ready = sem("s_qk_ready")
        s_xr_ready = sem("s_xr_ready")
        s_fs_stored = sem("s_fs_stored")
        s_s_psum = sem("s_s_psum")
        s_s_read = sem("s_s_read")
        s_sub_ready = sem("s_sub_ready")
        s_p_ready = sem("s_p_ready")
        s_v_psum = sem("s_v_psum")
        s_vm_ready = sem("s_vm_ready")
        s_turn_psum = sem("s_turn_psum")
        s_turned = sem("s_turned")
        s_o_psum = sem("s_o_psum")
        s_o_ready = sem("s_o_ready")
        s_rs_done = sem("s_rs_done")
        s_u_psum = sem("s_u_psum")
        s_r_ready = sem("s_r_ready")
        s_mean_psum = sem("s_mean_psum")
        s_xc_ready = sem("s_xc_ready")
        s_sqn_ready = sem("s_sqn_ready")
        s_var_psum = sem("s_var_psum")
        s_sdn_ready = sem("s_sdn_ready")
        s_x_ready = sem("s_x_ready")
        s_pool_ready = sem("s_pool_ready")
        s_gsum_ready = sem("s_gsum_ready")
        s_g1p = sem("s_g1p")
        s_g1r = sem("s_g1r")
        s_g2p = sem("s_g2p")
        s_g2r = sem("s_g2r")
        s_g3p = sem("s_g3p")
        s_g3r = sem("s_g3r")
        s_l1p = sem("s_l1p")
        s_l1r = sem("s_l1r")
        s_l2p = sem("s_l2p")
        s_l2r = sem("s_l2r")
        s_l3p = sem("s_l3p")
        s_l3r = sem("s_l3r")
        s_l4p = sem("s_l4p")
        s_th_ready = sem("s_th_ready")
        s_f_ready = sem("s_f_ready")
        s_qb_ready = sem("s_qb_ready")
        s_lg_psum = sem("s_lg_psum")
        s_lg_sub = sem("s_lg_sub")
        s_lg_exp = sem("s_lg_exp")
        s_sc_ready = sem("s_sc_ready")
        s_tr_psum = sem("s_tr_psum")
        s_se_ready = sem("s_se_ready")
        s_srt_ready = sem("s_srt_ready")
        s_sh_psum = sem("s_sh_psum")
        s_m_ready = sem("s_m_ready")
        s_st_ready = sem("s_st_ready")
        s_st_psum = sem("s_st_psum")
        s_dg_ready = sem("s_dg_ready")
        s_g_psum = sem("s_g_psum")
        s_d_ready = sem("s_d_ready")
        s_d_psum = sem("s_d_psum")
        s_cnt_ready = sem("s_cnt_ready")
        s_cnt_psum = sem("s_cnt_psum")
        s_mk_ready = sem("s_mk_ready")
        s_sum_psum = sem("s_sum_psum")
        s_fs_ready = sem("s_fs_ready")
        s_ug_psum = sem("s_ug_psum")
        s_u_ready = sem("s_u_ready")
        s_g_read = sem("s_g_read")
        s_hs_ready = sem("s_hs_ready")
        s_y_psum = sem("s_y_psum")
        s_y_ready = sem("s_y_ready")
        s_ag_ready = sem("s_ag_ready")
        s_yt_psum = sem("s_yt_psum")
        s_out_ready = sem("s_out_ready")
        s_stored = sem("s_stored")
        s_dve_n = sem("s_dve_n")
        s_act_n = sem("s_act_n")
        s_pool_n = sem("s_pool_n")
        s_ld_x = [sem(f"s_ld_x{i}") for i in range(3)]
        s_fb_ld = [sem(f"s_fb_ld{i}") for i in range(FB)]
        block = ctx.enter_context(nc.Block())

        def hs_(half):
            return slice(half * HALF, (half + 1) * HALF)

        def split(ap):
            return ap.rearrange("p (b t) -> p b t", t=SEQ)

        @block.sync
        def _(sp):
            sp.dma_start(cst[:], d["cst"]).then_inc(s_ld_cst, 16)
            sp.dma_start(par[:], d["par"]).then_inc(s_ld_par, 16)
            sp.dma_start(wa0[:, 0:2], d["wa0"][:, 0:2]).then_inc(s_ld_a0k, 16)
            for i in range(3):
                sp.dma_start(w_proj[:, 2 * i:2 * i + 2], d["w_proj"][:, 2 * i:2 * i + 2]).then_inc(s_ld_x[i], 16)
                sp.dma_start(patches[:, 2 * i:2 * i + 2], d["patches"][:, 2 * i:2 * i + 2]).then_inc(s_ld_x[i], 16)
            sp.dma_start(posb[:], d["pos"]).then_inc(s_ld_pos, 16)
            sp.dma_start(wa0[:, 2:4], d["wa0"][:, 2:4]).then_inc(s_ld_a0v, 16)
            sp.dma_start(cw[:], d["cw"]).then_inc(s_ld_cn, 16)
            sp.dma_start(gw[:], d["gw"]).then_inc(s_ld_gc, 16)
            sp.dma_start(wr[:], d["wr"]).then_inc(s_ld_wr, 16)
            sp.dma_start(br[:], d["br"]).then_inc(s_ld_wr, 16)
            sp.dma_start(bdown[:], d["bdown"]).then_inc(s_ld_misc, 16)
            sp.dma_start(bup[:], d["bup"]).then_inc(s_ld_misc, 16)
            sp.dma_start(bgate[:], d["bgate"]).then_inc(s_ld_misc, 16)
            sp.dma_start(wup[:], d["wup"]).then_inc(s_ld_up, 16)
            sp.dma_start(wgate[:], d["wgate"]).then_inc(s_ld_gate, 16)
            sp.dma_start(wdown[:], d["wdown"]).then_inc(s_ld_down, 16)
            sp.wait_ge(s_u_psum, 1)
            sp.dma_start(wa1[:], d["wa1"]).then_inc(s_ld_a1, 16)
            sp.wait_ge(s_fs_ready, 1)
            for half in range(2):
                sp.dma_start(fs_dram[:, hs_(half)], fst[NX * half:NX * half + NX, :]).then_inc(s_fs_stored, 16)
            sp.wait_ge(s_fs_stored, 32)
            for p in range(XP):
                if p >= FB:
                    sp.wait_ge(s_hs_ready, 2 * (p - FB) + 2)
                for j in range(2):
                    sp.dma_start(fb[XH * j:XH * j + XH, p % FB, :],
                                 fs_dram[2 * p + j:2 * p + j + 1, :].to_broadcast([XH, NT])).then_inc(s_fb_ld[p % FB], 16)
            for i in range(TTN):
                sp.wait_ge(s_out_ready, i + 1)
                sp.dma_start(out[i * TT:(i + 1) * TT, :], ofin[:, i, :]).then_inc(s_stored, 16)
            sp.wait_ge(s_stored, 16 * TTN)

        cw1 = cw[:, 0:2 * E].rearrange("p (c n) -> p c n", c=EC)
        cw2 = cw[:, 2 * E:2 * E + 2 * P].rearrange("p (c n) -> p c n", c=EC)
        cw3 = cw[:, 2 * E + 2 * P:2 * E + 2 * P + 64]
        cw4 = cw[0:64, 2 * E + 2 * P + 64:2 * E + 2 * P + 64 + P]
        gw1 = gw[:, 0:2 * P].rearrange("p (c n) -> p c n", c=EC)
        gw2 = gw[:, 2 * P:2 * P + 64]
        gw3 = gw[0:64, 2 * P + 64:2 * P + 64 + P]

        def layer_in(layer):
            return ha if layer == 0 else hb

        def pass_io(cy):
            return [(hb, res), (res, xc), (xc, res)][cy]

        @block.tensor
        def _(pe):
            def proj(w, x, bank, half_first=True):
                for half in range(2):
                    for c in range(EC):
                        for k in range(EC):
                            ins = pe.matmul(ps[:, bank + 2 * c + half, 0:HALF], w[:, k, c * P:(c + 1) * P],
                                            x[:, k, hs_(half)], start=(k == 0), stop=(k == EC - 1))
                return ins

            pe.wait_ge(s_ld_cst, 16)
            pe.wait_ge(s_ld_a0k, 16)
            for m in range(2):
                for ci in range(EC):
                    for co_ in range(EC):
                        ins = pe.matmul(ps[:, 4 + m, ci * E + co_ * P:ci * E + co_ * P + P],
                                        wa0[:, m, co_, ci * P:(ci + 1) * P], C("center"), start=True, stop=True)
                ins.then_inc(s_w_psum, 1)

            for k in range(KD):
                if k % 2 == 0:
                    pe.wait_ge(s_ld_x[k // 2], 32)
                for half in range(2):
                    for c in range(EC):
                        ins = pe.matmul(ps[:, 2 * c + half, 0:HALF], w_proj[:, k, c * P:(c + 1) * P],
                                        patches[:, k, hs_(half)], start=(k == 0), stop=(k == KD - 1))
            ins.then_inc(s_tok_psum, 1)

            def norm_stats(n):
                for half in range(2):
                    pe.wait_ge(s_r_ready, 2 * n + half + 1)
                    for c in range(EC):
                        ins = pe.matmul(ps[:, 4 + half, 0:HALF], C("all_mean"), res[:, c, hs_(half)],
                                        start=(c == 0), stop=(c == EC - 1))
                    ins.then_inc(s_mean_psum, 1)
                for half in range(2):
                    pe.wait_ge(s_sqn_ready, 2 * n + half + 1)
                    for c in range(EC):
                        ins = pe.matmul(ps[:, 6 + half, 0:HALF], C("all_mean"), sq[:, c, hs_(half)],
                                        start=(c == 0), stop=(c == EC - 1))
                    ins.then_inc(s_var_psum, 1)

            def attention(layer):
                x = layer_in(layer)
                w = wa0 if layer == 0 else wa1
                if layer == 0:
                    pe.wait_ge(s_w_ready, 2)
                    pe.wait_ge(s_h0_ready, 4)
                    proj(wkc[:, 0], x, 0).then_inc(s_kraw, 1)
                    proj(wkc[:, 1], x, 4).then_inc(s_qraw, 1)
                    for m, (psum, squares) in enumerate(((s_kvar, s_sq_k), (s_qvar, s_sq_q))):
                        pe.wait_ge(squares, 1)
                        pe.wait_ge(s_kcopy, m + 1)
                        buf = sq if m == 0 else sd
                        for half in range(2):
                            for c in range(EC):
                                ins = pe.matmul(ps[:, 4 * m + 2 * c + half, 0:HALF], C("head_mean"),
                                                buf[:, c, hs_(half)], start=True, stop=True)
                        ins.then_inc(psum, 1)
                else:
                    pe.wait_ge(s_ld_a1, 16)
                    pe.wait_ge(s_x_ready, 4)
                    proj(wa1[:, 1], x, 0).then_inc(s_kraw, 1)
                    proj(wa1[:, 0], x, 4).then_inc(s_qraw, 1)
                pe.wait_ge(s_ld_a0v, 16)

                def scores(n, i):
                    if i >= 2:
                        pe.wait_ge(s_s_read if layer == 0 else s_sub_ready, n - 1)
                    for j in range(2):
                        b = 2 * i + j
                        for c in range(EC):
                            ins = pe.matmul(ps[QP * j:QP * j + QP, 2 * (i % 2) + c, 0:HPC * SEQ],
                                            qt[:, c, b * SEQ:b * SEQ + QP], kb[:, c, :, b * SEQ:(b + 1) * SEQ],
                                            start=True, stop=True)
                    ins.then_inc(s_s_psum, 1)

                def values(n, i):
                    if n:
                        pe.wait_ge(s_vm_ready, n)
                    for j in range(2):
                        pe.wait_ge(s_xr_ready, 2 * n + j + 1)
                        for k in range(EC):
                            ins = pe.matmul(ps[0:TRI * SEQ, 6, j * E:(j + 1) * E], xr[:, j, k, :], w[:, 2, k, :],
                                            start=(k == 0), stop=(k == EC - 1))
                    ins.then_inc(s_v_psum, 1)

                def turn(i):
                    n = n0 + i
                    if n:
                        pe.wait_ge(s_turned, n + layer)
                    if i < PAIRS:
                        pe.wait_ge(s_p_ready, n + 1)
                        for t in range(NTRI):
                            ins = pe.transpose(ps[0:TRI * SEQ, 4 + t // 3, (t % 3) * P:(t % 3 + 1) * P],
                                               psb[:, n % 2, TRI * t:TRI * t + TRI, :], ident)
                    if i >= 1:
                        pe.wait_ge(s_o_ready, n)
                        for c in range(EC):
                            ins = pe.transpose(ps[:, 4 + c, 3 * P:4 * P], osb[:, (n - 1) % 2, c * P:(c + 1) * P], ident)
                    ins.then_inc(s_turn_psum, 1)

                def weigh(n):
                    pe.wait_ge(s_turned, n + layer + 1)
                    pe.wait_ge(s_vm_ready, n + 1)
                    if n:
                        pe.wait_ge(s_o_ready, n)
                    for j in range(2):
                        for t in range(NTRI):
                            a, b_ = TRI * HD * t, min(TRI * HD * (t + 1), E)
                            ins = pe.matmul(ps[QP * j:QP * j + QP, 7, a:b_], pt[:, n % 2, t, QP * j:QP * j + QP],
                                            vm[:, n % 2, j, a:b_], start=True, stop=True)
                    ins.then_inc(s_o_psum, 1)

                n0 = PAIRS * layer
                pe.wait_ge(s_qk_ready, layer + 1)
                for i in range(PAIRS + 2):
                    if i < PAIRS:
                        scores(n0 + i, i)
                    if i >= 1:
                        turn(i - 1)
                    if i < PAIRS:
                        values(n0 + i, i)
                    if 1 <= i <= PAIRS:
                        weigh(n0 + i - 1)
                pe.wait_ge(s_turned, (PAIRS + 1) * (layer + 1))
                proj(w[:, 3], cx, 0).then_inc(s_u_psum, 1)

            attention(0)
            norm_stats(0)

            pe.wait_ge(s_ld_gc, 16)
            pe.wait_ge(s_gsum_ready, 1)
            for k in range(EC):
                ins = pe.matmul(ps[:, 3, 320:320 + B], gw1[:, k, :], gsum[:, k, :], start=(k == 0), stop=(k == EC - 1))
            ins.then_inc(s_g1p, 1)
            pe.wait_ge(s_g1r, 1)
            pe.matmul(ps[0:64, 3, 336:336 + B], gw2, gg1[:], start=True, stop=True).then_inc(s_g2p, 1)
            pe.wait_ge(s_g2r, 1)
            pe.matmul(ps[:, 3, 352:352 + B], gw3, gg2[:], start=True, stop=True).then_inc(s_g3p, 1)
            pe.wait_ge(s_ld_cn, 16)
            pe.wait_ge(s_g3r, 1)
            for cy in range(CYCLES):
                xin, _ = pass_io(cy)
                for half in range(2):
                    u = 2 * cy + half
                    if cy == 0:
                        pe.wait_ge(s_x_ready, half + 1)
                    else:
                        pe.wait_ge(s_f_ready, u - 1)
                    for c in range(EC):
                        for k in range(EC):
                            ins = pe.matmul(ps[:, 4 * half + c, 0:HALF], cw1[:, k, c * P:(c + 1) * P],
                                            xin[:, k, hs_(half)], start=(k == 0), stop=(k == EC - 1))
                    ins.then_inc(s_l1p, 1)
                for half in range(2):
                    pe.wait_ge(s_l1r, 2 * cy + half + 1)
                    for k in range(EC):
                        ins = pe.matmul(ps[:, 4 * half + 2, 0:HALF], cw2[:, k, :], g1[:, k, hs_(half)],
                                        start=(k == 0), stop=(k == EC - 1))
                    ins.then_inc(s_l2p, 1)
                for half in range(2):
                    pe.wait_ge(s_l2r, 2 * cy + half + 1)
                    pe.matmul(ps[0:64, 4 * half + 3, 0:HALF], cw3, g2[:, hs_(half)], start=True, stop=True)\
                      .then_inc(s_l3p, 1)
                for half in range(2):
                    pe.wait_ge(s_l3r, 2 * cy + half + 1)
                    pe.matmul(ps[:, 4 * half, 0:HALF], cw4, g3[:, hs_(half)], start=True, stop=True)\
                      .then_inc(s_l4p, 1)
            norm_stats(1)
            attention(1)
            norm_stats(2)

            pe.wait_ge(s_ld_wr, 32)
            pe.wait_ge(s_x_ready, 6)
            for i in range(TTN):
                for k in range(EC):
                    ins = pe.matmul(ps[0:TT, 3, i * NX:(i + 1) * NX], ha[:, k, i * TT:(i + 1) * TT], wr[:, k, :],
                                    start=(k == 0), stop=(k == EC - 1))
            ins.then_inc(s_lg_psum, 1)
            pe.wait_ge(s_sc_ready, 1)
            for i in range(TTN // 2):
                ins = pe.transpose(ps[:, 3, i * TT:(i + 1) * TT], sc[:, i, :, :].rearrange("p h e -> p (h e)"), ident[0:TT, 0:TT])
            ins.then_inc(s_tr_psum, 1)
            pe.wait_ge(s_se_ready, 1)
            pe.wait_ge(s_srt_ready, 1)
            pe.matmul(ps[0:NX, 2, 0:HALF], ident[:, NX:P], srt[:], start=True, stop=True).then_inc(s_sh_psum, 1)
            both = C("to_both", NX)
            pe.wait_ge(s_st_ready, 1)
            pe.wait_ge(s_m_ready, 1)
            pe.matmul(ps[:, 1, 0:2 * NG], both, st[:], start=True, stop=True).then_inc(s_st_psum, 1)
            pe.wait_ge(s_dg_ready, 1)
            for j in range(2):
                pe.matmul(ps[0:NX, 4 + j, 0:HALF], C("ones", NX)[:, 0:NX],
                          dg[:].rearrange("p g e -> p (g e)")[:, hs_(j)], start=True, stop=True)\
                  .then_inc(s_g_psum, 1)
            pe.wait_ge(s_d_ready, 1)
            pe.matmul(ps[:, 0, 0:NG], both, dsel[:], start=True, stop=True).then_inc(s_d_psum, 1)
            pe.wait_ge(s_cnt_ready, nk)
            pe.matmul(ps[:, 2, 0:nk], C("same_expert"), cnt[:, 0:nk], start=True, stop=False)
            pe.matmul(ps[:, 2, 0:nk], C("to_second"), cnt[:, nk:2 * nk], start=False, stop=True)\
              .then_inc(s_cnt_psum, 1)
            pe.wait_ge(s_mk_ready, 1)
            pe.matmul(ps[:, 3, 0:HALF], C("same_half"), msc[:], start=True, stop=True).then_inc(s_sum_psum, 1)

            pe.wait_ge(s_fs_ready, 1)
            pe.wait_ge(s_ld_up, 16)
            pe.wait_ge(s_ld_gate, 16)
            pe.wait_ge(s_ld_down, 16)

            def down(p):
                pe.wait_ge(s_hs_ready, 2 * p + 2)
                for half in range(2):
                    for c in range(EC):
                        ins = pe.matmul(ps[:, 2 * c + half, 0:HALF], wdown[:, p, c * P:(c + 1) * P],
                                        hw[:, p % 2, hs_(half)], start=(p == 0), stop=False)
                ins.then_inc(s_y_psum, 1)

            for p in range(XP):
                for half in range(2):
                    n = 2 * p + half
                    if n >= 2:
                        pe.wait_ge(s_g_read, n - 1)
                    for w_, bank in ((wup, 4), (wgate, 5)):
                        for k in range(EC):
                            ins = pe.matmul(ps[:, bank + 2 * (n % 2), 0:HALF], w_[:, k, 2 * p:2 * p + 2, :],
                                            ha[:, k, hs_(half)], start=(k == 0), stop=(k == EC - 1))
                    ins.then_inc(s_ug_psum, 1)
                if p >= 1:
                    down(p - 1)
            down(XP - 1)
            pe.wait_ge(s_ld_misc, 48)
            for half in range(2):
                for c in range(EC):
                    ins = pe.matmul(ps[:, 2 * c + half, 0:HALF], bdown[NX * half:NX * half + NX, c * P:(c + 1) * P],
                                    fst[NX * half:NX * half + NX, :], start=False, stop=True)
            ins.then_inc(s_y_psum, 1)
            pe.wait_ge(s_y_ready, 1)
            for i in range(TTN):
                for c in range(EC):
                    ins = pe.transpose(ps[0:TT, 4 + i // 2, (i % 2) * E + c * P:(i % 2) * E + (c + 1) * P],
                                       res[:, c, i * TT:(i + 1) * TT], ident)
                if i % 2:
                    ins.then_inc(s_yt_psum, 1)

        @block.scalar
        def _(act):
            act.wait_ge(s_ld_par, 16)
            act.wait_ge(s_ld_cst, 16)
            act.memzero(qt[:, :, NT:NT + QP]).then_inc(s_act_n, 1)
            for m in range(2):
                act.wait_ge(s_w_psum, m + 1)
                act.activation(wkc[:, m].rearrange("p c n -> p (c n)"), ps[:, 4 + m, :], ACT.Copy)\
                   .then_inc(s_w_ready, 1)

            def bank4(first, half=None):
                return ps[:, first:first + 4, 0:HALF].rearrange("p (c h) n -> p c h n", c=EC)

            def halves(x):
                return x[:, :, 0:NT].rearrange("p c (h n) -> p c h n", h=2)

            def norm(n):
                for half in range(2):
                    act.wait_ge(s_xc_ready, 2 * n + half + 1)
                    act.activation(sq[:, :, hs_(half)], xc[:, :, hs_(half)], ACT.Square).then_inc(s_sqn_ready, 1)
                for half in range(2):
                    act.wait_ge(s_var_psum, 2 * n + half + 1)
                    act.activation(sd[:, 0, hs_(half)], ps[:, 6 + half, 0:HALF], ACT.Sqrt, bias=C("eps"))\
                       .then_inc(s_sdn_ready, 1)

            def attention(layer):
                if layer == 0:
                    act.wait_ge(s_kcopy, 1)
                    act.activation(sq, kc[:], ACT.Square).then_inc(s_sq_k, 1)
                    act.wait_ge(s_kcopy, 2)
                    act.activation(sd, cx[:], ACT.Square).then_inc(s_sq_q, 1)
                    for m, (psum, done, buf) in enumerate(((s_kvar, s_sd_k, sq), (s_qvar, s_sd_q, sd))):
                        act.wait_ge(psum, 1)
                        for c in range(EC):
                            ins = act.activation(halves(buf)[:, c], bank4(4 * m)[:, c], ACT.Sqrt, bias=C("eps"))
                        ins.then_inc(done, 1)
                else:
                    for m, (psum, bias, buf) in enumerate(((s_kraw, "bk", kc), (s_qraw, "bq", cx))):
                        act.wait_ge(psum, 2)
                        for c in range(EC):
                            ins = act.activation(halves(buf)[:, c], bank4(4 * m)[:, c], ACT.Identity,
                                                 bias=par_col(bias + ("1" if c else "")))
                        ins.then_inc(s_qb_ready, 1)
                n0 = PAIRS * layer

                def exps(n):
                    act.wait_ge(s_sub_ready, n + 1)
                    if n >= 2:
                        act.wait_ge(s_turn_psum, n - 1 + layer)
                        act.wait_ge(s_rs_done, n - 1)
                    act.activation(psb[:, n % 2, 0:HEADS, :], ssb[:, n % 2], ACT.Exp, scale=0.25)\
                       .then_inc(s_p_ready, 1)

                def keep_turned(i):
                    n = n0 + i
                    act.wait_ge(s_turn_psum, n + layer + 1)
                    if i < PAIRS:
                        if n >= 2:
                            act.wait_ge(s_o_psum, n - 1)
                        ins = act.activation(pt[:, n % 2].rearrange("p (a t) q -> p a (t q)", a=2),
                                             ps[0:TRI * SEQ, 4:6, 0:3 * P], ACT.Copy)
                    if i >= 1:
                        for c in range(EC):
                            dst = cx[:, c, 2 * (i - 1) * SEQ:2 * i * SEQ].rearrange("p (j t) -> p j t", j=2)
                            src = ps[:, 4 + c, 3 * P:4 * P].rearrange("p (j q) -> p j q", j=2)[:, :, 0:SEQ]
                            if layer == 0:
                                ins = act.activation(dst, src, ACT.Copy)
                            else:
                                ins = act.activation(dst, src, ACT.Identity, bias=par_col("bv1" if c else "bv"))
                    ins.then_inc(s_turned, 1)

                for i in range(PAIRS + 2):
                    if i >= 1:
                        keep_turned(i - 1)
                    if i < PAIRS:
                        exps(n0 + i)

            attention(0)
            norm(0)
            act.wait_ge(s_g1p, 1)
            act.activation(gg1[:], ps[:, 3, 320:320 + B], ACT.Gelu, bias=par_col("gc_b1"), scale=1.0 / SEQ)\
               .then_inc(s_g1r, 1)
            act.wait_ge(s_g2p, 1)
            act.activation(gg2[:], ps[0:64, 3, 336:336 + B], ACT.Gelu, bias=par_col("gc_b2", 64)).then_inc(s_g2r, 1)
            act.wait_ge(s_g3p, 1)
            act.wait_ge(s_pool_ready, 1)
            act.activation(gth[:], ps[:, 3, 352:352 + B], ACT.Tanh, bias=gco[:, 1:2], scale=0.5).then_inc(s_g3r, 1)
            for cy in range(CYCLES):
                for half in range(2):
                    act.wait_ge(s_l1p, 2 * cy + half + 1)
                    for c in range(EC):
                        ins = act.activation(g1[:, c, hs_(half)], ps[:, 4 * half + c, 0:HALF], ACT.Gelu,
                                             bias=par_col("cn_b11" if c else "cn_b1"))
                    ins.then_inc(s_l1r, 1)
                for half in range(2):
                    act.wait_ge(s_l2p, 2 * cy + half + 1)
                    act.activation(g2[:, hs_(half)], ps[:, 4 * half + 2, 0:HALF], ACT.Gelu, bias=par_col("cn_b2"))\
                       .then_inc(s_l2r, 1)
                for half in range(2):
                    act.wait_ge(s_l3p, 2 * cy + half + 1)
                    act.activation(g3[:, hs_(half)], ps[0:64, 4 * half + 3, 0:HALF], ACT.Gelu,
                                   bias=par_col("cn_b3", 64)).then_inc(s_l3r, 1)
                for half in range(2):
                    act.wait_ge(s_l4p, 2 * cy + half + 1)
                    act.activation(th[:, hs_(half)], ps[:, 4 * half, 0:HALF], ACT.Tanh, bias=gco[:, 0:1], scale=0.5)\
                       .then_inc(s_th_ready, 1)
            norm(1)
            attention(1)
            norm(2)
            act.wait_ge(s_lg_sub, 1)
            act.activation(sc[:].rearrange("p i h e -> p h i e"), lg[:].rearrange("p (h i) e -> p h i e", h=2), ACT.Exp).then_inc(s_lg_exp, 1)
            act.wait_ge(s_ld_misc, 48)
            for n in range(2 * XP):
                act.wait_ge(s_ug_psum, n + 1)
                if n >= 2:
                    act.wait_ge(s_g_read, n - 1)
                act.activation(uu[:, n % 2, :], ps[:, 4 + 2 * (n % 2), 0:HALF], ACT.Silu, bias=bup[:, n // 2:n // 2 + 1])\
                   .then_inc(s_u_ready, 1)
            act.wait_ge(s_ag_ready, TTN)
            act.activation(sdf[:], ag[:, :, 1], ACT.Sqrt, bias=C("eps", TT)).then_inc(s_sdn_ready, 1)

        @block.gpsimd
        def _(pool):
            for j in range(2):
                pool.memset(psb[:, j, HEADS:NTRI * TRI, :], 0.0).then_inc(s_pool_n, 1)
            for layer in range(2):
                x = layer_in(layer)
                if layer == 0:
                    pool.wait_ge(s_h0_ready, 4)
                else:
                    pool.wait_ge(s_x_ready, 4)
                for i in range(PAIRS):
                    if layer or i:
                        pool.wait_ge(s_v_psum, PAIRS * layer + i)
                    for j in range(2):
                        b = 2 * i + j
                        rep = x[:, :, b * SEQ:(b + 1) * SEQ].unsqueeze(2).to_broadcast([P, EC, TRI, SEQ])
                        pool.tensor_copy(xr[:, j].rearrange("p k (r t) -> p k r t", r=TRI), rep).then_inc(s_xr_ready, 1)
            pool.wait_ge(s_ld_cst, 16)
            pool.wait_ge(s_x_ready, 6)
            last = NT - NX
            pool.memset(before[:, 0:last], 1.0).then_inc(s_pool_n, 1)
            pool.tensor_copy(before[:, last:NT], C("before", NX)).then_inc(s_pool_n, 1)
            pool.memset(before[:, NT:NT + last], 0.0).then_inc(s_pool_n, 1)

        @block.vector
        def _(v):
            marked = [0]

            def mark(ins):
                marked[0] += 1
                return ins.then_inc(s_dve_n, 1)

            def chain(ins):
                mark(ins)
                v.wait_ge(s_dve_n, marked[0])

            v.wait_ge(s_ld_par, 16)
            v.wait_ge(s_ld_cst, 16)
            v.wait_ge(s_ld_pos, 16)
            v.wait_ge(s_pool_n, 2)
            chain(v.tensor_scalar(gco[:, 0:1], par_col("cn_b4"), 0.5, None, ALU.mult))
            v.tensor_scalar(gco[:, 1:2], par_col("gc_b3"), 0.5, None, ALU.mult).then_inc(s_pool_ready, 1)
            for c in range(EC):
                mark(v.tensor_scalar(posb[:, c], posb[:, c], par_col("b_proj1" if c else "b_proj"), None, ALU.add))
            v.wait_ge(s_dve_n, marked[0])
            v.wait_ge(s_tok_psum, 1)
            for c in range(EC):
                for half in range(2):
                    v.tensor_tensor(split(ha[:, c, hs_(half)]), split(ps[:, 2 * c + half, 0:HALF]),
                                    posb[:, c].unsqueeze(1).to_broadcast([P, B // 2, SEQ]), ALU.add)\
                     .then_inc(s_h0_ready, 1)

            def halves(x):
                return x[:, :, 0:NT].rearrange("p c (h n) -> p c h n", h=2)

            def norm(n, dst):
                for half in range(2):
                    v.wait_ge(s_mean_psum, 2 * n + half + 1)
                    v.wait_ge(s_r_ready, 2 * n + half + 1)
                    v.tensor_tensor(xc[:, :, hs_(half)], res[:, :, hs_(half)],
                                    ps[:, 4 + half, 0:HALF].unsqueeze(1).to_broadcast([P, EC, HALF]), ALU.subtract)\
                     .then_inc(s_xc_ready, 1)
                for half in range(2):
                    v.wait_ge(s_sdn_ready, 2 * n + half + 1)
                    chain(v.reciprocal(rs[:, 0, hs_(half)], sd[:, 0, hs_(half)]))
                    if half == 0:
                        v.wait_ge(s_xc_ready, 2 * n + 2)
                    v.tensor_tensor(dst[:, :, hs_(half)], xc[:, :, hs_(half)],
                                    rs[:, 0, hs_(half)].unsqueeze(1).to_broadcast([P, EC, HALF]), ALU.mult)\
                     .then_inc(s_x_ready, 1)

            def attention(layer):
                if layer == 0:
                    for j, col in enumerate(("kln_w", "kln_b")):
                        mark(v.tensor_scalar(scal[:, j], C("head_of"), par_col(col), None, ALU.mult))
                    v.wait_ge(s_kraw, 1)
                    for c in range(EC):
                        for half in range(2):
                            ins = v.tensor_copy(kc[:, c, hs_(half)], ps[:, 2 * c + half, 0:HALF])
                    ins.then_inc(s_kcopy, 1)
                    v.wait_ge(s_qraw, 1)
                    for c in range(EC):
                        for half in range(2):
                            ins = v.tensor_copy(cx[:, c, hs_(half)], ps[:, 4 + 2 * c + half, 0:HALF])
                    ins.then_inc(s_kcopy, 1)
                    v.wait_ge(s_kcopy, 2)
                    v.wait_ge(s_sd_k, 1)
                    chain(v.reciprocal(rs[:], sq[:]))
                    chain(v.tensor_tensor(kc[:], kc[:], rs[:], ALU.mult))
                    for h in range(HPC):
                        for c in range(EC):
                            mark(v.tensor_scalar(kb[:, c, h, :], kc[:, c, :], scal[:, 0, h:h + 1],
                                                     scal[:, 1, h:h + 1], ALU.mult, ALU.add))
                    v.wait_ge(s_sd_q, 1)
                    chain(v.reciprocal(rs[:], sd[:]))
                    chain(v.tensor_tensor(cx[:], cx[:], rs[:], ALU.mult))
                    v.wait_ge(s_act_n, 1)
                    v.tensor_scalar(qt[:, :, 0:NT], cx[:], par_col("qln_w"), par_col("qln_b"), ALU.mult, ALU.add)\
                     .then_inc(s_qk_ready, 1)
                else:
                    cosb = C("cos").unsqueeze(1).to_broadcast([P, EC * B, SEQ])
                    sinb = C("sin").unsqueeze(1).to_broadcast([P, EC * B, SEQ])

                    def blocks(x):
                        return x[:, :, 0:NT].rearrange("p c (b t) -> p (c b) t", t=SEQ) if x is not qt else None
                    v.wait_ge(s_qb_ready, 1)
                    chain(v.stream_shuffle(rs[:], kc[:], SHUFFLE))
                    mark(v.tensor_tensor(blocks(rs), blocks(rs), sinb, ALU.mult))
                    chain(v.tensor_tensor(blocks(kc), blocks(kc), cosb, ALU.mult))
                    chain(v.tensor_tensor(kc[:], kc[:], rs[:], ALU.add))
                    for h in range(HPC):
                        for c in range(EC):
                            mark(v.tensor_scalar(kb[:, c, h, :], kc[:, c, :], C("head_of")[:, h:h + 1], None,
                                                     ALU.mult))
                    v.wait_ge(s_qb_ready, 2)
                    v.wait_ge(s_dve_n, marked[0])
                    chain(v.stream_shuffle(rs[:], cx[:], SHUFFLE))
                    mark(v.tensor_tensor(blocks(rs), blocks(rs), sinb, ALU.mult))
                    chain(v.tensor_tensor(blocks(cx), blocks(cx), cosb, ALU.mult))
                    v.tensor_tensor(qt[:, :, 0:NT], cx[:], rs[:], ALU.add).then_inc(s_qk_ready, 1)

                n0 = PAIRS * layer

                def spread(a):
                    return a.unsqueeze(2).to_broadcast([P, HEADS, SEQ])

                def keep_values(n):
                    v.wait_ge(s_v_psum, n + 1)
                    if n >= 2:
                        v.wait_ge(s_o_psum, n - 1)
                    v.tensor_tensor(vm[:, n % 2], ps[0:TRI * SEQ, 6, :].rearrange("p (j e) -> p j e", j=2),
                                    C("v_mask", TRI * SEQ).unsqueeze(1).to_broadcast([TRI * SEQ, 2, E]), ALU.mult)\
                     .then_inc(s_vm_ready, 1)

                def shift(n, i):
                    a = n % 2
                    pss = ps[:, 2 * a:2 * a + 2, 0:HPC * SEQ].rearrange("p c (h t) -> p c h t", t=SEQ)
                    sh = ssb[:, a].rearrange("p (c h) t -> p c h t", c=EC)
                    v.wait_ge(s_s_psum, n + 1)
                    if n >= 2:
                        v.wait_ge(s_p_ready, n - 1)
                    if layer == 0:
                        causal = C("causal").unsqueeze(1).unsqueeze(1).to_broadcast([P, EC, HPC, SEQ])
                        v.tensor_tensor(sh, pss, causal, ALU.add).then_inc(s_s_read, 1)
                        v.wait_ge(s_s_read, n + 1)
                        chain(v.tensor_reduce(mx[:, a], ssb[:, a], AX.X, ALU.max))
                        v.tensor_tensor(ssb[:, a], ssb[:, a], spread(mx[:, a]), ALU.subtract).then_inc(s_sub_ready, 1)
                    else:
                        mv = mx[:, a].rearrange("p (c h) -> p c h", c=EC)
                        chain(v.tensor_reduce(mv, pss, AX.X, ALU.max))
                        v.tensor_tensor(sh, pss, mv.unsqueeze(3).to_broadcast([P, EC, HPC, SEQ]), ALU.subtract)\
                         .then_inc(s_sub_ready, 1)

                def sums(n):
                    a = n % 2
                    v.wait_ge(s_p_ready, n + 1)
                    v.tensor_reduce(sm[:, a], psb[:, a, 0:HEADS, :], AX.X, ALU.add).then_inc(s_rs_done, 1)
                    v.wait_ge(s_rs_done, n + 1)
                    chain(v.reciprocal(rc[:, a], sm[:, a]))

                def keep_weighed(n):
                    a = n % 2
                    v.wait_ge(s_o_psum, n + 1)
                    if n >= 2:
                        v.wait_ge(s_turn_psum, n + layer)
                    v.tensor_tensor(osb[:, a].rearrange("p (h d) -> p h d", d=HD),
                                    ps[:, 7, 0:E].rearrange("p (h d) -> p h d", d=HD),
                                    rc[:, a].unsqueeze(2).to_broadcast([P, HEADS, HD]), ALU.mult)\
                     .then_inc(s_o_ready, 1)

                for i in range(PAIRS + 1):
                    if i < PAIRS:
                        shift(n0 + i, i)
                    if i >= 1:
                        sums(n0 + i - 1)
                    if i < PAIRS:
                        keep_values(n0 + i)
                    if i >= 1:
                        keep_weighed(n0 + i - 1)
                v.wait_ge(s_u_psum, layer + 1)
                x = layer_in(layer)
                for half in range(2):
                    for c in range(EC):
                        if layer == 0:
                            ins = v.tensor_tensor(res[:, c, hs_(half)], ps[:, 2 * c + half, 0:HALF], x[:, c, hs_(half)],
                                                  ALU.add)
                        else:
                            ins = v.scalar_tensor_tensor(res[:, c, hs_(half)], ps[:, 2 * c + half, 0:HALF],
                                                         par_col("bo1" if c else "bo"), x[:, c, hs_(half)],
                                                         ALU.add, ALU.add)
                    ins.then_inc(s_r_ready, 1)

            attention(0)
            norm(0, hb)
            v.wait_ge(s_x_ready, 2)
            for c in range(EC):
                ins = v.tensor_reduce(gsum[:, c], split(hb[:, c, :]), AX.X, ALU.add)
            ins.then_inc(s_gsum_ready, 1)
            v.wait_ge(s_g3r, 1)
            chain(v.tensor_scalar(cg[:], gth[:], par_col("ar"), 0.7, ALU.mult, ALU.mult))
            mark(v.tensor_scalar(cg[:], cg[:], 0.1, None, ALU.add))
            chain(v.tensor_scalar(scal[:, 0, 0:1], par_col("ar"), 0.3, None, ALU.mult))
            for cy in range(CYCLES):
                xin, xout = pass_io(cy)
                for half in range(2):
                    u = 2 * cy + half
                    t_ = hs_(half)
                    v.wait_ge(s_th_ready, u + 1)
                    if cy > 0:
                        v.wait_ge(s_f_ready, u - 1)
                    cgb = cg[:, half * B // 2:(half + 1) * B // 2].unsqueeze(2).to_broadcast([P, B // 2, SEQ])
                    chain(v.scalar_tensor_tensor(split(co[:, t_]), split(th[:, t_]), scal[:, 0, 0:1], cgb,
                                                 ALU.mult, ALU.add))
                    mark(v.scalar_tensor_tensor(g1[:, 0, t_], xin[:, 1, t_], C("sign"), co[:, t_], ALU.mult, ALU.mult))
                    chain(v.scalar_tensor_tensor(g1[:, 1, t_], xin[:, 0, t_], C("minus_sign"), co[:, t_], ALU.mult, ALU.mult))
                    ins = v.tensor_tensor(xout[:, :, t_], xin[:, :, t_], g1[:, :, t_], ALU.add)
                    ins.then_inc(s_f_ready, 1)
            for half in range(2):
                v.wait_ge(s_f_ready, 2 * CYCLES - 1 + half)
                v.tensor_tensor(res[:, :, hs_(half)], res[:, :, hs_(half)], hb[:, :, hs_(half)], ALU.add)\
                 .then_inc(s_r_ready, 1)
            norm(1, hb)
            attention(1)
            norm(2, ha)

            v.wait_ge(s_lg_psum, 1)
            v.wait_ge(s_ld_wr, 32)
            chain(v.tensor_tensor(lg[:], ps[0:TT, 3, 0:TTN * NX].rearrange("p (i e) -> p i e", e=NX),
                                  br[:].unsqueeze(1).to_broadcast([TT, TTN, NX]), ALU.add))
            chain(v.tensor_reduce(lm[:], lg[:], AX.X, ALU.max))
            v.tensor_tensor(lg[:], lg[:], lm[:].unsqueeze(2).to_broadcast([TT, TTN, NX]), ALU.subtract)\
             .then_inc(s_lg_sub, 1)
            v.wait_ge(s_lg_exp, 1)
            chain(v.tensor_reduce(ls[:].rearrange("p (i h) -> p i h", h=2), sc[:], AX.X, ALU.add))
            chain(v.reciprocal(lr[:], ls[:]))
            flat = sc[:].rearrange("p i h e -> p (i h) e")
            v.tensor_tensor(flat, flat, lr[:].unsqueeze(2).to_broadcast([TT, TTN, NX]), ALU.mult)\
             .then_inc(s_sc_ready, 1)
            v.wait_ge(s_tr_psum, 1)
            mark(v.tensor_copy(wk[:], ps[:, 3, 0:HALF]))
            v.tensor_copy(se[:], ps[:, 3, 0:HALF]).then_inc(s_se_ready, 1)
            v.wait_ge(s_dve_n, marked[0])
            for k in range(HALF // 8):
                ins = v.max(srt[:, 8 * k:8 * k + 8], wk[:])
                if k == HALF // 8 - 1:
                    ins.then_inc(s_srt_ready, 1)
                    v.wait_ge(s_srt_ready, 1)
                else:
                    chain(ins)
                    chain(v.match_replace(wk[:], srt[:, 8 * k:8 * k + 8], wk[:], -1.0))
            mark(v.tensor_copy(ma[:, 0:HALF], srt[0:NX, :]))
            v.wait_ge(s_sh_psum, 1)
            ins = v.tensor_copy(ma[:, HALF:NT][:, ::-1], ps[0:NX, 2, 0:HALF])
            ins.then_inc(s_m_ready, 1)
            v.wait_ge(s_m_ready, 1)
            v.wait_ge(s_dve_n, marked[0])
            top = NT - GROUP
            mark(v.tensor_tensor(mb[:, top:NT], ma[:, 0:GROUP], ma[:, top:NT], ALU.max))
            chain(v.tensor_tensor(ma[:, 0:GROUP], ma[:, 0:GROUP], ma[:, top:NT], ALU.min))
            src, dst = ma, mb
            for m in (256, 128, 64):
                a = src[:, 0:512].rearrange("p (n two m) -> p n two m", two=2, m=m)
                b_ = dst[:, 0:512].rearrange("p (n two m) -> p n two m", two=2, m=m)
                mark(v.tensor_tensor(b_[:, :, 0, :], a[:, :, 0, :], a[:, :, 1, :], ALU.min))
                chain(v.tensor_tensor(b_[:, :, 1, :], a[:, :, 0, :], a[:, :, 1, :], ALU.max))
                src, dst = dst, src
            blocks_ = src[:].rearrange("p (g n) -> p g n", n=GROUP)
            mark(v.tensor_reduce(st[:, 0:NG][:, ::-1], blocks_, AX.X, ALU.add))
            ins = v.tensor_reduce(st[:, NG:2 * NG][:, ::-1], blocks_, AX.X, ALU.min)
            ins.then_inc(s_st_ready, 1)
            v.wait_ge(s_dve_n, marked[0])
            v.tensor_tensor(dg[:], ident[0:NX, 0:NX].unsqueeze(1).to_broadcast([NX, NG, NX]),
                            st[:, 0:NG].unsqueeze(2).to_broadcast([NX, NG, NX]), ALU.mult).then_inc(s_dg_ready, 1)
            v.wait_ge(s_st_psum, 1)
            mark(v.tensor_copy(st2[:], ps[:, 1, 0:2 * NG]))
            for j in range(2):
                v.wait_ge(s_g_psum, j + 1)
                mark(v.tensor_copy(gall[:, hs_(j)], ps[0:NX, 4 + j, 0:HALF]))
            v.wait_ge(s_dve_n, marked[0])
            v.wait_ge(s_pool_n, 5)
            for g in range(NG):
                mark(v.tensor_scalar(junk[0:NX, :], gall[:], st[:, g:g + 1], None, ALU.is_gt, ALU.add,
                                         accum_out=rank[:, g:g + 1]))
                earlier = before[:, NT - NX - NX * g:2 * NT - NX - NX * g]
                chain(v.scalar_tensor_tensor(junk2, gall[:], st[:, g:g + 1], earlier, ALU.is_equal, ALU.mult,
                                             accum_out=rank[:, NG + g:NG + g + 1]))
            chain(v.tensor_tensor(sel[:], rank[:, 0:NG], rank[:, NG:2 * NG], ALU.add))
            chain(v.tensor_scalar(sel[:], sel[:], float(BUDGET), None, ALU.is_lt))
            mark(v.tensor_copy(dsel[:, NG - 1:NG], sel[:, NG - 1:NG]))
            ins = v.tensor_tensor(dsel[:, 0:NG - 1], sel[:, 0:NG - 1], sel[:, 1:NG], ALU.subtract)
            ins.then_inc(s_d_ready, 1)
            for k in range(nk):
                mark(v.tensor_scalar(gt[:, k], se[:], st2[:, NG + k:NG + k + 1], None, ALU.is_gt, ALU.add,
                                         accum_out=cnt[:, k:k + 1]))
                v.tensor_scalar(eq[:, k], se[:], st2[:, NG + k:NG + k + 1], None, ALU.is_equal, ALU.add,
                                accum_out=cnt[:, nk + k:nk + k + 1]).then_inc(s_cnt_ready, 1)
            v.wait_ge(s_d_psum, 1)
            mark(v.tensor_copy(dsel2[:], ps[:, 0, 0:NG]))
            v.wait_ge(s_cnt_psum, 1)
            mark(v.tensor_copy(base[:], ps[:, 2, 0:nk]))
            v.wait_ge(s_dve_n, marked[0])
            mark(v.tensor_scalar(mask[:], se[:], 0.0, dsel2[:, nk:nk + 1], ALU.mult, ALU.add))
            for k in range(nk):
                chain(v.tensor_tensor_scan(cum[:], eq[:, k], C("ones")[:, 0:1].to_broadcast([P, HALF]), base[:, k:k + 1],
                                           ALU.add, ALU.mult))
                mark(v.scalar_tensor_tensor(mask[:], gt[:, k], dsel2[:, k:k + 1], mask[:], ALU.mult, ALU.add))
                chain(v.scalar_tensor_tensor(ine[:], cum[:], float(GROUP * (k + 1)), eq[:, k], ALU.is_le, ALU.mult))
                chain(v.scalar_tensor_tensor(mask[:], ine[:], dsel2[:, k:k + 1], mask[:], ALU.mult, ALU.add))
            v.tensor_tensor(msc[:], mask[:], se[:], ALU.mult).then_inc(s_mk_ready, 1)
            v.wait_ge(s_sum_psum, 1)
            chain(v.tensor_scalar(rden[:], ps[:, 3, 0:HALF], 1e-6, None, ALU.add))
            chain(v.reciprocal(rden[:], rden[:]))
            v.wait_ge(s_mk_ready, 1)
            v.tensor_tensor(fst[:], msc[:], rden[:], ALU.mult).then_inc(s_fs_ready, 1)

            v.wait_ge(s_ld_misc, 48)
            for n in range(2 * XP):
                p, half = n // 2, n % 2
                v.wait_ge(s_u_ready, n + 1)
                ins = v.scalar_tensor_tensor(hh[:, n % 2], ps[:, 5 + 2 * (n % 2), 0:HALF], bgate[:, p:p + 1],
                                             uu[:, n % 2], ALU.add, ALU.mult)
                ins.then_inc(s_g_read, 1)
                v.wait_ge(s_g_read, n + 1)
                v.wait_ge(s_fb_ld[p % FB], 32 * (p // FB + 1))
                if p >= 2:
                    v.wait_ge(s_y_psum, p - 1)
                v.tensor_tensor(hw[:, p % 2, hs_(half)], hh[:, n % 2], fb[:, p % FB, hs_(half)], ALU.mult)\
                 .then_inc(s_hs_ready, 1)
            v.wait_ge(s_y_psum, XP + 1)
            for c in range(EC):
                ins = v.tensor_tensor(res[:, c].rearrange("p (h n) -> p h n", h=2), ps[:, 2 * c:2 * c + 2, 0:HALF],
                                      ha[:, c].rearrange("p (h n) -> p h n", h=2), ALU.add)
            ins.then_inc(s_y_ready, 1)
            for i in range(TTN):
                v.wait_ge(s_yt_psum, i // 2 + 1)
                chain(v.bn_stats(bn[:, i], ps[0:TT, 4 + i // 2, (i % 2) * E:(i % 2 + 1) * E]))
                v.bn_aggr(ag[:, i], bn[:, i]).then_inc(s_ag_ready, 1)
            v.wait_ge(s_sdn_ready, 7)
            chain(v.reciprocal(rsf[:], sdf[:]))
            for i in range(TTN):
                v.tensor_scalar(ofin[:, i], ps[0:TT, 4 + i // 2, (i % 2) * E:(i % 2 + 1) * E], ag[:, i, 0:1],
                                rsf[:, i:i + 1], ALU.subtract, ALU.mult).then_inc(s_out_ready, 1)


def _layout(a):
    def chunks(w):
        return np.ascontiguousarray(w.reshape(-1, P, w.shape[1]).transpose(1, 0, 2))

    x = a["x"].reshape(B, 6, 16, 6, 16, 3).transpose(2, 4, 5, 0, 1, 3).reshape(768, NT)
    cols = {
        "kln_w": np.tile(a["L0_attn_kln_w"], HPC), "kln_b": np.tile(a["L0_attn_kln_b"], HPC),
        "qln_w": np.tile(a["L0_attn_qln_w"], HPC), "qln_b": np.tile(a["L0_attn_qln_b"], HPC),
        "b_proj": a["L0_tok_b_proj"], "cn_b1": a["L0_ffn_cn_b1"], "cn_b2": a["L0_ffn_cn_b2"],
        "cn_b3": a["L0_ffn_cn_b3"], "cn_b4": np.tile(a["L0_ffn_cn_b4"], P), "gc_b1": a["L0_ffn_gc_b1"],
        "gc_b2": a["L0_ffn_gc_b2"], "gc_b3": np.tile(a["L0_ffn_gc_b3"], P), "ar": np.tile(a["L0_ffn_adaptive_range"], P),
        "bq": a["L1_attn_bq"], "bk": a["L1_attn_bk"], "bv": a["L1_attn_bv"], "bo": a["L1_attn_bo"],
    }
    par = np.zeros((P, NPAR), np.float32)
    for name, v in cols.items():
        for c in range(-(-len(v) // P)):
            part = v[c * P:(c + 1) * P]
            par[:len(part), PCOL[name + ("1" if c else "")]] = part

    def top(w, rows=P):
        full = np.zeros((rows, w.shape[1]), np.float32)
        full[:w.shape[0]] = w
        return full

    cw = np.concatenate([chunks(a["L0_ffn_cn_w1"]).reshape(P, -1), chunks(a["L0_ffn_cn_w2"]).reshape(P, -1),
                         a["L0_ffn_cn_w3"], top(np.tile(a["L0_ffn_cn_w4"], (1, P)))], axis=1)
    gw = np.concatenate([chunks(a["L0_ffn_gc_w1"]).reshape(P, -1), a["L0_ffn_gc_w2"],
                         top(np.tile(a["L0_ffn_gc_w3"], (1, P)))], axis=1)

    def experts_in(w):
        return w.reshape(NX, EC, P, XH).transpose(2, 1, 0, 3)

    return {
        "cst": CONST, "par": par, "patches": chunks(x), "w_proj": chunks(a["L0_tok_W_proj"].T),
        "pos": chunks(a["L0_tok_pos_emb"].T),
        "wa0": np.stack([chunks(a["L0_attn_Wk"]), chunks(a["L0_attn_Wq"]), chunks(a["L0_attn_Wv"].T),
                         chunks(a["L0_attn_Wu"].T)], axis=1),
        "wa1": np.stack([chunks(a["L1_attn_" + n]) for n in ("Wq", "Wk", "Wv", "Wo")], axis=1),
        "cw": cw, "gw": gw, "wr": chunks(a["L1_ffn_Wr"]), "br": np.tile(a["L1_ffn_br"][None, :], (TT, 1)),
        "bdown": np.tile(a["L1_ffn_bdown"], (2, 1)), "bup": a["L1_ffn_bup"].reshape(XP, P).T,
        "bgate": a["L1_ffn_bgate"].reshape(XP, P).T,
        "wup": experts_in(a["L1_ffn_Wup"]), "wgate": experts_in(a["L1_ffn_Wgate"]),
        "wdown": a["L1_ffn_Wdown"].reshape(XP, P, E).transpose(1, 0, 2),
    }


def kernel(**inputs):
    import concourse.bacc as _bacc
    from concourse.bass_utils import run_bass_kernel_spmd as _run

    arrays = {k: np.ascontiguousarray(v) for k, v in _layout({k: np.asarray(v) for k, v in inputs.items()}).items()}
    nc = _bacc.Bacc("TRN2", target_bir_lowering=False, num_devices=1)
    d = {k: nc.dram_tensor(k + "_in", v.shape, F32, kind="ExternalInput").ap() for k, v in arrays.items()}
    out = nc.dram_tensor("out", (NT, E), F32, kind="ExternalOutput").ap()
    build(nc, d, out)
    r = _run(nc, [{k + "_in": v for k, v in arrays.items()}], core_ids=[0])
    return r.results[0]["out"].reshape(B, SEQ, E)
```

```python
from contextlib import ExitStack

import numpy as np

import concourse.bass as bass
from concourse import mybir

F32 = mybir.dt.float32
F32R = mybir.dt.float32r
ALU = mybir.AluOpType
ACT = mybir.ActivationFunctionType
AX = mybir.AxisListType

P = 128
B, SEQ, E = 16, 36, 256
NT = B * SEQ
HALF = NT // 2
EC = E // P
KD = 768 // P
HEADS, HD = 16, 16
HPC = P // HD
QP = 64
PAIRS = B // 2
TRI = 3
NTRI = 6
TT, TTN = 96, 6
NX, XH = 64, 64
XP = NX // 2
GROUP = 64
NG = NT // GROUP
NGH = (NG + 1) // 2
BUDGET = NG * 16
EPS = 1e-5
NEG = -1e30
CYCLES = 3
WU = 2 * XP
WS = 4
HS = 4
HEAD = 1
LAG = 2
AHEAD = 3
TURN = {"scores": 6, "shift": 40, "sums": 48, "groups": 51, "selected": 65, "counts": 74, "total": 98}
FB = 3
FP = 2

CST = {}


def _constants():
    parts = []
    at = 0

    def put(name, a):
        nonlocal at
        full = np.zeros((P, a.shape[1]), np.float32)
        full[:a.shape[0]] = a
        CST[name] = (at, a.shape[1])
        parts.append(full)
        at += a.shape[1]

    p = np.arange(P)
    same_head = (p[:, None] // HD == p[None, :] // HD).astype(np.float32)
    put("ident", np.eye(P, dtype=np.float32))
    put("center", np.eye(P, dtype=np.float32) - same_head / HD)
    put("head_mean", same_head / HD)
    put("all_mean", np.full((P, P), 1.0 / E, np.float32))
    put("ones", np.ones((P, P), np.float32))
    put("same_half", (p[:, None] // NX == p[None, :] // NX).astype(np.float32))
    put("same_expert", (p[:, None] % NX == p[None, :] % NX).astype(np.float32))
    put("to_both", (p[:, None] == p[None, :] % NX).astype(np.float32))
    put("to_second", ((p[:, None] + NX) == p[None, :]).astype(np.float32))
    h = np.arange(E) // HD
    put("v_mask", (h[None, :] % TRI == (np.arange(TRI * SEQ) // SEQ)[:, None]).astype(np.float32))
    q = p % QP
    causal = np.where((np.arange(SEQ)[None, :] > q[:, None]) & (q[:, None] < SEQ), NEG, 0.0)
    put("causal", causal.astype(np.float32))
    put("head_of", (p[:, None] // HD == np.arange(HPC)[None, :]).astype(np.float32))
    put("sign", np.where(p < 64, 1.0, -1.0).astype(np.float32)[:, None])
    put("minus_sign", np.where(p < 64, -1.0, 1.0).astype(np.float32)[:, None])
    put("eps", np.full((P, 1), EPS, np.float32))
    half = HD // 2
    inv = (np.float32(1.0) / np.float32(10000.0) ** (np.arange(0, HD, 2, dtype=np.float32) / np.float32(HD))).astype(np.float32)
    ang = (np.arange(SEQ, dtype=np.float32)[None, :] * inv[:, None]).astype(np.float32)
    put("cos", np.cos(ang)[p % half])
    put("sin", np.sin(ang)[p % half] * np.where(p % HD < half, -1.0, 1.0)[:, None].astype(np.float32))
    put("before", (np.arange(NX)[None, :] < (p % NX)[:, None]).astype(np.float32))
    return np.concatenate(parts, axis=1)


CONST = _constants()

PAR = ["kln_w", "kln_b", "qln_w", "qln_b", "b_proj", "b_proj1", "cn_b1", "cn_b11", "cn_b2", "cn_b3", "cn_b4",
       "gc_b1", "gc_b2", "gc_b3", "ar", "bq", "bq1", "bk", "bk1", "bv", "bv1", "bo", "bo1"]
PCOL = {n: i for i, n in enumerate(PAR)}
NPAR = len(PAR)
SHUFFLE = [p - 8 if p % 16 >= 8 else p + 8 for p in range(32)]


def build(nc, d, out):
    ctx = ExitStack()
    with ctx:
        def sb(name, shape, dt=F32):
            return ctx.enter_context(nc.sbuf_tensor(name, shape, dt))

        def sem(name):
            return ctx.enter_context(nc.semaphore(name))

        ps = ctx.enter_context(nc.psum_tensor("ps", [P, 8, 512], F32))
        big_at = -(-nc.sbuf_base // 32) * 32
        big = sb("big", [P, EC * HPC * NT])
        tmp = sb("tmp", [P, 4224])
        cst = sb("cst", [P, CONST.shape[1]])
        par = sb("par", [P, NPAR])
        posb = sb("posb", [P, EC, SEQ])
        into = sb("into", [P, 4 * EC * E + WU * E])
        wa0 = into[:, 0:4 * EC * E].rearrange("p (m c n) -> p m c n", m=4, c=EC)
        wa1 = wa0
        w_in = into[:, 4 * EC * E:].rearrange("p (u c n) -> p u c n", c=EC, n=P)
        hh = into[:, 0:XP * NT].rearrange("p (x n) -> p x n", n=NT)
        cw = sb("cw", [P, 2 * E + 2 * P + 64 + P])
        gw = sb("gw", [P, 2 * P + 64 + P])
        wr = sb("wr", [P, EC, NX])
        br = sb("br", [TT, NX])
        bdown = sb("bdown", [P, E])
        bup = sb("bup", [P, XP])
        bgate = sb("bgate", [P, XP])
        wdown = sb("wdown", [P, XP, E])

        ha = sb("ha", [P, EC, NT])
        hb = sb("hb", [P, EC, NT])
        res = sb("res", [P, EC, NT])
        xc = sb("xc", [P, EC, NT])
        qt = sb("qt", [P, EC, NT + QP])
        kc = res

        def part(area, at, *shape, rows=P):
            n = int(np.prod(shape))
            flat = area[0:rows, at:at + n]
            if len(shape) == 1:
                return flat
            axes = "abcd"[:len(shape)]
            return flat.rearrange(f"p ({' '.join(axes)}) -> p {' '.join(axes)}",
                                  **{x: k for x, k in zip(axes[1:], shape[1:])})

        patches = part(big, 0, KD, NT)
        w_proj = part(big, KD * NT, KD, E)
        wkc = part(big, KD * (NT + E), 2, EC, E)
        kb = part(big, 0, EC, HPC, NT)
        sq = part(tmp, 0, EC, NT)
        sd = part(tmp, EC * NT, EC, NT)
        rs = part(tmp, 2 * EC * NT, EC, NT)
        scal = sb("scal", [P, 2, HPC])
        xr = sb("xr", [P, 2, EC, TRI * SEQ])
        vm = part(tmp, 0, 2, 2, E, rows=TRI * SEQ)
        ssb = part(tmp, 1024, 2, HEADS, SEQ)
        pt = part(tmp, 2176, 2, NTRI, P, rows=TRI * SEQ)
        osb = part(tmp, 3712, 2, E)
        psb = sb("psb", [P, 2, NTRI * TRI, SEQ])
        mx = sb("mx", [P, 2, HEADS])
        sm = sb("sm", [P, 2, HEADS])
        rc = sb("rc", [P, 2, HEADS])
        cx = sb("cx", [P, EC, NT])

        g1 = part(big, 0, EC, NT)
        g2 = part(big, 2 * NT, NT)
        g3 = part(big, 3 * NT, NT, rows=64)
        th = part(big, 4 * NT, NT)
        co = part(big, 5 * NT, NT)
        gsum = sb("gsum", [P, EC, B])
        gg1 = sb("gg1", [P, B])
        gg2 = sb("gg2", [64, B])
        gth = sb("gth", [P, B])
        gco = sb("gco", [P, 2])
        cg = sb("cg", [P, B])
        nk = NG - 1
        lg = part(tmp, 0, TTN, NX, rows=TT)
        sc = part(tmp, 384, TTN // 2, 2, NX, rows=TT)
        se = part(tmp, 768, HALF)
        wk = part(tmp, 1056, HALF)
        srt = part(tmp, 1344, HALF)
        alt = part(tmp, 3648, HALF)
        junk = part(tmp, 1632, NT)
        junk2 = part(tmp, 2208, NT)
        cum = part(tmp, 1632, 2, HALF)
        ine = part(tmp, 2208, 2, HALF)
        mask = part(tmp, 2784, HALF)
        msc = part(tmp, 3072, HALF)
        rden = part(tmp, 3360, HALF)
        ma = cx[0:NX, 0, :]
        mb = cx[0:NX, 1, :]
        dg = kc[0:NX, 0, :].rearrange("p (g e) -> p g e", e=NX)
        mask2 = kc[:, 1, 0:HALF]
        eq = part(big, 0, nk, HALF)
        gt = part(big, nk * HALF, nk, HALF)
        lm = sb("lm", [TT, TTN])
        ls = sb("ls", [TT, TTN])
        lr = sb("lr", [TT, TTN])
        st = sb("st", [NX, 2 * NG])
        st2 = sb("st2", [P, 2 * NG])
        st3 = sb("st3", [P, NGH])
        rank = sb("rank", [P, 2 * NGH])
        sel = sb("sel", [P, NG])
        sel2 = sb("sel2", [P, NG])
        dsel = sb("dsel", [P, NG])
        cnt = sb("cnt", [P, 2 * nk])
        base = sb("base", [P, nk])
        fs_dram = nc.dram_tensor("fs_dram", (NX, NT), F32, kind="Internal").ap()
        fb = part(tmp, 0, FB, FP, NT)
        fst = sb("fst", [P, HALF])
        uu = qt[:].rearrange("p c n -> p (c n)")[:, 0:2 * NT].rearrange("p (s n) -> p s n", s=2)
        vv = hb
        hw = [xc[:, 0], xc[:, 1], part(tmp, FB * FP * NT, NT)]
        h_parts = nc.alloc_sbuf_tensor_at("h_parts", [P, HS, 2, NT], F32R, offset=big_at)
        before = xc[:].rearrange("p c n -> p (c n)")[:, 0:2 * NT - NX]
        parts = nc.alloc_sbuf_tensor_at("parts", [P, 2 * EC * NT + WS * 2 * E], F32R, offset=big_at + 4 * 2 * nk * HALF)
        x_hi = parts[:, 0:EC * NT].rearrange("p (c n) -> p c n", c=EC)
        x_lo = parts[:, EC * NT:2 * EC * NT].rearrange("p (c n) -> p c n", c=EC)
        w_parts = parts[:, 2 * EC * NT:].rearrange("p (s part n) -> p s part n", s=WS, part=2)
        ofin = part(big, 0, TTN, E, rows=TT)
        bn = sb("bn", [TT, TTN, 6])
        ag = sb("ag", [TT, TTN, 2])
        sdf = sb("sdf", [TT, TTN])
        rsf = sb("rsf", [TT, TTN])

        def C(name, rows=P):
            a, n = CST[name]
            return cst[0:rows, a:a + n]

        def par_col(name, rows=P):
            return par[0:rows, PCOL[name]:PCOL[name] + 1]

        ident = C("ident")

        s_ld_cst = sem("s_ld_cst")
        s_ld_par = sem("s_ld_par")
        s_ld_pos = sem("s_ld_pos")
        s_ld_a0k = sem("s_ld_a0k")
        s_ld_a0v = sem("s_ld_a0v")
        s_ld_cn = sem("s_ld_cn")
        s_ld_gc = sem("s_ld_gc")
        s_ld_a1 = sem("s_ld_a1")
        s_ld_wr = sem("s_ld_wr")
        s_ld_misc = sem("s_ld_misc")
        s_ld_in = sem("s_ld_in")
        s_ld_down = sem("s_ld_down")
        s_w_psum = sem("s_w_psum")
        s_w_ready = sem("s_w_ready")
        s_tok_psum = sem("s_tok_psum")
        s_h0_ready = sem("s_h0_ready")
        s_kraw = sem("s_kraw")
        s_qraw = sem("s_qraw")
        s_kcopy = sem("s_kcopy")
        s_sq_k = sem("s_sq_k")
        s_sq_q = sem("s_sq_q")
        s_kvar = sem("s_kvar")
        s_qvar = sem("s_qvar")
        s_sd_k = sem("s_sd_k")
        s_sd_q = sem("s_sd_q")
        s_qk_ready = sem("s_qk_ready")
        s_xr_ready = sem("s_xr_ready")
        s_fs_stored = sem("s_fs_stored")
        s_s_psum = sem("s_s_psum")
        s_s_read = sem("s_s_read")
        s_sub_ready = sem("s_sub_ready")
        s_p_ready = sem("s_p_ready")
        s_v_psum = sem("s_v_psum")
        s_vm_ready = sem("s_vm_ready")
        s_turn_psum = sem("s_turn_psum")
        s_turned = sem("s_turned")
        s_o_psum = sem("s_o_psum")
        s_o_ready = sem("s_o_ready")
        s_rs_done = sem("s_rs_done")
        s_u_psum = sem("s_u_psum")
        s_r_ready = sem("s_r_ready")
        s_mean_psum = sem("s_mean_psum")
        s_xc_ready = sem("s_xc_ready")
        s_sqn_ready = sem("s_sqn_ready")
        s_var_psum = sem("s_var_psum")
        s_sdn_ready = sem("s_sdn_ready")
        s_x_ready = sem("s_x_ready")
        s_pool_ready = sem("s_pool_ready")
        s_gsum_ready = sem("s_gsum_ready")
        s_g1p = sem("s_g1p")
        s_g1r = sem("s_g1r")
        s_g2p = sem("s_g2p")
        s_g2r = sem("s_g2r")
        s_g3p = sem("s_g3p")
        s_g3r = sem("s_g3r")
        s_l1p = sem("s_l1p")
        s_l1r = sem("s_l1r")
        s_l2p = sem("s_l2p")
        s_l2r = sem("s_l2r")
        s_l3p = sem("s_l3p")
        s_l3r = sem("s_l3r")
        s_l4p = sem("s_l4p")
        s_th_ready = sem("s_th_ready")
        s_f_ready = sem("s_f_ready")
        s_qb_ready = sem("s_qb_ready")
        s_lg_psum = sem("s_lg_psum")
        s_lg_sub = sem("s_lg_sub")
        s_lg_exp = sem("s_lg_exp")
        s_sc_ready = sem("s_sc_ready")
        s_tr_psum = sem("s_tr_psum")
        s_se_ready = sem("s_se_ready")
        s_srt_ready = sem("s_srt_ready")
        s_sh_psum = sem("s_sh_psum")
        s_m_ready = sem("s_m_ready")
        s_st_ready = sem("s_st_ready")
        s_st_psum = sem("s_st_psum")
        s_dg_ready = sem("s_dg_ready")
        s_g_psum = sem("s_g_psum")
        s_d_ready = sem("s_d_ready")
        s_rank_ready = sem("s_rank_ready")
        s_d_psum = sem("s_d_psum")
        s_cnt_ready = sem("s_cnt_ready")
        s_cnt_psum = sem("s_cnt_psum")
        s_mk_ready = sem("s_mk_ready")
        s_sum_psum = sem("s_sum_psum")
        s_fs_ready = sem("s_fs_ready")
        s_ug_psum = sem("s_ug_psum")
        s_ug_ready = sem("s_ug_ready")
        s_hh_ready = sem("s_hh_ready")
        s_xhi_ready = sem("s_xhi_ready")
        s_xlo_ready = sem("s_xlo_ready")
        s_whi_ready = sem("s_whi_ready")
        s_wlo_ready = sem("s_wlo_ready")
        s_hw_ready = sem("s_hw_ready")
        s_hhi_ready = sem("s_hhi_ready")
        s_hlo_ready = sem("s_hlo_ready")
        s_y_psum = sem("s_y_psum")
        s_y_ready = sem("s_y_ready")
        s_ag_ready = sem("s_ag_ready")
        s_yt_psum = sem("s_yt_psum")
        s_out_ready = sem("s_out_ready")
        s_stored = sem("s_stored")
        s_dve_n = sem("s_dve_n")
        s_act_n = sem("s_act_n")
        s_pool_n = sem("s_pool_n")
        s_ld_x = [sem(f"s_ld_x{i}") for i in range(3)]
        s_fb_ld = [sem(f"s_fb_ld{i}") for i in range(FB)]
        block = ctx.enter_context(nc.Block())

        def hs_(half):
            return slice(half * HALF, (half + 1) * HALF)

        def split(ap):
            return ap.rearrange("p (b t) -> p b t", t=SEQ)

        @block.sync
        def _(sp):
            sp.dma_start(cst[:], d["cst"]).then_inc(s_ld_cst, 16)
            sp.dma_start(par[:], d["par"]).then_inc(s_ld_par, 16)
            sp.dma_start(wa0[:, 0:2], d["wa0"][:, 0:2]).then_inc(s_ld_a0k, 16)
            for i in range(3):
                sp.dma_start(w_proj[:, 2 * i:2 * i + 2], d["w_proj"][:, 2 * i:2 * i + 2]).then_inc(s_ld_x[i], 16)
                sp.dma_start(patches[:, 2 * i:2 * i + 2], d["patches"][:, 2 * i:2 * i + 2]).then_inc(s_ld_x[i], 16)
            sp.dma_start(posb[:], d["pos"]).then_inc(s_ld_pos, 16)
            sp.dma_start(wa0[:, 2:4], d["wa0"][:, 2:4]).then_inc(s_ld_a0v, 16)
            sp.dma_start(cw[:], d["cw"]).then_inc(s_ld_cn, 16)
            sp.dma_start(gw[:], d["gw"]).then_inc(s_ld_gc, 16)
            sp.dma_start(wr[:], d["wr"]).then_inc(s_ld_wr, 16)
            sp.dma_start(br[:], d["br"]).then_inc(s_ld_wr, 16)
            sp.dma_start(bdown[:], d["bdown"]).then_inc(s_ld_misc, 16)
            sp.dma_start(bup[:], d["bup"]).then_inc(s_ld_misc, 16)
            sp.dma_start(bgate[:], d["bgate"]).then_inc(s_ld_misc, 16)
            sp.dma_start(into[:, 4 * EC * E:], d["w_in"]).then_inc(s_ld_in, 16)
            sp.dma_start(wdown[:], d["wdown"]).then_inc(s_ld_down, 16)
            sp.wait_ge(s_u_psum, 1)
            sp.dma_start(wa1[:], d["wa1"]).then_inc(s_ld_a1, 16)
            sp.wait_ge(s_fs_ready, 1)
            for half in range(2):
                sp.dma_start(fs_dram[:, hs_(half)], fst[NX * half:NX * half + NX, :]).then_inc(s_fs_stored, 16)
            sp.wait_ge(s_fs_stored, 32)
            fs_rows = fs_dram.rearrange("(p j) n -> j p n", j=2)
            for f in range(XP // FP):
                if f >= FB:
                    sp.wait_ge(s_hw_ready, FP * (f - FB + 1))
                for j in range(2):
                    sp.dma_start(fb[XH * j:XH * j + XH, f % FB],
                                 fs_rows[j:j + 1, FP * f:FP * f + FP, :].to_broadcast([XH, FP, NT]))\
                      .then_inc(s_fb_ld[f % FB], 16)
            for i in range(TTN):
                sp.wait_ge(s_out_ready, i + 1)
                sp.dma_start(out[i * TT:(i + 1) * TT, :], ofin[:, i, :]).then_inc(s_stored, 16)
            sp.wait_ge(s_stored, 16 * TTN)

        cw1 = cw[:, 0:2 * E].rearrange("p (c n) -> p c n", c=EC)
        cw2 = cw[:, 2 * E:2 * E + 2 * P].rearrange("p (c n) -> p c n", c=EC)
        cw3 = cw[:, 2 * E + 2 * P:2 * E + 2 * P + 64]
        cw4 = cw[0:64, 2 * E + 2 * P + 64:2 * E + 2 * P + 64 + P]
        gw1 = gw[:, 0:2 * P].rearrange("p (c n) -> p c n", c=EC)
        gw2 = gw[:, 2 * P:2 * P + 64]
        gw3 = gw[0:64, 2 * P + 64:2 * P + 64 + P]

        def layer_in(layer):
            return ha if layer == 0 else hb

        def pass_io(cy):
            return [(hb, res), (res, xc), (xc, res)][cy]

        @block.tensor
        def _(pe):
            def proj(w, x, bank, half_first=True):
                for half in range(2):
                    for c in range(EC):
                        for k in range(EC):
                            ins = pe.matmul(ps[:, bank + 2 * c + half, 0:HALF], w[:, k, c * P:(c + 1) * P],
                                            x[:, k, hs_(half)], start=(k == 0), stop=(k == EC - 1))
                return ins

            pe.wait_ge(s_ld_cst, 16)
            pe.wait_ge(s_ld_a0k, 16)
            for m in range(2):
                for ci in range(EC):
                    for co_ in range(EC):
                        ins = pe.matmul(ps[:, 4 + m, ci * E + co_ * P:ci * E + co_ * P + P],
                                        wa0[:, m, co_, ci * P:(ci + 1) * P], C("center"), start=True, stop=True)
                ins.then_inc(s_w_psum, 1)

            for k in range(KD):
                if k % 2 == 0:
                    pe.wait_ge(s_ld_x[k // 2], 32)
                for half in range(2):
                    for c in range(EC):
                        ins = pe.matmul(ps[:, 2 * c + half, 0:HALF], w_proj[:, k, c * P:(c + 1) * P],
                                        patches[:, k, hs_(half)], start=(k == 0), stop=(k == KD - 1))
            ins.then_inc(s_tok_psum, 1)

            def norm_stats(n):
                for half in range(2):
                    pe.wait_ge(s_r_ready, 2 * n + half + 1)
                    for c in range(EC):
                        ins = pe.matmul(ps[:, 4 + half, 0:HALF], C("all_mean"), res[:, c, hs_(half)],
                                        start=(c == 0), stop=(c == EC - 1))
                    ins.then_inc(s_mean_psum, 1)
                for half in range(2):
                    pe.wait_ge(s_sqn_ready, 2 * n + half + 1)
                    for c in range(EC):
                        ins = pe.matmul(ps[:, 6 + half, 0:HALF], C("all_mean"), sq[:, c, hs_(half)],
                                        start=(c == 0), stop=(c == EC - 1))
                    ins.then_inc(s_var_psum, 1)

            def attention(layer):
                x = layer_in(layer)
                w = wa0 if layer == 0 else wa1
                if layer == 0:
                    pe.wait_ge(s_w_ready, 2)
                    pe.wait_ge(s_h0_ready, 4)
                    proj(wkc[:, 0], x, 0).then_inc(s_kraw, 1)
                    proj(wkc[:, 1], x, 4).then_inc(s_qraw, 1)
                    for m, (psum, squares) in enumerate(((s_kvar, s_sq_k), (s_qvar, s_sq_q))):
                        pe.wait_ge(squares, 1)
                        pe.wait_ge(s_kcopy, m + 1)
                        buf = sq if m == 0 else sd
                        for half in range(2):
                            for c in range(EC):
                                ins = pe.matmul(ps[:, 4 * m + 2 * c + half, 0:HALF], C("head_mean"),
                                                buf[:, c, hs_(half)], start=True, stop=True)
                        ins.then_inc(psum, 1)
                else:
                    pe.wait_ge(s_ld_a1, 16)
                    pe.wait_ge(s_x_ready, 4)
                    proj(wa1[:, 1], x, 0).then_inc(s_kraw, 1)
                    proj(wa1[:, 0], x, 4).then_inc(s_qraw, 1)
                pe.wait_ge(s_ld_a0v, 16)

                def scores(n, i):
                    if i >= 2:
                        pe.wait_ge(s_s_read if layer == 0 else s_sub_ready, n - 1)
                    for j in range(2):
                        b = 2 * i + j
                        for c in range(EC):
                            ins = pe.matmul(ps[QP * j:QP * j + QP, 2 * (i % 2) + c, 0:HPC * SEQ],
                                            qt[:, c, b * SEQ:b * SEQ + QP], kb[:, c, :, b * SEQ:(b + 1) * SEQ],
                                            start=True, stop=True)
                    ins.then_inc(s_s_psum, 1)

                def values(n, i):
                    if n:
                        pe.wait_ge(s_vm_ready, n)
                    for j in range(2):
                        pe.wait_ge(s_xr_ready, 2 * n + j + 1)
                        for k in range(EC):
                            ins = pe.matmul(ps[0:TRI * SEQ, 6, j * E:(j + 1) * E], xr[:, j, k, :], w[:, 2, k, :],
                                            start=(k == 0), stop=(k == EC - 1))
                    ins.then_inc(s_v_psum, 1)

                def turn(i):
                    n = n0 + i
                    if n:
                        pe.wait_ge(s_turned, n + layer)
                    if i < PAIRS:
                        pe.wait_ge(s_p_ready, n + 1)
                        for t in range(NTRI):
                            ins = pe.transpose(ps[0:TRI * SEQ, 4 + t // 3, (t % 3) * P:(t % 3 + 1) * P],
                                               psb[:, n % 2, TRI * t:TRI * t + TRI, :], ident)
                    if i >= 1:
                        pe.wait_ge(s_o_ready, n)
                        for c in range(EC):
                            ins = pe.transpose(ps[:, 4 + c, 3 * P:4 * P], osb[:, (n - 1) % 2, c * P:(c + 1) * P], ident)
                    ins.then_inc(s_turn_psum, 1)

                def weigh(n):
                    pe.wait_ge(s_turned, n + layer + 1)
                    pe.wait_ge(s_vm_ready, n + 1)
                    if n:
                        pe.wait_ge(s_o_ready, n)
                    for j in range(2):
                        for t in range(NTRI):
                            a, b_ = TRI * HD * t, min(TRI * HD * (t + 1), E)
                            ins = pe.matmul(ps[QP * j:QP * j + QP, 7, a:b_], pt[:, n % 2, t, QP * j:QP * j + QP],
                                            vm[:, n % 2, j, a:b_], start=True, stop=True)
                    ins.then_inc(s_o_psum, 1)

                n0 = PAIRS * layer
                pe.wait_ge(s_qk_ready, layer + 1)
                for i in range(PAIRS + 2):
                    if i < PAIRS:
                        scores(n0 + i, i)
                    if i >= 1:
                        turn(i - 1)
                    if i < PAIRS:
                        values(n0 + i, i)
                    if 1 <= i <= PAIRS:
                        weigh(n0 + i - 1)
                pe.wait_ge(s_turned, (PAIRS + 1) * (layer + 1))
                proj(w[:, 3], cx, 0).then_inc(s_u_psum, 1)

            attention(0)
            norm_stats(0)

            pe.wait_ge(s_ld_gc, 16)
            pe.wait_ge(s_gsum_ready, 1)
            for k in range(EC):
                ins = pe.matmul(ps[:, 3, 320:320 + B], gw1[:, k, :], gsum[:, k, :], start=(k == 0), stop=(k == EC - 1))
            ins.then_inc(s_g1p, 1)
            pe.wait_ge(s_g1r, 1)
            pe.matmul(ps[0:64, 3, 336:336 + B], gw2, gg1[:], start=True, stop=True).then_inc(s_g2p, 1)
            pe.wait_ge(s_g2r, 1)
            pe.matmul(ps[:, 3, 352:352 + B], gw3, gg2[:], start=True, stop=True).then_inc(s_g3p, 1)
            pe.wait_ge(s_ld_cn, 16)
            pe.wait_ge(s_g3r, 1)
            for cy in range(CYCLES):
                xin, _ = pass_io(cy)
                for half in range(2):
                    u = 2 * cy + half
                    if cy == 0:
                        pe.wait_ge(s_x_ready, half + 1)
                    else:
                        pe.wait_ge(s_f_ready, u - 1)
                    for c in range(EC):
                        for k in range(EC):
                            ins = pe.matmul(ps[:, 4 * half + c, 0:HALF], cw1[:, k, c * P:(c + 1) * P],
                                            xin[:, k, hs_(half)], start=(k == 0), stop=(k == EC - 1))
                    ins.then_inc(s_l1p, 1)
                for half in range(2):
                    pe.wait_ge(s_l1r, 2 * cy + half + 1)
                    for k in range(EC):
                        ins = pe.matmul(ps[:, 4 * half + 2, 0:HALF], cw2[:, k, :], g1[:, k, hs_(half)],
                                        start=(k == 0), stop=(k == EC - 1))
                    ins.then_inc(s_l2p, 1)
                for half in range(2):
                    pe.wait_ge(s_l2r, 2 * cy + half + 1)
                    pe.matmul(ps[0:64, 4 * half + 3, 0:HALF], cw3, g2[:, hs_(half)], start=True, stop=True)\
                      .then_inc(s_l3p, 1)
                for half in range(2):
                    pe.wait_ge(s_l3r, 2 * cy + half + 1)
                    pe.matmul(ps[:, 4 * half, 0:HALF], cw4, g3[:, hs_(half)], start=True, stop=True)\
                      .then_inc(s_l4p, 1)
            norm_stats(1)
            attention(1)
            norm_stats(2)

            both = C("to_both", NX)

            def route(step):
                if step == "scores":
                    pe.wait_ge(s_sc_ready, 1)
                    for i in range(TTN // 2):
                        ins = pe.transpose(ps[:, 3, i * TT:(i + 1) * TT],
                                           sc[:, i, :, :].rearrange("p h e -> p (h e)"), ident[0:TT, 0:TT])
                    ins.then_inc(s_tr_psum, 1)
                elif step == "shift":
                    pe.wait_ge(s_srt_ready, 1)
                    pe.matmul(ps[0:NX, 2, 0:HALF], ident[:, NX:P], srt[:], start=True, stop=True).then_inc(s_sh_psum, 1)
                elif step == "sums":
                    pe.wait_ge(s_st_ready, 1)
                    pe.matmul(ps[:, 1, 0:2 * NG], both, st[:], start=True, stop=True).then_inc(s_st_psum, 1)
                elif step == "groups":
                    pe.wait_ge(s_dg_ready, 1)
                    for j, bank in enumerate((0, 2)):
                        pe.matmul(ps[:, bank, 0:HALF], C("ones", NX),
                                  dg[:].rearrange("p g e -> p (g e)")[:, hs_(j)], start=True, stop=True)\
                          .then_inc(s_g_psum, 1)
                elif step == "selected":
                    pe.wait_ge(s_d_ready, 2)
                    pe.matmul(ps[:, 1, 0:NG], C("same_expert"), sel[:], start=True, stop=True).then_inc(s_d_psum, 1)
                elif step == "counts":
                    pe.wait_ge(s_cnt_ready, nk)
                    pe.matmul(ps[:, 2, 0:nk], C("same_expert"), cnt[:, 0:nk], start=True, stop=False)
                    pe.matmul(ps[:, 2, 0:nk], C("to_second"), cnt[:, nk:2 * nk], start=False, stop=True)\
                      .then_inc(s_cnt_psum, 1)
                elif step == "total":
                    pe.wait_ge(s_mk_ready, 1)
                    pe.matmul(ps[:, 3, 0:HALF], C("same_half"), msc[:], start=True, stop=True).then_inc(s_sum_psum, 1)

            pe.wait_ge(s_ld_wr, 32)
            pe.wait_ge(s_x_ready, 6)
            for i in range(TTN):
                for k in range(EC):
                    ins = pe.matmul(ps[0:TT, 3, i * NX:(i + 1) * NX], ha[:, k, i * TT:(i + 1) * TT], wr[:, k, :],
                                    start=(k == 0), stop=(k == EC - 1))
            ins.then_inc(s_lg_psum, 1)

            pe.wait_ge(s_xhi_ready, 1)
            pe.wait_ge(s_xlo_ready, 1)
            for u in range(WU):
                pe.wait_ge(s_whi_ready, u + 1)
                pe.wait_ge(s_wlo_ready, u + 1)
                if u >= 2:
                    pe.wait_ge(s_ug_ready, u - 1)
                for half in range(2):
                    for step, at in TURN.items():
                        if at == 2 * u + half:
                            route(step)
                    for k in range(EC):
                        for w_part, x_part in ((0, x_hi), (0, x_lo), (1, x_hi)):
                            ins = pe.matmul(ps[:, 4 + 2 * (u % 2) + half, 0:HALF],
                                            w_parts[:, u % WS, w_part, k * P:(k + 1) * P], x_part[:, k, hs_(half)],
                                            start=(k == 0 and w_part == 0 and x_part is x_hi),
                                            stop=(k == EC - 1 and w_part == 1))
                ins.then_inc(s_ug_psum, 1)
            for step, at in TURN.items():
                if at >= 2 * WU:
                    route(step)

            pe.wait_ge(s_fs_ready, 1)
            for p in range(XP):
                pe.wait_ge(s_whi_ready, WU + p + 1)
                pe.wait_ge(s_wlo_ready, WU + p + 1)
                pe.wait_ge(s_hhi_ready, p + 1)
                pe.wait_ge(s_hlo_ready, p + 1)
                for half in range(2):
                    for c in range(EC):
                        for w_part, h_part in ((0, 0), (0, 1), (1, 0)):
                            ins = pe.matmul(ps[:, 2 * c + half, 0:HALF],
                                            w_parts[:, (WU + p) % WS, w_part, c * P:(c + 1) * P],
                                            h_parts[:, p % HS, h_part, hs_(half)],
                                            start=(p == 0 and w_part == 0 and h_part == 0), stop=False)
                ins.then_inc(s_y_psum, 1)
            pe.wait_ge(s_ld_misc, 48)
            for half in range(2):
                for c in range(EC):
                    ins = pe.matmul(ps[:, 2 * c + half, 0:HALF], bdown[NX * half:NX * half + NX, c * P:(c + 1) * P],
                                    fst[NX * half:NX * half + NX, :], start=False, stop=True)
            ins.then_inc(s_y_psum, 1)
            pe.wait_ge(s_y_ready, 1)
            for i in range(TTN):
                for c in range(EC):
                    ins = pe.transpose(ps[0:TT, 4 + i // 2, (i % 2) * E + c * P:(i % 2) * E + (c + 1) * P],
                                       res[:, c, i * TT:(i + 1) * TT], ident)
                if i % 2:
                    ins.then_inc(s_yt_psum, 1)

        @block.scalar
        def _(act):
            act.wait_ge(s_ld_par, 16)
            act.wait_ge(s_ld_cst, 16)
            act.memzero(qt[:, :, NT:NT + QP]).then_inc(s_act_n, 1)
            for m in range(2):
                act.wait_ge(s_w_psum, m + 1)
                act.activation(wkc[:, m].rearrange("p c n -> p (c n)"), ps[:, 4 + m, :], ACT.Copy)\
                   .then_inc(s_w_ready, 1)

            def bank4(first, half=None):
                return ps[:, first:first + 4, 0:HALF].rearrange("p (c h) n -> p c h n", c=EC)

            def halves(x):
                return x[:, :, 0:NT].rearrange("p c (h n) -> p c h n", h=2)

            def norm(n):
                for half in range(2):
                    act.wait_ge(s_xc_ready, 2 * n + half + 1)
                    act.activation(sq[:, :, hs_(half)], xc[:, :, hs_(half)], ACT.Square).then_inc(s_sqn_ready, 1)
                for half in range(2):
                    act.wait_ge(s_var_psum, 2 * n + half + 1)
                    act.activation(sd[:, 0, hs_(half)], ps[:, 6 + half, 0:HALF], ACT.Sqrt, bias=C("eps"))\
                       .then_inc(s_sdn_ready, 1)

            def attention(layer):
                if layer == 0:
                    act.wait_ge(s_kcopy, 1)
                    act.activation(sq, kc[:], ACT.Square).then_inc(s_sq_k, 1)
                    act.wait_ge(s_kcopy, 2)
                    act.activation(sd, cx[:], ACT.Square).then_inc(s_sq_q, 1)
                    for m, (psum, done, buf) in enumerate(((s_kvar, s_sd_k, sq), (s_qvar, s_sd_q, sd))):
                        act.wait_ge(psum, 1)
                        for c in range(EC):
                            ins = act.activation(halves(buf)[:, c], bank4(4 * m)[:, c], ACT.Sqrt, bias=C("eps"))
                        ins.then_inc(done, 1)
                else:
                    for m, (psum, bias, buf) in enumerate(((s_kraw, "bk", kc), (s_qraw, "bq", cx))):
                        act.wait_ge(psum, 2)
                        for c in range(EC):
                            ins = act.activation(halves(buf)[:, c], bank4(4 * m)[:, c], ACT.Identity,
                                                 bias=par_col(bias + ("1" if c else "")))
                        ins.then_inc(s_qb_ready, 1)
                n0 = PAIRS * layer

                def exps(n):
                    act.wait_ge(s_sub_ready, n + 1)
                    if n >= 2:
                        act.wait_ge(s_turn_psum, n - 1 + layer)
                        act.wait_ge(s_rs_done, n - 1)
                    act.activation(psb[:, n % 2, 0:HEADS, :], ssb[:, n % 2], ACT.Exp, scale=0.25)\
                       .then_inc(s_p_ready, 1)

                def keep_turned(i):
                    n = n0 + i
                    act.wait_ge(s_turn_psum, n + layer + 1)
                    if i < PAIRS:
                        if n >= 2:
                            act.wait_ge(s_o_psum, n - 1)
                        ins = act.activation(pt[:, n % 2].rearrange("p (a t) q -> p a (t q)", a=2),
                                             ps[0:TRI * SEQ, 4:6, 0:3 * P], ACT.Copy)
                    if i >= 1:
                        for c in range(EC):
                            dst = cx[:, c, 2 * (i - 1) * SEQ:2 * i * SEQ].rearrange("p (j t) -> p j t", j=2)
                            src = ps[:, 4 + c, 3 * P:4 * P].rearrange("p (j q) -> p j q", j=2)[:, :, 0:SEQ]
                            if layer == 0:
                                ins = act.activation(dst, src, ACT.Copy)
                            else:
                                ins = act.activation(dst, src, ACT.Identity, bias=par_col("bv1" if c else "bv"))
                    ins.then_inc(s_turned, 1)

                for i in range(PAIRS + 2):
                    if i >= 1:
                        keep_turned(i - 1)
                    if i < PAIRS:
                        exps(n0 + i)

            attention(0)
            norm(0)
            act.wait_ge(s_g1p, 1)
            act.activation(gg1[:], ps[:, 3, 320:320 + B], ACT.Gelu, bias=par_col("gc_b1"), scale=1.0 / SEQ)\
               .then_inc(s_g1r, 1)
            act.wait_ge(s_g2p, 1)
            act.activation(gg2[:], ps[0:64, 3, 336:336 + B], ACT.Gelu, bias=par_col("gc_b2", 64)).then_inc(s_g2r, 1)
            act.wait_ge(s_g3p, 1)
            act.wait_ge(s_pool_ready, 1)
            act.activation(gth[:], ps[:, 3, 352:352 + B], ACT.Tanh, bias=gco[:, 1:2], scale=0.5).then_inc(s_g3r, 1)
            for cy in range(CYCLES):
                for half in range(2):
                    act.wait_ge(s_l1p, 2 * cy + half + 1)
                    for c in range(EC):
                        ins = act.activation(g1[:, c, hs_(half)], ps[:, 4 * half + c, 0:HALF], ACT.Gelu,
                                             bias=par_col("cn_b11" if c else "cn_b1"))
                    ins.then_inc(s_l1r, 1)
                for half in range(2):
                    act.wait_ge(s_l2p, 2 * cy + half + 1)
                    act.activation(g2[:, hs_(half)], ps[:, 4 * half + 2, 0:HALF], ACT.Gelu, bias=par_col("cn_b2"))\
                       .then_inc(s_l2r, 1)
                for half in range(2):
                    act.wait_ge(s_l3p, 2 * cy + half + 1)
                    act.activation(g3[:, hs_(half)], ps[0:64, 4 * half + 3, 0:HALF], ACT.Gelu,
                                   bias=par_col("cn_b3", 64)).then_inc(s_l3r, 1)
                for half in range(2):
                    act.wait_ge(s_l4p, 2 * cy + half + 1)
                    act.activation(th[:, hs_(half)], ps[:, 4 * half, 0:HALF], ACT.Tanh, bias=gco[:, 0:1], scale=0.5)\
                       .then_inc(s_th_ready, 1)
            norm(1)
            attention(1)
            norm(2)
            act.wait_ge(s_x_ready, 6)
            act.activation(x_hi, ha[:], ACT.Copy).then_inc(s_xhi_ready, 1)

            def split_weights(u):
                if u >= WS:
                    if u - WS < WU:
                        act.wait_ge(s_ug_psum, u - WS + 1)
                    else:
                        act.wait_ge(s_y_psum, u - WS - WU + 1)
                w_ = w_in[:, u].rearrange("p c n -> p (c n)") if u < WU else wdown[:, u - WU]
                act.activation(w_parts[:, u % WS, 0], w_, ACT.Copy).then_inc(s_whi_ready, 1)

            act.wait_ge(s_ld_in, 16)
            act.wait_ge(s_ld_down, 16)
            act.wait_ge(s_ld_misc, 48)
            for u in range(AHEAD):
                split_weights(u)
            act.wait_ge(s_lg_sub, 1)
            act.activation(sc[:].rearrange("p i h e -> p h i e"), lg[:].rearrange("p (h i) e -> p h i e", h=2),
                           ACT.Exp).then_inc(s_lg_exp, 1)
            def split_hidden(p):
                act.wait_ge(s_hw_ready, p + 1)
                if p >= HS:
                    act.wait_ge(s_y_psum, p - HS + 1)
                act.activation(h_parts[:, p % HS, 0], hw[p % 3], ACT.Copy).then_inc(s_hhi_ready, 1)

            for u in range(WU):
                split_weights(u + AHEAD)
                p = u // 2
                if u == WU - 2:
                    for q in range(HEAD):
                        split_hidden(q)
                act.wait_ge(s_ug_psum, u + 1)
                if p >= 2:
                    act.wait_ge(s_hh_ready, p - 1)
                bank = 4 + 2 * (u % 2)
                if u % 2 == 0:
                    act.activation(uu[:, p % 2].rearrange("p (h n) -> p h n", h=2), ps[:, bank:bank + 2, 0:HALF],
                                   ACT.Silu, bias=bup[:, p:p + 1]).then_inc(s_ug_ready, 1)
                else:
                    act.activation(vv[:, p % 2].rearrange("p (h n) -> p h n", h=2), ps[:, bank:bank + 2, 0:HALF],
                                   ACT.Identity, bias=bgate[:, p:p + 1]).then_inc(s_ug_ready, 1)
            for p in range(XP):
                if p >= HEAD:
                    split_hidden(p)
                if AHEAD <= p + 1 < XP:
                    split_weights(WU + p + 1)
            act.wait_ge(s_ag_ready, TTN)
            act.activation(sdf[:], ag[:, :, 1], ACT.Sqrt, bias=C("eps", TT)).then_inc(s_sdn_ready, 1)

        @block.gpsimd
        def _(pool):
            for j in range(2):
                pool.memset(psb[:, j, HEADS:NTRI * TRI, :], 0.0).then_inc(s_pool_n, 1)
            for layer in range(2):
                x = layer_in(layer)
                if layer == 0:
                    pool.wait_ge(s_h0_ready, 4)
                else:
                    pool.wait_ge(s_x_ready, 4)
                for i in range(PAIRS):
                    if layer or i:
                        pool.wait_ge(s_v_psum, PAIRS * layer + i)
                    for j in range(2):
                        b = 2 * i + j
                        rep = x[:, :, b * SEQ:(b + 1) * SEQ].unsqueeze(2).to_broadcast([P, EC, TRI, SEQ])
                        pool.tensor_copy(xr[:, j].rearrange("p k (r t) -> p k r t", r=TRI), rep).then_inc(s_xr_ready, 1)
            pool.wait_ge(s_ld_cst, 16)
            pool.wait_ge(s_x_ready, 6)
            pool.memset(sel[:], 0.0).then_inc(s_pool_n, 1)
            for i, (rows, first) in enumerate(((slice(0, NX), 0), (slice(NX, P), NG - NGH))):
                at = NT - NX + NX * first
                pool.wait_ge(s_pool_n, 3 + 3 * i)
                pool.memset(before[rows, 0:at], 1.0).then_inc(s_pool_n, 1)
                pool.tensor_copy(before[rows, at:at + NX], C("before")[rows, :]).then_inc(s_pool_n, 1)
                pool.memset(before[rows, at + NX:2 * NT - NX], 0.0).then_inc(s_pool_n, 1)
            pool.wait_ge(s_pool_n, 9)

            def split_weights(u):
                pool.wait_ge(s_whi_ready, u + 1)
                w_ = w_in[:, u].rearrange("p c n -> p (c n)") if u < WU else wdown[:, u - WU]
                pool.tensor_tensor(w_parts[:, u % WS, 1], w_, w_parts[:, u % WS, 0].bitcast(F32), ALU.subtract)\
                    .then_inc(s_wlo_ready, 1)

            for u in range(AHEAD):
                split_weights(u)
            for u in range(WU):
                split_weights(u + AHEAD)
                if u % 2:
                    p = u // 2
                    pool.wait_ge(s_ug_ready, u + 1)
                    pool.tensor_tensor(hh[:, p], uu[:, p % 2], vv[:, p % 2], ALU.mult).then_inc(s_hh_ready, 1)
            for p in range(XP - AHEAD):
                split_weights(WU + p + AHEAD)

        @block.vector
        def _(v):
            marked = [0]

            def mark(ins):
                marked[0] += 1
                return ins.then_inc(s_dve_n, 1)

            def chain(ins):
                mark(ins)
                v.wait_ge(s_dve_n, marked[0])

            v.wait_ge(s_ld_par, 16)
            v.wait_ge(s_ld_cst, 16)
            v.wait_ge(s_ld_pos, 16)
            v.wait_ge(s_pool_n, 2)
            chain(v.tensor_scalar(gco[:, 0:1], par_col("cn_b4"), 0.5, None, ALU.mult))
            v.tensor_scalar(gco[:, 1:2], par_col("gc_b3"), 0.5, None, ALU.mult).then_inc(s_pool_ready, 1)
            for c in range(EC):
                mark(v.tensor_scalar(posb[:, c], posb[:, c], par_col("b_proj1" if c else "b_proj"), None, ALU.add))
            v.wait_ge(s_dve_n, marked[0])
            v.wait_ge(s_tok_psum, 1)
            for c in range(EC):
                for half in range(2):
                    v.tensor_tensor(split(ha[:, c, hs_(half)]), split(ps[:, 2 * c + half, 0:HALF]),
                                    posb[:, c].unsqueeze(1).to_broadcast([P, B // 2, SEQ]), ALU.add)\
                     .then_inc(s_h0_ready, 1)

            def halves(x):
                return x[:, :, 0:NT].rearrange("p c (h n) -> p c h n", h=2)

            def norm(n, dst):
                for half in range(2):
                    v.wait_ge(s_mean_psum, 2 * n + half + 1)
                    v.wait_ge(s_r_ready, 2 * n + half + 1)
                    v.tensor_tensor(xc[:, :, hs_(half)], res[:, :, hs_(half)],
                                    ps[:, 4 + half, 0:HALF].unsqueeze(1).to_broadcast([P, EC, HALF]), ALU.subtract)\
                     .then_inc(s_xc_ready, 1)
                for half in range(2):
                    v.wait_ge(s_sdn_ready, 2 * n + half + 1)
                    chain(v.reciprocal(rs[:, 0, hs_(half)], sd[:, 0, hs_(half)]))
                    if half == 0:
                        v.wait_ge(s_xc_ready, 2 * n + 2)
                    v.tensor_tensor(dst[:, :, hs_(half)], xc[:, :, hs_(half)],
                                    rs[:, 0, hs_(half)].unsqueeze(1).to_broadcast([P, EC, HALF]), ALU.mult)\
                     .then_inc(s_x_ready, 1)

            def attention(layer):
                if layer == 0:
                    for j, col in enumerate(("kln_w", "kln_b")):
                        mark(v.tensor_scalar(scal[:, j], C("head_of"), par_col(col), None, ALU.mult))
                    v.wait_ge(s_kraw, 1)
                    for c in range(EC):
                        for half in range(2):
                            ins = v.tensor_copy(kc[:, c, hs_(half)], ps[:, 2 * c + half, 0:HALF])
                    ins.then_inc(s_kcopy, 1)
                    v.wait_ge(s_qraw, 1)
                    for c in range(EC):
                        for half in range(2):
                            ins = v.tensor_copy(cx[:, c, hs_(half)], ps[:, 4 + 2 * c + half, 0:HALF])
                    ins.then_inc(s_kcopy, 1)
                    v.wait_ge(s_kcopy, 2)
                    v.wait_ge(s_sd_k, 1)
                    chain(v.reciprocal(rs[:], sq[:]))
                    chain(v.tensor_tensor(kc[:], kc[:], rs[:], ALU.mult))
                    for h in range(HPC):
                        for c in range(EC):
                            mark(v.tensor_scalar(kb[:, c, h, :], kc[:, c, :], scal[:, 0, h:h + 1],
                                                     scal[:, 1, h:h + 1], ALU.mult, ALU.add))
                    v.wait_ge(s_sd_q, 1)
                    chain(v.reciprocal(rs[:], sd[:]))
                    chain(v.tensor_tensor(cx[:], cx[:], rs[:], ALU.mult))
                    v.wait_ge(s_act_n, 1)
                    v.tensor_scalar(qt[:, :, 0:NT], cx[:], par_col("qln_w"), par_col("qln_b"), ALU.mult, ALU.add)\
                     .then_inc(s_qk_ready, 1)
                else:
                    cosb = C("cos").unsqueeze(1).to_broadcast([P, EC * B, SEQ])
                    sinb = C("sin").unsqueeze(1).to_broadcast([P, EC * B, SEQ])

                    def blocks(x):
                        return x[:, :, 0:NT].rearrange("p c (b t) -> p (c b) t", t=SEQ) if x is not qt else None
                    v.wait_ge(s_qb_ready, 1)
                    chain(v.stream_shuffle(rs[:], kc[:], SHUFFLE))
                    mark(v.tensor_tensor(blocks(rs), blocks(rs), sinb, ALU.mult))
                    chain(v.tensor_tensor(blocks(kc), blocks(kc), cosb, ALU.mult))
                    chain(v.tensor_tensor(kc[:], kc[:], rs[:], ALU.add))
                    for h in range(HPC):
                        for c in range(EC):
                            mark(v.tensor_scalar(kb[:, c, h, :], kc[:, c, :], C("head_of")[:, h:h + 1], None,
                                                     ALU.mult))
                    v.wait_ge(s_qb_ready, 2)
                    v.wait_ge(s_dve_n, marked[0])
                    chain(v.stream_shuffle(rs[:], cx[:], SHUFFLE))
                    mark(v.tensor_tensor(blocks(rs), blocks(rs), sinb, ALU.mult))
                    chain(v.tensor_tensor(blocks(cx), blocks(cx), cosb, ALU.mult))
                    v.tensor_tensor(qt[:, :, 0:NT], cx[:], rs[:], ALU.add).then_inc(s_qk_ready, 1)

                n0 = PAIRS * layer

                def spread(a):
                    return a.unsqueeze(2).to_broadcast([P, HEADS, SEQ])

                def keep_values(n):
                    v.wait_ge(s_v_psum, n + 1)
                    if n >= 2:
                        v.wait_ge(s_o_psum, n - 1)
                    v.tensor_tensor(vm[:, n % 2], ps[0:TRI * SEQ, 6, :].rearrange("p (j e) -> p j e", j=2),
                                    C("v_mask", TRI * SEQ).unsqueeze(1).to_broadcast([TRI * SEQ, 2, E]), ALU.mult)\
                     .then_inc(s_vm_ready, 1)

                def shift(n, i):
                    a = n % 2
                    pss = ps[:, 2 * a:2 * a + 2, 0:HPC * SEQ].rearrange("p c (h t) -> p c h t", t=SEQ)
                    sh = ssb[:, a].rearrange("p (c h) t -> p c h t", c=EC)
                    v.wait_ge(s_s_psum, n + 1)
                    if n >= 2:
                        v.wait_ge(s_p_ready, n - 1)
                    if layer == 0:
                        causal = C("causal").unsqueeze(1).unsqueeze(1).to_broadcast([P, EC, HPC, SEQ])
                        v.tensor_tensor(sh, pss, causal, ALU.add).then_inc(s_s_read, 1)
                        v.wait_ge(s_s_read, n + 1)
                        chain(v.tensor_reduce(mx[:, a], ssb[:, a], AX.X, ALU.max))
                        v.tensor_tensor(ssb[:, a], ssb[:, a], spread(mx[:, a]), ALU.subtract).then_inc(s_sub_ready, 1)
                    else:
                        mv = mx[:, a].rearrange("p (c h) -> p c h", c=EC)
                        chain(v.tensor_reduce(mv, pss, AX.X, ALU.max))
                        v.tensor_tensor(sh, pss, mv.unsqueeze(3).to_broadcast([P, EC, HPC, SEQ]), ALU.subtract)\
                         .then_inc(s_sub_ready, 1)

                def sums(n):
                    a = n % 2
                    v.wait_ge(s_p_ready, n + 1)
                    v.tensor_reduce(sm[:, a], psb[:, a, 0:HEADS, :], AX.X, ALU.add).then_inc(s_rs_done, 1)
                    v.wait_ge(s_rs_done, n + 1)
                    chain(v.reciprocal(rc[:, a], sm[:, a]))

                def keep_weighed(n):
                    a = n % 2
                    v.wait_ge(s_o_psum, n + 1)
                    if n >= 2:
                        v.wait_ge(s_turn_psum, n + layer)
                    v.tensor_tensor(osb[:, a].rearrange("p (h d) -> p h d", d=HD),
                                    ps[:, 7, 0:E].rearrange("p (h d) -> p h d", d=HD),
                                    rc[:, a].unsqueeze(2).to_broadcast([P, HEADS, HD]), ALU.mult)\
                     .then_inc(s_o_ready, 1)

                for i in range(PAIRS + 1):
                    if i < PAIRS:
                        shift(n0 + i, i)
                    if i >= 1:
                        sums(n0 + i - 1)
                    if i < PAIRS:
                        keep_values(n0 + i)
                    if i >= 1:
                        keep_weighed(n0 + i - 1)
                v.wait_ge(s_u_psum, layer + 1)
                x = layer_in(layer)
                for half in range(2):
                    for c in range(EC):
                        if layer == 0:
                            ins = v.tensor_tensor(res[:, c, hs_(half)], ps[:, 2 * c + half, 0:HALF], x[:, c, hs_(half)],
                                                  ALU.add)
                        else:
                            ins = v.scalar_tensor_tensor(res[:, c, hs_(half)], ps[:, 2 * c + half, 0:HALF],
                                                         par_col("bo1" if c else "bo"), x[:, c, hs_(half)],
                                                         ALU.add, ALU.add)
                    ins.then_inc(s_r_ready, 1)

            attention(0)
            norm(0, hb)
            v.wait_ge(s_x_ready, 2)
            for c in range(EC):
                ins = v.tensor_reduce(gsum[:, c], split(hb[:, c, :]), AX.X, ALU.add)
            ins.then_inc(s_gsum_ready, 1)
            v.wait_ge(s_g3r, 1)
            chain(v.tensor_scalar(cg[:], gth[:], par_col("ar"), 0.7, ALU.mult, ALU.mult))
            mark(v.tensor_scalar(cg[:], cg[:], 0.1, None, ALU.add))
            chain(v.tensor_scalar(scal[:, 0, 0:1], par_col("ar"), 0.3, None, ALU.mult))
            for cy in range(CYCLES):
                xin, xout = pass_io(cy)
                for half in range(2):
                    u = 2 * cy + half
                    t_ = hs_(half)
                    v.wait_ge(s_th_ready, u + 1)
                    if cy > 0:
                        v.wait_ge(s_f_ready, u - 1)
                    cgb = cg[:, half * B // 2:(half + 1) * B // 2].unsqueeze(2).to_broadcast([P, B // 2, SEQ])
                    chain(v.scalar_tensor_tensor(split(co[:, t_]), split(th[:, t_]), scal[:, 0, 0:1], cgb,
                                                 ALU.mult, ALU.add))
                    mark(v.scalar_tensor_tensor(g1[:, 0, t_], xin[:, 1, t_], C("sign"), co[:, t_], ALU.mult, ALU.mult))
                    chain(v.scalar_tensor_tensor(g1[:, 1, t_], xin[:, 0, t_], C("minus_sign"), co[:, t_], ALU.mult, ALU.mult))
                    ins = v.tensor_tensor(xout[:, :, t_], xin[:, :, t_], g1[:, :, t_], ALU.add)
                    ins.then_inc(s_f_ready, 1)
            for half in range(2):
                v.wait_ge(s_f_ready, 2 * CYCLES - 1 + half)
                v.tensor_tensor(res[:, :, hs_(half)], res[:, :, hs_(half)], hb[:, :, hs_(half)], ALU.add)\
                 .then_inc(s_r_ready, 1)
            norm(1, hb)
            attention(1)
            norm(2, ha)

            v.wait_ge(s_xhi_ready, 1)
            v.tensor_tensor(x_lo, ha[:], x_hi.bitcast(F32), ALU.subtract).then_inc(s_xlo_ready, 1)

            v.wait_ge(s_lg_psum, 1)
            v.wait_ge(s_ld_wr, 32)
            chain(v.tensor_tensor(lg[:], ps[0:TT, 3, 0:TTN * NX].rearrange("p (i e) -> p i e", e=NX),
                                  br[:].unsqueeze(1).to_broadcast([TT, TTN, NX]), ALU.add))
            chain(v.tensor_reduce(lm[:], lg[:], AX.X, ALU.max))
            v.tensor_tensor(lg[:], lg[:], lm[:].unsqueeze(2).to_broadcast([TT, TTN, NX]), ALU.subtract)\
             .then_inc(s_lg_sub, 1)
            v.wait_ge(s_lg_exp, 1)
            chain(v.tensor_reduce(ls[:].rearrange("p (i h) -> p i h", h=2), sc[:], AX.X, ALU.add))
            chain(v.reciprocal(lr[:], ls[:]))
            flat = sc[:].rearrange("p i h e -> p (i h) e")
            v.tensor_tensor(flat, flat, lr[:].unsqueeze(2).to_broadcast([TT, TTN, NX]), ALU.mult)\
             .then_inc(s_sc_ready, 1)
            v.wait_ge(s_tr_psum, 1)
            mark(v.tensor_copy(wk[:], ps[:, 3, 0:HALF]))
            v.tensor_copy(se[:], ps[:, 3, 0:HALF]).then_inc(s_se_ready, 1)
            v.wait_ge(s_dve_n, marked[0])
            quarter = HALF // 2
            up_, down_ = wk[:, 0:quarter], wk[:, quarter:HALF]
            back = srt[:, ::-1]
            for k in range(quarter // 8):
                for q_, s_ in ((up_, srt), (down_, back)):
                    v.wait_ge(s_dve_n, marked[0] - 1)
                    mark(v.max(s_[:, 8 * k:8 * k + 8], q_))
                if k < quarter // 8 - 1:
                    for q_, s_ in ((up_, srt), (down_, back)):
                        v.wait_ge(s_dve_n, marked[0] - 1)
                        mark(v.match_replace(q_, s_[:, 8 * k:8 * k + 8], q_, -1.0))
            v.wait_ge(s_dve_n, marked[0])
            far = 256
            near = HALF - far
            mark(v.tensor_tensor(alt[:, far:HALF], srt[:, 0:near], srt[:, far:HALF], ALU.max))
            chain(v.tensor_tensor(srt[:, 0:near], srt[:, 0:near], srt[:, far:HALF], ALU.min))
            src, dst = srt, alt
            for m in (128, 64, 32, 16, 8, 4, 2, 1):
                n = far if m >= near else HALF
                a = src[:, 0:n].rearrange("p (n two m) -> p n two m", two=2, m=m)
                b_ = dst[:, 0:n].rearrange("p (n two m) -> p n two m", two=2, m=m)
                mark(v.tensor_tensor(b_[:, :, 0, :], a[:, :, 0, :], a[:, :, 1, :], ALU.min))
                ins = v.tensor_tensor(b_[:, :, 1, :], a[:, :, 0, :], a[:, :, 1, :], ALU.max)
                if m == 1:
                    ins.then_inc(s_srt_ready, 1)
                    v.wait_ge(s_srt_ready, 1)
                    v.wait_ge(s_dve_n, marked[0])
                else:
                    chain(ins)
                src, dst = dst, src
            mark(v.tensor_copy(ma[:, 0:HALF][:, ::-1], srt[0:NX, :]))
            v.wait_ge(s_sh_psum, 1)
            ins = v.tensor_copy(ma[:, HALF:NT], ps[0:NX, 2, 0:HALF])
            ins.then_inc(s_m_ready, 1)
            v.wait_ge(s_m_ready, 1)
            v.wait_ge(s_dve_n, marked[0])
            top = NT - GROUP
            mark(v.tensor_tensor(mb[:, top:NT], ma[:, 0:GROUP], ma[:, top:NT], ALU.max))
            chain(v.tensor_tensor(ma[:, 0:GROUP], ma[:, 0:GROUP], ma[:, top:NT], ALU.min))
            src, dst = ma, mb
            for m in (256, 128, 64):
                a = src[:, 0:512].rearrange("p (n two m) -> p n two m", two=2, m=m)
                b_ = dst[:, 0:512].rearrange("p (n two m) -> p n two m", two=2, m=m)
                mark(v.tensor_tensor(b_[:, :, 0, :], a[:, :, 0, :], a[:, :, 1, :], ALU.min))
                chain(v.tensor_tensor(b_[:, :, 1, :], a[:, :, 0, :], a[:, :, 1, :], ALU.max))
                src, dst = dst, src
            blocks_ = src[:].rearrange("p (g n) -> p g n", n=GROUP)
            mark(v.tensor_reduce(st[:, 0:NG][:, ::-1], blocks_, AX.X, ALU.add))
            ins = v.tensor_reduce(st[:, NG:2 * NG][:, ::-1], blocks_, AX.X, ALU.min)
            ins.then_inc(s_st_ready, 1)
            v.wait_ge(s_dve_n, marked[0])
            v.tensor_tensor(dg[:], ident[0:NX, 0:NX].unsqueeze(1).to_broadcast([NX, NG, NX]),
                            st[:, 0:NG].unsqueeze(2).to_broadcast([NX, NG, NX]), ALU.mult).then_inc(s_dg_ready, 1)
            v.wait_ge(s_st_psum, 1)
            mark(v.tensor_copy(st2[:], ps[:, 1, 0:2 * NG]))
            mark(v.tensor_copy(st3[0:NX, :], ps[0:NX, 1, 0:NGH]))
            mark(v.tensor_copy(st3[NX:P, :], ps[NX:P, 1, NG - NGH:NG]))
            v.wait_ge(s_dve_n, marked[0])
            v.wait_ge(s_g_psum, 2)
            v.wait_ge(s_pool_n, 9)
            gall = ps[:, 0:3:2, 0:HALF]
            for g in range(NGH):
                v.tensor_scalar(junk[:].rearrange("p (j n) -> p j n", j=2), gall, st3[:, g:g + 1], None,
                                ALU.is_gt, ALU.add, accum_out=rank[:, g:g + 1]).then_inc(s_rank_ready, 1)
                at = NT - NX - NX * g
                earlier = before[:, at:at + NT].rearrange("p (j n) -> p j n", j=2)
                if g:
                    v.wait_ge(s_dve_n, marked[0])
                mark(v.scalar_tensor_tensor(junk2[:].rearrange("p (j n) -> p j n", j=2), gall, st3[:, g:g + 1], earlier,
                                            ALU.is_equal, ALU.mult, accum_out=rank[:, NGH + g:NGH + g + 1]))
                v.wait_ge(s_rank_ready, g + 1)
            v.wait_ge(s_dve_n, marked[0])
            chain(v.tensor_tensor(rank[:, 0:NGH], rank[:, 0:NGH], rank[:, NGH:2 * NGH], ALU.add))
            v.tensor_scalar(sel[0:NX, 0:NGH], rank[0:NX, 0:NGH], float(BUDGET), None, ALU.is_lt).then_inc(s_d_ready, 1)
            v.tensor_scalar(sel[NX:P, NGH:NG], rank[NX:P, 2 * NGH - NG:NGH], float(BUDGET), None, ALU.is_lt)\
             .then_inc(s_d_ready, 1)
            for k in range(nk):
                mark(v.tensor_scalar(gt[:, k], se[:], st2[:, NG + k:NG + k + 1], None, ALU.is_gt, ALU.add,
                                         accum_out=cnt[:, k:k + 1]))
                v.tensor_scalar(eq[:, k], se[:], st2[:, NG + k:NG + k + 1], None, ALU.is_equal, ALU.add,
                                accum_out=cnt[:, nk + k:nk + k + 1]).then_inc(s_cnt_ready, 1)
            v.wait_ge(s_d_psum, 1)
            mark(v.tensor_copy(sel2[:], ps[:, 1, 0:NG]))
            v.wait_ge(s_cnt_psum, 1)
            mark(v.tensor_copy(base[:], ps[:, 2, 0:nk]))
            v.wait_ge(s_dve_n, marked[0])
            mark(v.tensor_tensor(dsel[:, 0:nk], sel2[:, 0:nk], sel2[:, 1:NG], ALU.subtract))
            mark(v.tensor_scalar(mask[:], se[:], 0.0, sel2[:, nk:NG], ALU.mult, ALU.add))
            mark(v.tensor_scalar(mask2[:], se[:], 0.0, None, ALU.mult))
            v.wait_ge(s_dve_n, marked[0])
            for k in range(nk + 1):
                if k < nk:
                    v.wait_ge(s_dve_n, marked[0] - 1)
                    mark(v.tensor_tensor_scan(cum[:, k % 2], eq[:, k], C("ones")[:, 0:1].to_broadcast([P, HALF]),
                                              base[:, k:k + 1], ALU.add, ALU.mult))
                if k >= 1:
                    v.wait_ge(s_dve_n, marked[0] - (1 if k < nk else 0))
                    mark(v.scalar_tensor_tensor(mask2[:], ine[:, (k - 1) % 2], dsel[:, k - 1:k], mask2[:], ALU.mult, ALU.add))
                if k < nk:
                    v.wait_ge(s_dve_n, marked[0] - 1)
                    mark(v.scalar_tensor_tensor(mask[:], gt[:, k], dsel[:, k:k + 1], mask[:], ALU.mult, ALU.add))
                    v.wait_ge(s_dve_n, marked[0] - 1)
                    mark(v.scalar_tensor_tensor(ine[:, k % 2], cum[:, k % 2], float(GROUP * (k + 1)), eq[:, k],
                                                ALU.is_le, ALU.mult))
            v.wait_ge(s_dve_n, marked[0])
            chain(v.tensor_tensor(mask[:], mask[:], mask2[:], ALU.add))
            v.tensor_tensor(msc[:], mask[:], se[:], ALU.mult).then_inc(s_mk_ready, 1)
            v.wait_ge(s_sum_psum, 1)
            chain(v.tensor_scalar(rden[:], ps[:, 3, 0:HALF], 1e-6, None, ALU.add))
            chain(v.reciprocal(rden[:], rden[:]))
            v.wait_ge(s_mk_ready, 1)
            v.tensor_tensor(fst[:], msc[:], rden[:], ALU.mult).then_inc(s_fs_ready, 1)

            for p in range(XP + LAG):
                if p < XP:
                    v.wait_ge(s_hh_ready, p + 1)
                    v.wait_ge(s_fb_ld[p // FP % FB], 32 * (p // FP // FB + 1))
                    if p >= 3:
                        v.wait_ge(s_hlo_ready, p - 2)
                    v.tensor_tensor(hw[p % 3], hh[:, p], fb[:, p // FP % FB, p % FP], ALU.mult).then_inc(s_hw_ready, 1)
                if p >= LAG:
                    q = p - LAG
                    v.wait_ge(s_hhi_ready, q + 1)
                    v.tensor_tensor(h_parts[:, q % HS, 1], hw[q % 3], h_parts[:, q % HS, 0].bitcast(F32), ALU.subtract)\
                     .then_inc(s_hlo_ready, 1)
            v.wait_ge(s_y_psum, XP + 1)
            for c in range(EC):
                ins = v.tensor_tensor(res[:, c].rearrange("p (h n) -> p h n", h=2), ps[:, 2 * c:2 * c + 2, 0:HALF],
                                      ha[:, c].rearrange("p (h n) -> p h n", h=2), ALU.add)
            ins.then_inc(s_y_ready, 1)
            for i in range(TTN):
                v.wait_ge(s_yt_psum, i // 2 + 1)
                chain(v.bn_stats(bn[:, i], ps[0:TT, 4 + i // 2, (i % 2) * E:(i % 2 + 1) * E]))
                v.bn_aggr(ag[:, i], bn[:, i]).then_inc(s_ag_ready, 1)
            v.wait_ge(s_sdn_ready, 7)
            chain(v.reciprocal(rsf[:], sdf[:]))
            for i in range(TTN):
                v.tensor_scalar(ofin[:, i], ps[0:TT, 4 + i // 2, (i % 2) * E:(i % 2 + 1) * E], ag[:, i, 0:1],
                                rsf[:, i:i + 1], ALU.subtract, ALU.mult).then_inc(s_out_ready, 1)


def _layout(a):
    def chunks(w):
        return np.ascontiguousarray(w.reshape(-1, P, w.shape[1]).transpose(1, 0, 2))

    x = a["x"].reshape(B, 6, 16, 6, 16, 3).transpose(2, 4, 5, 0, 1, 3).reshape(768, NT)
    cols = {
        "kln_w": np.tile(a["L0_attn_kln_w"], HPC), "kln_b": np.tile(a["L0_attn_kln_b"], HPC),
        "qln_w": np.tile(a["L0_attn_qln_w"], HPC), "qln_b": np.tile(a["L0_attn_qln_b"], HPC),
        "b_proj": a["L0_tok_b_proj"], "cn_b1": a["L0_ffn_cn_b1"], "cn_b2": a["L0_ffn_cn_b2"],
        "cn_b3": a["L0_ffn_cn_b3"], "cn_b4": np.tile(a["L0_ffn_cn_b4"], P), "gc_b1": a["L0_ffn_gc_b1"],
        "gc_b2": a["L0_ffn_gc_b2"], "gc_b3": np.tile(a["L0_ffn_gc_b3"], P), "ar": np.tile(a["L0_ffn_adaptive_range"], P),
        "bq": a["L1_attn_bq"], "bk": a["L1_attn_bk"], "bv": a["L1_attn_bv"], "bo": a["L1_attn_bo"],
    }
    par = np.zeros((P, NPAR), np.float32)
    for name, v in cols.items():
        for c in range(-(-len(v) // P)):
            part = v[c * P:(c + 1) * P]
            par[:len(part), PCOL[name + ("1" if c else "")]] = part

    def top(w, rows=P):
        full = np.zeros((rows, w.shape[1]), np.float32)
        full[:w.shape[0]] = w
        return full

    cw = np.concatenate([chunks(a["L0_ffn_cn_w1"]).reshape(P, -1), chunks(a["L0_ffn_cn_w2"]).reshape(P, -1),
                         a["L0_ffn_cn_w3"], top(np.tile(a["L0_ffn_cn_w4"], (1, P)))], axis=1)
    gw = np.concatenate([chunks(a["L0_ffn_gc_w1"]).reshape(P, -1), a["L0_ffn_gc_w2"],
                         top(np.tile(a["L0_ffn_gc_w3"], (1, P)))], axis=1)

    def experts_in(w):
        return w.reshape(XP, 2, EC, P, XH).transpose(3, 0, 2, 1, 4).reshape(P, XP, E)

    return {
        "cst": CONST, "par": par, "patches": chunks(x), "w_proj": chunks(a["L0_tok_W_proj"].T),
        "pos": chunks(a["L0_tok_pos_emb"].T),
        "wa0": np.stack([chunks(a["L0_attn_Wk"]), chunks(a["L0_attn_Wq"]), chunks(a["L0_attn_Wv"].T),
                         chunks(a["L0_attn_Wu"].T)], axis=1),
        "wa1": np.stack([chunks(a["L1_attn_" + n]) for n in ("Wq", "Wk", "Wv", "Wo")], axis=1),
        "cw": cw, "gw": gw, "wr": chunks(a["L1_ffn_Wr"]), "br": np.tile(a["L1_ffn_br"][None, :], (TT, 1)),
        "bdown": np.tile(a["L1_ffn_bdown"], (2, 1)), "bup": a["L1_ffn_bup"].reshape(XP, P).T,
        "bgate": a["L1_ffn_bgate"].reshape(XP, P).T,
        "w_in": np.stack([experts_in(a["L1_ffn_Wup"]), experts_in(a["L1_ffn_Wgate"])], axis=2).reshape(P, WU * E),
        "wdown": a["L1_ffn_Wdown"].reshape(XP, P, E).transpose(1, 0, 2),
    }


def kernel(**inputs):
    import concourse.bacc as _bacc
    from concourse.bass_utils import run_bass_kernel_spmd as _run

    arrays = {k: np.ascontiguousarray(v) for k, v in _layout({k: np.asarray(v) for k, v in inputs.items()}).items()}
    nc = _bacc.Bacc("TRN2", target_bir_lowering=False, num_devices=1)
    d = {k: nc.dram_tensor(k + "_in", v.shape, F32, kind="ExternalInput").ap() for k, v in arrays.items()}
    out = nc.dram_tensor("out", (NT, E), F32, kind="ExternalOutput").ap()
    build(nc, d, out)
    r = _run(nc, [{k + "_in": v for k, v in arrays.items()}], core_ids=[0])
    return r.results[0]["out"].reshape(B, SEQ, E)
```

```python
from contextlib import ExitStack

import numpy as np

import concourse.bass as bass
from concourse import mybir

F32 = mybir.dt.float32
F32R = mybir.dt.float32r
ALU = mybir.AluOpType
ACT = mybir.ActivationFunctionType
AX = mybir.AxisListType

P = 128
B, SEQ, E = 16, 36, 256
NT = B * SEQ
HALF = NT // 2
EC = E // P
KD = 768 // P
HEADS, HD = 16, 16
HPC = P // HD
QP = 64
QT = NT // 4
POOL_HEADS = (4, 2)
DVE_HEADS = 4
PAIRS = B // 2
TRI = 3
NTRI = 6
TT, TTN = 96, 6
NX, XH = 64, 64
XP = NX // 2
GROUP = 64
NG = NT // GROUP
NGH = (NG + 1) // 2
BUDGET = NG * 16
EPS = 1e-5
NEG = -1e30
CYCLES = 3
DVE_TILES, ACT_TILES = (0, 1, 2, 3), (4, 5)
STORES = (0, 4, 1, 5, 2, 3)
WU = 2 * XP
WS = 4
HS = 4
HEAD = 1
LAG = 2
AHEAD = 3
TURN = {"scores": 8, "shift": 41, "sums": 48, "groups": 51, "selected": 65, "counts": 74, "total": 98}
FB = 3
FP = 2

CST = {}


def _constants():
    parts = []
    at = 0

    def put(name, a):
        nonlocal at
        full = np.zeros((P, a.shape[1]), np.float32)
        full[:a.shape[0]] = a
        CST[name] = (at, a.shape[1])
        parts.append(full)
        at += a.shape[1]

    p = np.arange(P)
    same_head = (p[:, None] // HD == p[None, :] // HD).astype(np.float32)
    put("center", np.eye(P, dtype=np.float32) - same_head / HD)
    put("ident", np.eye(P, dtype=np.float32))
    row = np.arange(32)
    put("head_rows", np.concatenate([(row[None, :] % (HPC * EC) == c * HPC + p[:, None] // HD) / HD
                                     for c in range(EC)], axis=1))
    put("head_back", np.concatenate([p[:, None] % 32 == c * HPC + p[None, :] // HD for c in range(EC)], axis=1))
    put("all_mean", np.full((P, P), 1.0 / E, np.float32))
    put("ones", np.ones((P, P), np.float32))
    put("same_half", (p[:, None] // NX == p[None, :] // NX).astype(np.float32))
    put("same_expert", (p[:, None] % NX == p[None, :] % NX).astype(np.float32))
    put("v_mask", np.concatenate([((c * HPC + p[:, None] // HD) % TRI == np.arange(TRI)[None, :]) for c in range(EC)],
                                 axis=1))
    q = p % QP
    causal = np.where((np.arange(SEQ)[None, :] > q[:, None]) & (q[:, None] < SEQ), NEG, 0.0)
    put("causal", causal.astype(np.float32))
    put("head_of", (p[:, None] // HD == np.arange(HPC)[None, :]).astype(np.float32))
    put("sign", np.where(p < 64, 1.0, -1.0).astype(np.float32)[:, None])
    put("minus_sign", np.where(p < 64, -1.0, 1.0).astype(np.float32)[:, None])
    put("eps", np.full((P, 1), EPS, np.float32))
    half = HD // 2
    inv = (np.float32(1.0) / np.float32(10000.0) ** (np.arange(0, HD, 2, dtype=np.float32) / np.float32(HD))).astype(np.float32)
    ang = (np.arange(SEQ, dtype=np.float32)[None, :] * inv[:, None]).astype(np.float32)
    put("cos", np.cos(ang)[p % half])
    put("sin", np.sin(ang)[p % half] * np.where(p % HD < half, -1.0, 1.0)[:, None].astype(np.float32))
    put("before", (np.arange(NX)[None, :] < (p % NX)[:, None]).astype(np.float32))
    return np.concatenate(parts, axis=1)


CONST = _constants()

PAR = ["kln_w", "kln_b", "qln_w", "qln_b", "b_proj", "b_proj1", "cn_b1", "cn_b11", "cn_b2", "cn_b3", "cn_b4",
       "gc_b1", "gc_b2", "gc_b3", "ar", "bq", "bq1", "bk", "bk1", "bv", "bv1", "bo", "bo1"]
PCOL = {n: i for i, n in enumerate(PAR)}
NPAR = len(PAR)
SHUFFLE = [p - 8 if p % 16 >= 8 else p + 8 for p in range(32)]


def build(nc, d, out):
    ctx = ExitStack()
    with ctx:
        def sb(name, shape, dt=F32):
            return ctx.enter_context(nc.sbuf_tensor(name, shape, dt))

        def sem(name):
            return ctx.enter_context(nc.semaphore(name))

        ps = ctx.enter_context(nc.psum_tensor("ps", [P, 8, 512], F32))
        big_at = -(-nc.sbuf_base // 32) * 32
        big = sb("big", [P, EC * HPC * NT])
        tmp = sb("tmp", [P, 4224])
        cst = sb("cst", [P, CONST.shape[1]])
        par = sb("par", [P, NPAR])
        posb = sb("posb", [P, EC, SEQ])
        into = sb("into", [P, 4 * EC * E + WU * E])
        wa0 = into[:, 0:4 * EC * E].rearrange("p (m c n) -> p m c n", m=4, c=EC)
        wa1 = wa0
        w_in = into[:, 4 * EC * E:].rearrange("p (u c n) -> p u c n", c=EC, n=P)
        hh = into[:, 0:XP * NT].rearrange("p (x n) -> p x n", n=NT)
        cw = sb("cw", [P, 2 * E + 2 * P + 64 + P])
        gw = sb("gw", [P, 2 * P + 64 + P])
        wr = sb("wr", [P, EC, NX])
        br = sb("br", [TT, NX])
        bdown = sb("bdown", [P, E])
        bup = sb("bup", [P, XP])
        bgate = sb("bgate", [P, XP])
        wdown = sb("wdown", [P, XP, E])

        ha = sb("ha", [P, EC, NT])
        hb = sb("hb", [P, EC, NT])
        res = sb("res", [P, EC, NT])
        xc = sb("xc", [P, EC, NT])
        qt = sb("qt", [P, EC, NT + QP])
        kc = res

        def part(area, at, *shape, rows=P):
            n = int(np.prod(shape))
            flat = area[0:rows, at:at + n]
            if len(shape) == 1:
                return flat
            axes = "abcd"[:len(shape)]
            return flat.rearrange(f"p ({' '.join(axes)}) -> p {' '.join(axes)}",
                                  **{x: k for x, k in zip(axes[1:], shape[1:])})

        patches = part(big, 0, KD, NT)
        w_proj = part(big, KD * NT, KD, E)
        wkc = part(big, KD * (NT + E), 2, EC, E)
        kb = part(big, 0, EC, HPC, NT)
        sq = part(tmp, 0, EC, NT)
        sd = part(tmp, EC * NT, EC, NT)
        rs = part(tmp, 2 * EC * NT, EC, NT)
        hsd = part(tmp, 2 * EC * NT, 2, QT)
        hrs = part(tmp, 2 * EC * NT + 2 * QT, 2, QT)
        scal = sb("scal", [P, 2, HPC])
        xr = sb("xr", [P, 2, EC, TRI * SEQ])
        vm = part(tmp, 0, 2, 2, E, rows=TRI * SEQ)
        ssb = part(tmp, 1024, 2, HEADS, SEQ)
        pt = part(tmp, 2176, 2, NTRI, P, rows=TRI * SEQ)
        osb = part(tmp, 3712, 2, E)
        psb = sb("psb", [P, 2, NTRI * TRI, SEQ])
        mx = sb("mx", [P, 2, HEADS])
        sm = sb("sm", [P, 2, HEADS])
        rc = sb("rc", [P, 2, HEADS])
        cx = sb("cx", [P, EC, NT])

        g1 = part(big, 0, EC, NT)
        g2 = part(big, 2 * NT, NT)
        g3 = part(big, 3 * NT, NT, rows=64)
        th = part(big, 4 * NT, NT)
        co = part(big, 5 * NT, NT)
        gsum = sb("gsum", [P, EC, B])
        gg1 = sb("gg1", [P, B])
        gg2 = sb("gg2", [64, B])
        gth = sb("gth", [P, B])
        gco = sb("gco", [P, 2])
        cg = sb("cg", [P, B])
        nk = NG - 1
        lg = part(tmp, 0, TTN, NX, rows=TT)
        sc = part(tmp, 384, TTN // 2, 2, NX, rows=TT)
        se = part(tmp, 768, HALF)
        wk = part(tmp, 1056, HALF)
        srt = part(tmp, 1344, HALF)
        alt = part(tmp, 3648, HALF)
        junk = part(tmp, 1632, NT)
        junk2 = part(tmp, 2208, NT)
        cum = part(tmp, 1632, 2, HALF)
        ine = part(tmp, 2208, 2, HALF)
        mask = part(tmp, 2784, HALF)
        msc = part(tmp, 3072, HALF)
        rden = part(tmp, 3360, HALF)
        ma = cx[0:NX, 0, :]
        mb = cx[0:NX, 1, :]
        dg = kc[0:NX, 0, :].rearrange("p (g e) -> p g e", e=NX)
        mask2 = kc[:, 1, 0:HALF]
        eq = part(big, 0, nk, HALF)
        gt = part(big, nk * HALF, nk, HALF)
        lm = sb("lm", [TT, TTN])
        ls = sb("ls", [TT, TTN])
        lr = sb("lr", [TT, TTN])
        st = sb("st", [NX, 2 * NG])
        st2 = sb("st2", [P, 2 * NG])
        st3 = sb("st3", [P, NGH])
        rank = sb("rank", [P, 2 * NGH])
        sel = sb("sel", [P, NG])
        sel2 = sb("sel2", [P, NG])
        dsel = sb("dsel", [P, NG])
        cnt = sb("cnt", [P, 2 * nk])
        base = sb("base", [P, nk])
        fs_dram = nc.dram_tensor("fs_dram", (NX, NT), F32, kind="Internal").ap()
        fb = part(tmp, 0, FB, FP, NT)
        fst = sb("fst", [P, HALF])
        uu = qt[:].rearrange("p c n -> p (c n)")[:, 0:2 * NT].rearrange("p (s n) -> p s n", s=2)
        vv = hb
        hw = [xc[:, 0], xc[:, 1], part(tmp, FB * FP * NT, NT)]
        h_parts = nc.alloc_sbuf_tensor_at("h_parts", [P, HS, 2, NT], F32R, offset=big_at)
        before = xc[:].rearrange("p c n -> p (c n)")[:, 0:2 * NT - NX]
        parts = nc.alloc_sbuf_tensor_at("parts", [P, 2 * EC * NT + WS * 2 * E], F32R, offset=big_at + 4 * 2 * nk * HALF)
        x_hi = parts[:, 0:EC * NT].rearrange("p (c n) -> p c n", c=EC)
        x_lo = parts[:, EC * NT:2 * EC * NT].rearrange("p (c n) -> p c n", c=EC)
        w_parts = parts[:, 2 * EC * NT:].rearrange("p (s part n) -> p s part n", s=WS, part=2)
        ofin = part(big, 0, TTN, E, rows=TT)
        bn = sb("bn", [TT, TTN, 6])
        ag = sb("ag", [TT, TTN, 2])
        sdf = sb("sdf", [TT, TTN])
        rsf = sb("rsf", [TT, TTN])
        nmr = sb("nmr", [TT, TTN])

        def C(name, rows=P):
            a, n = CST[name]
            return cst[0:rows, a:a + n]

        def par_col(name, rows=P):
            return par[0:rows, PCOL[name]:PCOL[name] + 1]

        ident = C("ident")

        s_ld_cst = sem("s_ld_cst")
        s_ld_par = sem("s_ld_par")
        s_ld_pos = sem("s_ld_pos")
        s_ld_a0k = sem("s_ld_a0k")
        s_ld_a0v = sem("s_ld_a0v")
        s_ld_cn = sem("s_ld_cn")
        s_ld_gc = sem("s_ld_gc")
        s_ld_a1 = sem("s_ld_a1")
        s_ld_wr = sem("s_ld_wr")
        s_ld_misc = sem("s_ld_misc")
        s_ld_in = sem("s_ld_in")
        s_ld_down = sem("s_ld_down")
        s_w_psum = sem("s_w_psum")
        s_w_ready = sem("s_w_ready")
        s_tok_psum = sem("s_tok_psum")
        s_h0_ready = sem("s_h0_ready")
        s_kraw = sem("s_kraw")
        s_qraw = sem("s_qraw")
        s_kcopy = sem("s_kcopy")
        s_sq_k = sem("s_sq_k")
        s_sq_q = sem("s_sq_q")
        s_kvar = sem("s_kvar")
        s_bn_ready = sem("s_bn_ready")
        s_rsf_ready = sem("s_rsf_ready")
        s_out_act_ready = sem("s_out_act_ready")
        s_y_done = sem("s_y_done")
        s_pt_ready = sem("s_pt_ready")
        s_ld_center = sem("s_ld_center")
        s_vt_psum = sem("s_vt_psum")
        s_vt_ready = sem("s_vt_ready")
        s_back_first = sem("s_back_first")
        s_rope_n = sem("s_rope_n")
        s_qswap_ready = sem("s_qswap_ready")
        s_q1_psum = sem("s_q1_psum")
        s_k1_psum = sem("s_k1_psum")
        s_kb2_ready = sem("s_kb2_ready")
        s_kb_ready = sem("s_kb_ready")
        s_q_ready = sem("s_q_ready")
        s_qhat_ready = sem("s_qhat_ready")
        s_khat_ready = sem("s_khat_ready")
        s_back_psum = sem("s_back_psum")
        s_hrs_ready = sem("s_hrs_ready")
        s_hsd_ready = sem("s_hsd_ready")
        s_scal_ready = sem("s_scal_ready")
        s_qvar = sem("s_qvar")
        s_xr_ready = sem("s_xr_ready")
        s_fs_stored = sem("s_fs_stored")
        s_s_psum = sem("s_s_psum")
        s_s_read = sem("s_s_read")
        s_sub_ready = sem("s_sub_ready")
        s_p_ready = sem("s_p_ready")
        s_v_psum = sem("s_v_psum")
        s_vm_ready = sem("s_vm_ready")
        s_turn_psum = sem("s_turn_psum")
        s_turned = sem("s_turned")
        s_o_psum = sem("s_o_psum")
        s_o_ready = sem("s_o_ready")
        s_rs_done = sem("s_rs_done")
        s_u_psum = sem("s_u_psum")
        s_r_ready = sem("s_r_ready")
        s_mean_psum = sem("s_mean_psum")
        s_xc_ready = sem("s_xc_ready")
        s_sqn_ready = sem("s_sqn_ready")
        s_var_psum = sem("s_var_psum")
        s_sdn_ready = sem("s_sdn_ready")
        s_x_ready = sem("s_x_ready")
        s_pool_ready = sem("s_pool_ready")
        s_gsum_ready = sem("s_gsum_ready")
        s_g1p = sem("s_g1p")
        s_g1r = sem("s_g1r")
        s_g2p = sem("s_g2p")
        s_g2r = sem("s_g2r")
        s_g3p = sem("s_g3p")
        s_g3r = sem("s_g3r")
        s_l1p = sem("s_l1p")
        s_l1r = sem("s_l1r")
        s_l2p = sem("s_l2p")
        s_l2r = sem("s_l2r")
        s_l3p = sem("s_l3p")
        s_l3r = sem("s_l3r")
        s_l4p = sem("s_l4p")
        s_th_ready = sem("s_th_ready")
        s_f_ready = sem("s_f_ready")
        s_qb_ready = sem("s_qb_ready")
        s_lg_psum = sem("s_lg_psum")
        s_lg_sub = sem("s_lg_sub")
        s_lg_exp = sem("s_lg_exp")
        s_sc_ready = sem("s_sc_ready")
        s_tr_psum = sem("s_tr_psum")
        s_se_ready = sem("s_se_ready")
        s_srt_ready = sem("s_srt_ready")
        s_sh_psum = sem("s_sh_psum")
        s_m_ready = sem("s_m_ready")
        s_st_ready = sem("s_st_ready")
        s_st_psum = sem("s_st_psum")
        s_dg_ready = sem("s_dg_ready")
        s_g_psum = sem("s_g_psum")
        s_d_ready = sem("s_d_ready")
        s_rank_ready = sem("s_rank_ready")
        s_d_psum = sem("s_d_psum")
        s_cnt_ready = sem("s_cnt_ready")
        s_cnt_psum = sem("s_cnt_psum")
        s_mk_ready = sem("s_mk_ready")
        s_sum_psum = sem("s_sum_psum")
        s_fs_ready = sem("s_fs_ready")
        s_ug_psum = sem("s_ug_psum")
        s_ug_ready = sem("s_ug_ready")
        s_hh_ready = sem("s_hh_ready")
        s_xhi_ready = sem("s_xhi_ready")
        s_xlo_ready = sem("s_xlo_ready")
        s_whi_ready = sem("s_whi_ready")
        s_wlo_ready = sem("s_wlo_ready")
        s_hw_ready = sem("s_hw_ready")
        s_hhi_ready = sem("s_hhi_ready")
        s_hlo_ready = sem("s_hlo_ready")
        s_y_psum = sem("s_y_psum")
        s_y_ready = sem("s_y_ready")
        s_ag_ready = sem("s_ag_ready")
        s_yt_psum = sem("s_yt_psum")
        s_out_ready = sem("s_out_ready")
        s_stored = sem("s_stored")
        s_dve_n = sem("s_dve_n")
        s_act_n = sem("s_act_n")
        s_pool_n = sem("s_pool_n")
        s_ld_x = [sem(f"s_ld_x{i}") for i in range(3)]
        s_fb_ld = [sem(f"s_fb_ld{i}") for i in range(FB)]
        block = ctx.enter_context(nc.Block())

        def hs_(half):
            return slice(half * HALF, (half + 1) * HALF)

        def split(ap):
            return ap.rearrange("p (b t) -> p b t", t=SEQ)

        @block.sync
        def _(sp):
            for i in range(3):
                sp.dma_start(w_proj[:, 2 * i:2 * i + 2], d["w_proj"][:, 2 * i:2 * i + 2]).then_inc(s_ld_x[i], 16)
                sp.dma_start(patches[:, 2 * i:2 * i + 2], d["patches"][:, 2 * i:2 * i + 2]).then_inc(s_ld_x[i], 16)
                if i == 0:
                    sp.dma_start(cst[:, 0:P], d["cst"][:, 0:P]).then_inc(s_ld_center, 16)
                    sp.dma_start(wa0[:, 0:2], d["wa0"][:, 0:2]).then_inc(s_ld_a0k, 16)
            sp.dma_start(par[:], d["par"]).then_inc(s_ld_par, 16)
            sp.dma_start(posb[:], d["pos"]).then_inc(s_ld_pos, 16)
            sp.dma_start(cst[:, P:], d["cst"][:, P:]).then_inc(s_ld_cst, 16)
            sp.dma_start(wa0[:, 2:4], d["wa0"][:, 2:4]).then_inc(s_ld_a0v, 16)
            sp.dma_start(cw[:], d["cw"]).then_inc(s_ld_cn, 16)
            sp.dma_start(gw[:], d["gw"]).then_inc(s_ld_gc, 16)
            sp.dma_start(wr[:], d["wr"]).then_inc(s_ld_wr, 16)
            sp.dma_start(br[:], d["br"]).then_inc(s_ld_wr, 16)
            sp.dma_start(bdown[:], d["bdown"]).then_inc(s_ld_misc, 16)
            sp.dma_start(bup[:], d["bup"]).then_inc(s_ld_misc, 16)
            sp.dma_start(bgate[:], d["bgate"]).then_inc(s_ld_misc, 16)
            sp.dma_start(into[:, 4 * EC * E:], d["w_in"]).then_inc(s_ld_in, 16)
            sp.dma_start(wdown[:], d["wdown"]).then_inc(s_ld_down, 16)
            sp.wait_ge(s_u_psum, 2)
            sp.dma_start(wa1[:], d["wa1"]).then_inc(s_ld_a1, 16)
            sp.wait_ge(s_fs_ready, 1)
            for half in range(2):
                sp.dma_start(fs_dram[:, hs_(half)], fst[NX * half:NX * half + NX, :]).then_inc(s_fs_stored, 16)
            sp.wait_ge(s_fs_stored, 32)
            fs_rows = fs_dram.rearrange("(p j) n -> j p n", j=2)
            for f in range(XP // FP):
                if f >= FB:
                    sp.wait_ge(s_hw_ready, FP * (f - FB + 1))
                for j in range(2):
                    sp.dma_start(fb[XH * j:XH * j + XH, f % FB],
                                 fs_rows[j:j + 1, FP * f:FP * f + FP, :].to_broadcast([XH, FP, NT]))\
                      .then_inc(s_fb_ld[f % FB], 16)
            for i in STORES:
                if i in DVE_TILES:
                    sp.wait_ge(s_out_ready, DVE_TILES.index(i) + 1)
                else:
                    sp.wait_ge(s_out_act_ready, ACT_TILES.index(i) + 1)
                sp.dma_start(out[i * TT:(i + 1) * TT, :], ofin[:, i, :]).then_inc(s_stored, 16)
            sp.wait_ge(s_stored, 16 * TTN)

        cw1 = cw[:, 0:2 * E].rearrange("p (c n) -> p c n", c=EC)
        cw2 = cw[:, 2 * E:2 * E + 2 * P].rearrange("p (c n) -> p c n", c=EC)
        cw3 = cw[:, 2 * E + 2 * P:2 * E + 2 * P + 64]
        cw4 = cw[0:64, 2 * E + 2 * P + 64:2 * E + 2 * P + 64 + P]
        gw1 = gw[:, 0:2 * P].rearrange("p (c n) -> p c n", c=EC)
        gw2 = gw[:, 2 * P:2 * P + 64]
        gw3 = gw[0:64, 2 * P + 64:2 * P + 64 + P]

        def layer_in(layer):
            return ha if layer == 0 else hb

        def outputs_of(i):
            if i == PAIRS:
                return ((PAIRS - 2, 3 * P), (PAIRS - 1, 0))
            return ((i - 2, 3 * P),) if i >= 2 else ()

        def values_of(layer):
            return hb if layer == 0 else ha

        def pass_io(cy):
            return [(hb, res), (res, xc), (xc, res)][cy]

        @block.tensor
        def _(pe):
            def proj(w, x, bank, half_first=True):
                for half in range(2):
                    for c in range(EC):
                        for k in range(EC):
                            ins = pe.matmul(ps[:, bank + 2 * c + half, 0:HALF], w[:, k, c * P:(c + 1) * P],
                                            x[:, k, hs_(half)], start=(k == 0), stop=(k == EC - 1))
                return ins

            for k in range(KD):
                if k % 2 == 0:
                    pe.wait_ge(s_ld_x[k // 2], 32)
                for half in range(2):
                    for c in range(EC):
                        ins = pe.matmul(ps[:, 2 * c + half, 0:HALF], w_proj[:, k, c * P:(c + 1) * P],
                                        patches[:, k, hs_(half)], start=(k == 0), stop=(k == KD - 1))
                if k == 1:
                    pe.wait_ge(s_ld_center, 16)
                    pe.wait_ge(s_ld_a0k, 16)
                    for m in range(2):
                        for ci in range(EC):
                            for co_ in range(EC):
                                ins = pe.matmul(ps[:, 4 + m, ci * E + co_ * P:ci * E + co_ * P + P],
                                                wa0[:, m, co_, ci * P:(ci + 1) * P], C("center"), start=True, stop=True)
                        ins.then_inc(s_w_psum, 1)
            ins.then_inc(s_tok_psum, 1)

            def mean(n, half):
                pe.wait_ge(s_r_ready, 2 * n + half + 1)
                for c in range(EC):
                    ins = pe.matmul(ps[:, 6 + half, 0:HALF], C("all_mean"), res[:, c, hs_(half)],
                                    start=(c == 0), stop=(c == EC - 1))
                ins.then_inc(s_mean_psum, 1)

            def variance(n, half):
                pe.wait_ge(s_sqn_ready, 2 * n + half + 1)
                for c in range(EC):
                    ins = pe.matmul(ps[:, 3 * half, 0:HALF], C("all_mean"), sq[:, c, hs_(half)],
                                    start=(c == 0), stop=(c == EC - 1))
                ins.then_inc(s_var_psum, 1)

            def attention(layer):
                x = layer_in(layer)
                w = wa0 if layer == 0 else wa1

                def project_values(half):
                    if layer == 0:
                        pe.wait_ge(s_ld_a0v, 16)
                        pe.wait_ge(s_kcopy, half + 1)
                    else:
                        pe.wait_ge(s_qb_ready, 2 * half + 2)
                    for c in range(EC):
                        for k in range(EC):
                            ins = pe.matmul(ps[:, 2 + 4 * half + c if layer == 0 else 4 + half + 2 * c, 0:HALF],
                                            w[:, 2, k, c * P:(c + 1) * P], x[:, k, hs_(half)],
                                            start=(k == 0), stop=(k == EC - 1))
                    ins.then_inc(s_vt_psum, 1)

                def back(m):
                    pe.wait_ge(s_hrs_ready, m + 1)
                    pe.wait_ge(s_vt_ready, m + 1)
                    for t in (0, 2, 1, 3):
                        if t == 1:
                            pe.wait_ge(s_back_first, 2 * m + 2)
                        for c in range(EC):
                            ins = pe.matmul(ps[:, 4 * m + 2 * (t // 2) + c, (t % 2) * QT:(t % 2 + 1) * QT],
                                            C("head_back")[32 * t:32 * t + 32, c * P:(c + 1) * P],
                                            hrs[32 * t:32 * t + 32, m], start=True, stop=True)
                        ins.then_inc(s_back_psum if t % 2 else s_back_first, 1)

                if layer == 0:
                    pe.wait_ge(s_w_ready, 2)
                    pe.wait_ge(s_h0_ready, 4)
                    proj(wkc[:, 0], x, 0).then_inc(s_kraw, 1)
                    proj(wkc[:, 1], x, 4).then_inc(s_qraw, 1)
                    pe.wait_ge(s_ld_cst, 16)
                    for m, (psum, squares) in enumerate(((s_kvar, s_sq_k), (s_qvar, s_sq_q))):
                        pe.wait_ge(squares, 1)
                        pe.wait_ge(s_kcopy, m + 1)
                        buf = sq if m == 0 else sd
                        for t in range(4):
                            for c in range(EC):
                                ins = pe.matmul(ps[32 * t:32 * t + 32, 4 * m, 0:QT],
                                                C("head_rows")[:, 32 * c:32 * c + 32], buf[:, c, t * QT:(t + 1) * QT],
                                                start=(c == 0), stop=(c == EC - 1))
                        ins.then_inc(psum, 1)
                        project_values(m)
                    for m in range(2):
                        back(m)
                else:
                    pe.wait_ge(s_ld_a1, 16)
                    for half in range(2):
                        pe.wait_ge(s_x_ready, 3 + half)
                        for m, psum in ((1, s_k1_psum), (0, s_q1_psum)):
                            for c in range(EC):
                                for k in range(EC):
                                    ins = pe.matmul(ps[:, 4 * (1 - m) + 2 * c + half, 0:HALF],
                                                    wa1[:, m, k, c * P:(c + 1) * P], x[:, k, hs_(half)],
                                                    start=(k == 0), stop=(k == EC - 1))
                            ins.then_inc(psum, 1)
                    for half in range(2):
                        project_values(half)

                def scores(n, i):
                    if i == PAIRS // 2 - 1:
                        pe.wait_ge(s_q_ready, 2 * layer + 2)
                    if i == PAIRS // 2:
                        pe.wait_ge(s_kb2_ready, 2 + 2 * layer)
                    if i >= 2:
                        pe.wait_ge(s_s_read if layer == 0 else s_sub_ready, n - 1)
                    for j in range(2):
                        b = 2 * i + j
                        for c in range(EC):
                            ins = pe.matmul(ps[QP * j:QP * j + QP, 2 * (i % 2) + c, 0:HPC * SEQ],
                                            qt[:, c, b * SEQ:b * SEQ + QP], kb[:, c, :, b * SEQ:(b + 1) * SEQ],
                                            start=True, stop=True)
                    ins.then_inc(s_s_psum, 1)

                def values(n, i):
                    if i == 0:
                        pe.wait_ge(s_qhat_ready if layer == 0 else s_qb_ready, 2 + 2 * layer)
                    if n:
                        pe.wait_ge(s_vm_ready, n)
                    for j in range(2):
                        pe.wait_ge(s_xr_ready, 2 * n + j + 1)
                        for c in range(EC):
                            ins = pe.transpose(ps[0:TRI * SEQ, 6, j * E + c * P:j * E + c * P + P], xr[:, j, c, :], ident)
                    ins.then_inc(s_v_psum, 1)

                def turn(i):
                    n = n0 + i
                    if i == 0:
                        pe.wait_ge(s_vt_ready, 2 * layer + 2)
                    if n:
                        pe.wait_ge(s_pt_ready, n)
                    if i >= 3 or layer:
                        pe.wait_ge(s_turned, (PAIRS - 1) * layer + max(i - 2, 0))
                    if i < PAIRS:
                        pe.wait_ge(s_p_ready, n + 1)
                        for t in range(NTRI):
                            ins = pe.transpose(ps[0:TRI * SEQ, 4 + t // 3, (t % 3) * P:(t % 3 + 1) * P],
                                               psb[:, n % 2, TRI * t:TRI * t + TRI, :], ident)
                    for o, at in outputs_of(i):
                        pe.wait_ge(s_o_ready, n0 + o + 1)
                        for c in range(EC):
                            ins = pe.transpose(ps[:, 4 + c, at:at + P], osb[:, (n0 + o) % 2, c * P:(c + 1) * P], ident)
                    ins.then_inc(s_turn_psum, 1)

                def weigh(n):
                    pe.wait_ge(s_pt_ready, n + 1)
                    pe.wait_ge(s_vm_ready, n + 1)
                    if n:
                        pe.wait_ge(s_o_ready, n)
                    for j in range(2):
                        for t in range(NTRI):
                            a, b_ = TRI * HD * t, min(TRI * HD * (t + 1), E)
                            ins = pe.matmul(ps[QP * j:QP * j + QP, 7, a:b_], pt[:, n % 2, t, QP * j:QP * j + QP],
                                            vm[:, n % 2, j, a:b_], start=True, stop=True)
                    ins.then_inc(s_o_psum, 1)

                def project_out(half):
                    for c in range(EC):
                        for k in range(EC):
                            ins = pe.matmul(ps[:, 2 * half + c, 0:HALF], w[:, 3, k, c * P:(c + 1) * P],
                                            cx[:, k, hs_(half)], start=(k == 0), stop=(k == EC - 1))
                    ins.then_inc(s_u_psum, 1)

                n0 = PAIRS * layer
                values(n0, 0)
                pe.wait_ge(s_kb_ready, 2 * layer + 2)
                pe.wait_ge(s_q_ready, 2 * layer + 1)
                scores(n0, 0)
                for i in range(PAIRS + 2):
                    if i >= 1:
                        turn(i - 1)
                    if i + 1 < PAIRS:
                        scores(n0 + i + 1, i + 1)
                    if i == PAIRS:
                        pe.wait_ge(s_s_read if layer == 0 else s_sub_ready, n0 + PAIRS - 1)
                        project_out(0)
                    if 1 <= i <= PAIRS:
                        weigh(n0 + i - 1)
                    if 1 <= i < PAIRS:
                        values(n0 + i, i)
                    if i == PAIRS:
                        mean(2 * layer, 0)
                pe.wait_ge(s_turned, (PAIRS - 1) * (layer + 1))
                project_out(1)
                variance(2 * layer, 0)
                mean(2 * layer, 1)
                variance(2 * layer, 1)

            attention(0)

            def global_net(layer):
                if layer == 1:
                    pe.wait_ge(s_ld_gc, 16)
                    pe.wait_ge(s_gsum_ready, 1)
                    pe.wait_ge(s_l1r, EC)
                    for k in range(EC):
                        ins = pe.matmul(ps[:, 1, 320:320 + B], gw1[:, k, :], gsum[:, k, :],
                                        start=(k == 0), stop=(k == EC - 1))
                    ins.then_inc(s_g1p, 1)
                elif layer == 2:
                    pe.wait_ge(s_g1r, 1)
                    pe.matmul(ps[0:64, 1, 336:336 + B], gw2, gg1[:], start=True, stop=True).then_inc(s_g2p, 1)
                else:
                    pe.wait_ge(s_g2r, 1)
                    pe.matmul(ps[:, 1, 352:352 + B], gw3, gg2[:], start=True, stop=True).then_inc(s_g3p, 1)

            pe.wait_ge(s_ld_cn, 16)
            for cy in range(CYCLES):
                xin, _ = pass_io(cy)
                for half in range(2):
                    u = 2 * cy + half
                    if cy == 0:
                        pe.wait_ge(s_x_ready, half + 1)
                    else:
                        pe.wait_ge(s_g3r, 1)
                    for k in range(EC):
                        if cy > 0:
                            pe.wait_ge(s_f_ready, EC * (u - 2) + k + 1)
                        for c in range(EC):
                            ins = pe.matmul(ps[:, 4 * half + c, 0:HALF], cw1[:, k, c * P:(c + 1) * P],
                                            xin[:, k, hs_(half)], start=(k == 0), stop=(k == EC - 1))
                            if k == EC - 1:
                                ins.then_inc(s_l1p, 1)
                if cy == 0:
                    global_net(1)
                for half in range(2):
                    for k in range(EC):
                        pe.wait_ge(s_l1r, EC * (2 * cy + half) + k + 1)
                        ins = pe.matmul(ps[:, 4 * half + 2, 0:HALF], cw2[:, k, :], g1[:, k, hs_(half)],
                                        start=(k == 0), stop=(k == EC - 1))
                    ins.then_inc(s_l2p, 1)
                    if cy == 0:
                        global_net(2 + half)
                for half in range(2):
                    pe.wait_ge(s_l2r, 2 * cy + half + 1)
                    pe.matmul(ps[0:64, 4 * half + 3, 0:HALF], cw3, g2[:, hs_(half)], start=True, stop=True)\
                      .then_inc(s_l3p, 1)
                for half in range(2):
                    pe.wait_ge(s_l3r, 2 * cy + half + 1)
                    pe.matmul(ps[:, 4 * half, 0:HALF], cw4, g3[:, hs_(half)], start=True, stop=True)\
                      .then_inc(s_l4p, 1)
            for half in range(2):
                mean(1, half)
            for half in range(2):
                variance(1, half)
            attention(1)

            both = C("same_expert", NX)

            def route(step):
                if step == "scores":
                    pe.wait_ge(s_sc_ready, 1)
                    for i in range(TTN // 2):
                        ins = pe.transpose(ps[:, 3, i * TT:(i + 1) * TT],
                                           sc[:, i, :, :].rearrange("p h e -> p (h e)"), ident[0:TT, 0:TT])
                    ins.then_inc(s_tr_psum, 1)
                elif step == "shift":
                    pe.wait_ge(s_srt_ready, 1)
                    pe.matmul(ps[0:NX, 2, 0:HALF], ident[:, NX:P], srt[:], start=True, stop=True).then_inc(s_sh_psum, 1)
                elif step == "sums":
                    pe.wait_ge(s_st_ready, 1)
                    pe.matmul(ps[:, 1, 0:2 * NG], both, st[:], start=True, stop=True).then_inc(s_st_psum, 1)
                elif step == "groups":
                    pe.wait_ge(s_dg_ready, 1)
                    for j, bank in enumerate((0, 2)):
                        pe.matmul(ps[:, bank, 0:HALF], C("ones", NX),
                                  dg[:].rearrange("p g e -> p (g e)")[:, hs_(j)], start=True, stop=True)\
                          .then_inc(s_g_psum, 1)
                elif step == "selected":
                    pe.wait_ge(s_d_ready, 2)
                    pe.matmul(ps[:, 1, 0:NG], C("same_expert"), sel[:], start=True, stop=True).then_inc(s_d_psum, 1)
                elif step == "counts":
                    pe.wait_ge(s_cnt_ready, nk)
                    pe.matmul(ps[0:NX, 2, 0:nk], C("same_expert")[:, 0:NX], cnt[:, 0:nk], start=True, stop=True)
                    pe.matmul(ps[NX:P, 2, 0:nk], C("same_expert")[:, NX:P], cnt[:, 0:nk], start=True, stop=False)
                    pe.matmul(ps[NX:P, 2, 0:nk], ident[0:NX, 0:NX], cnt[0:NX, nk:2 * nk], start=False, stop=True)\
                      .then_inc(s_cnt_psum, 1)
                elif step == "total":
                    pe.wait_ge(s_mk_ready, 1)
                    pe.matmul(ps[:, 3, 0:HALF], C("same_half"), msc[:], start=True, stop=True).then_inc(s_sum_psum, 1)

            def logits(half):
                pe.wait_ge(s_x_ready, 5 + half)
                for i in range(half * TTN // 2, (half + 1) * TTN // 2):
                    for k in range(EC):
                        ins = pe.matmul(ps[0:TT, 2, i * NX:(i + 1) * NX], ha[:, k, i * TT:(i + 1) * TT], wr[:, k, :],
                                        start=(k == 0), stop=(k == EC - 1))
                ins.then_inc(s_lg_psum, 1)

            pe.wait_ge(s_ld_wr, 32)
            logits(0)

            for u in range(WU):
                pe.wait_ge(s_whi_ready, u + 1)
                pe.wait_ge(s_wlo_ready, u + 1)
                if u >= 2:
                    pe.wait_ge(s_ug_ready, u - 1)
                for half in range(2):
                    if u == 0:
                        if half:
                            logits(1)
                        pe.wait_ge(s_xhi_ready, half + 1)
                        pe.wait_ge(s_xlo_ready, half + 1)
                    for step, at in TURN.items():
                        if at == 2 * u + half:
                            route(step)
                    for k in range(EC):
                        for w_part, x_part in ((0, x_hi), (0, x_lo), (1, x_hi)):
                            ins = pe.matmul(ps[:, 4 + 2 * (u % 2) + half, 0:HALF],
                                            w_parts[:, u % WS, w_part, k * P:(k + 1) * P], x_part[:, k, hs_(half)],
                                            start=(k == 0 and w_part == 0 and x_part is x_hi),
                                            stop=(k == EC - 1 and w_part == 1))
                ins.then_inc(s_ug_psum, 1)
            for step, at in TURN.items():
                if at >= 2 * WU:
                    route(step)

            pe.wait_ge(s_fs_ready, 1)
            pe.wait_ge(s_ld_misc, 48)
            for p in range(XP):
                pe.wait_ge(s_whi_ready, WU + p + 1)
                pe.wait_ge(s_wlo_ready, WU + p + 1)
                pe.wait_ge(s_hhi_ready, p + 1)
                pe.wait_ge(s_hlo_ready, p + 1)
                for half in range(2):
                    for c in range(EC):
                        for w_part, h_part in ((0, 0), (0, 1), (1, 0)):
                            ins = pe.matmul(ps[:, 2 * half + c, 0:HALF],
                                            w_parts[:, (WU + p) % WS, w_part, c * P:(c + 1) * P],
                                            h_parts[:, p % HS, h_part, hs_(half)],
                                            start=(p == 0 and w_part == 0 and h_part == 0), stop=False)
                        if p == XP - 1:
                            ins = pe.matmul(ps[:, 2 * half + c, 0:HALF],
                                            bdown[NX * half:NX * half + NX, c * P:(c + 1) * P],
                                            fst[NX * half:NX * half + NX, :], start=False, stop=True)
                    if p == XP - 1:
                        ins.then_inc(s_y_done, 1)
                if p < XP - 1:
                    ins.then_inc(s_y_psum, 1)
            for i in range(TTN):
                if i % (TTN // 2) == 0:
                    pe.wait_ge(s_y_ready, 2 * i // TTN + 1)
                for c in range(EC):
                    ins = pe.transpose(ps[0:TT, 4 + i // 2, (i % 2) * E + c * P:(i % 2) * E + (c + 1) * P],
                                       res[:, c, i * TT:(i + 1) * TT], ident)
                if i % 2:
                    ins.then_inc(s_yt_psum, 1)

        @block.scalar
        def _(act):
            act.preload_act_table(ACT.Sqrt)
            act.memzero(qt[:, :, NT:NT + QP]).then_inc(s_act_n, 1)
            for m in range(2):
                act.wait_ge(s_w_psum, m + 1)
                act.activation(wkc[:, m].rearrange("p c n -> p (c n)"), ps[:, 4 + m, :], ACT.Copy)\
                   .then_inc(s_w_ready, 1)

            def bank4(first, half=None):
                return ps[:, first:first + 4, 0:HALF].rearrange("p (c h) n -> p c h n", c=EC)

            def halves(x):
                return x[:, :, 0:NT].rearrange("p c (h n) -> p c h n", h=2)

            def square(n, half):
                act.wait_ge(s_xc_ready, 2 * n + half + 1)
                act.activation(sq[:, :, hs_(half)], xc[:, :, hs_(half)], ACT.Square).then_inc(s_sqn_ready, 1)

            def deviation(n, half):
                act.wait_ge(s_var_psum, 2 * n + half + 1)
                act.activation(sd[:, 0, hs_(half)], ps[:, 3 * half, 0:HALF], ACT.Sqrt, bias=C("eps"))\
                   .then_inc(s_sdn_ready, 1)

            def split_weights(u):
                if u >= WS:
                    if u - WS < WU:
                        act.wait_ge(s_ug_psum, u - WS + 1)
                    else:
                        act.wait_ge(s_y_psum, u - WS - WU + 1)
                w_ = w_in[:, u].rearrange("p c n -> p (c n)") if u < WU else wdown[:, u - WU]
                act.activation(w_parts[:, u % WS, 0], w_, ACT.Copy).then_inc(s_whi_ready, 1)

            def attention(layer):
                def spread_keys(half, first, last):
                    for h in range(first, last):
                        for c in range(EC):
                            if layer == 0:
                                ins = act.activation(kb[:, c, h, hs_(half)], kc[:, c, hs_(half)], ACT.Identity,
                                                     bias=scal[:, 1, h:h + 1], scale=scal[:, 0, h:h + 1])
                            else:
                                ins = act.activation(kb[:, c, h, hs_(half)], kc[:, c, hs_(half)], ACT.Copy,
                                                     scale=C("head_of")[:, h:h + 1])
                    return ins

                if layer == 0:
                    act.wait_ge(s_ld_par, 16)
                    act.wait_ge(s_ld_cst, 16)
                    act.wait_ge(s_kcopy, 1)
                    act.activation(sq, kc[:], ACT.Square).then_inc(s_sq_k, 1)
                    act.wait_ge(s_kcopy, 2)
                    act.activation(sd, cx[:], ACT.Square).then_inc(s_sq_q, 1)
                    for m, psum in enumerate((s_kvar, s_qvar)):
                        act.wait_ge(psum, 1)
                        act.activation(hsd[:, m], ps[:, 4 * m, 0:QT], ACT.Sqrt, bias=C("eps")).then_inc(s_hsd_ready, 1)
                    act.wait_ge(s_scal_ready, 1)
                    act.wait_ge(s_khat_ready, 1)
                    spread_keys(0, DVE_HEADS, HPC).then_inc(s_kb_ready, 1)
                    for half in range(2):
                        act.wait_ge(s_qhat_ready, half + 1)
                        act.activation(qt[:, :, hs_(half)], cx[:, :, hs_(half)], ACT.Identity, bias=par_col("qln_b"),
                                       scale=par_col("qln_w")).then_inc(s_q_ready, 1)
                else:
                    for half in range(2):
                        for m, (psum, bias, buf) in enumerate(((s_k1_psum, "bk", kc), (s_q1_psum, "bq", cx))):
                            act.wait_ge(psum, half + 1)
                            for c in range(EC):
                                ins = act.activation(buf[:, c, hs_(half)], ps[:, 4 * m + 2 * c + half, 0:HALF],
                                                     ACT.Identity, bias=par_col(bias + ("1" if c else "")))
                            ins.then_inc(s_qb_ready, 1)
                    act.wait_ge(s_khat_ready, 3)
                    spread_keys(0, DVE_HEADS, HPC).then_inc(s_kb_ready, 1)
                n0 = PAIRS * layer

                def exps(n):
                    act.wait_ge(s_sub_ready, n + 1)
                    if n >= 2:
                        act.wait_ge(s_turn_psum, n - 1 + layer)
                        act.wait_ge(s_rs_done, n - 1)
                    act.activation(psb[:, n % 2, 0:HEADS, :], ssb[:, n % 2], ACT.Exp, scale=0.25)\
                       .then_inc(s_p_ready, 1)

                def keep_turned(i):
                    n = n0 + i
                    act.wait_ge(s_turn_psum, n + layer + 1)
                    if i < PAIRS:
                        if n >= 2:
                            act.wait_ge(s_o_psum, n - 1)
                        ins = act.activation(pt[:, n % 2].rearrange("p (a t) q -> p a (t q)", a=2),
                                             ps[0:TRI * SEQ, 4:6, 0:3 * P], ACT.Copy)
                        ins.then_inc(s_pt_ready, 1)
                    for o, at in outputs_of(i):
                        for c in range(EC):
                            dst = cx[:, c, 2 * o * SEQ:2 * (o + 1) * SEQ].rearrange("p (j t) -> p j t", j=2)
                            src = ps[:, 4 + c, at:at + P].rearrange("p (j q) -> p j q", j=2)[:, :, 0:SEQ]
                            if layer == 0:
                                ins = act.activation(dst, src, ACT.Copy)
                            else:
                                ins = act.activation(dst, src, ACT.Identity, bias=par_col("bv1" if c else "bv"))
                    if i >= 2:
                        ins.then_inc(s_turned, 1)

                def keep_values(n):
                    act.wait_ge(s_v_psum, n + 1)
                    if n >= 2:
                        act.wait_ge(s_o_psum, n - 1)
                    act.activation(vm[:, n % 2].rearrange("p j e -> p (j e)"), ps[0:TRI * SEQ, 6, :], ACT.Copy)\
                       .then_inc(s_vm_ready, 1)

                for i in range(PAIRS + 2):
                    if i >= 1:
                        keep_turned(i - 1)
                    if i == layer:
                        act.wait_ge(s_khat_ready, 2 * layer + 2)
                    if layer <= i < 3:
                        mine = HPC - POOL_HEADS[layer]
                        steps = 3 - layer
                        ins = spread_keys(1, mine * (i - layer) // steps, mine * (i - layer + 1) // steps)
                        if i == 2:
                            ins.then_inc(s_kb2_ready, 1)
                    if i < PAIRS:
                        exps(n0 + i)
                        keep_values(n0 + i)
                act.preload_act_table(ACT.Sqrt)
                for half in range(2):
                    square(2 * layer, half)
                    if layer == 1 and half == 0:
                        act.wait_ge(s_ld_in, 16)
                        act.wait_ge(s_ld_down, 16)
                        for u in range(AHEAD):
                            split_weights(u)
                    deviation(2 * layer, half)

            attention(0)

            def global_net(layer):
                if layer == 1:
                    act.wait_ge(s_g1p, 1)
                    act.activation(gg1[:], ps[:, 1, 320:320 + B], ACT.Gelu, bias=par_col("gc_b1"), scale=1.0 / SEQ)\
                       .then_inc(s_g1r, 1)
                elif layer == 2:
                    act.wait_ge(s_g2p, 1)
                    act.activation(gg2[:], ps[0:64, 1, 336:336 + B], ACT.Gelu, bias=par_col("gc_b2", 64))\
                       .then_inc(s_g2r, 1)
                else:
                    act.wait_ge(s_g3p, 1)
                    act.wait_ge(s_pool_ready, 1)
                    act.activation(gth[:], ps[:, 1, 352:352 + B], ACT.Tanh, bias=gco[:, 1:2], scale=0.5)\
                       .then_inc(s_g3r, 1)

            for cy in range(CYCLES):
                for half in range(2):
                    for c in range(EC):
                        act.wait_ge(s_l1p, EC * (2 * cy + half) + c + 1)
                        act.activation(g1[:, c, hs_(half)], ps[:, 4 * half + c, 0:HALF], ACT.Gelu,
                                       bias=par_col("cn_b11" if c else "cn_b1")).then_inc(s_l1r, 1)
                if cy == 0:
                    global_net(1)
                for half in range(2):
                    act.wait_ge(s_l2p, 2 * cy + half + 1)
                    act.activation(g2[:, hs_(half)], ps[:, 4 * half + 2, 0:HALF], ACT.Gelu, bias=par_col("cn_b2"))\
                       .then_inc(s_l2r, 1)
                    if cy == 0:
                        global_net(2 + half)
                for half in range(2):
                    act.wait_ge(s_l3p, 2 * cy + half + 1)
                    act.activation(g3[:, hs_(half)], ps[0:64, 4 * half + 3, 0:HALF], ACT.Gelu,
                                   bias=par_col("cn_b3", 64)).then_inc(s_l3r, 1)
                for half in range(2):
                    act.wait_ge(s_l4p, 2 * cy + half + 1)
                    act.activation(th[:, hs_(half)], ps[:, 4 * half, 0:HALF], ACT.Tanh, bias=gco[:, 0:1], scale=0.5)\
                       .then_inc(s_th_ready, 1)
            act.preload_act_table(ACT.Sqrt)
            for half in range(2):
                square(1, half)
            for half in range(2):
                deviation(1, half)
            attention(1)
            for half in range(2):
                act.wait_ge(s_x_ready, 5 + half)
                act.activation(x_hi[:, :, hs_(half)], ha[:, :, hs_(half)], ACT.Copy).then_inc(s_xhi_ready, 1)

            act.wait_ge(s_ld_misc, 48)
            act.preload_act_table(ACT.Exp)
            split_weights(AHEAD)
            act.wait_ge(s_lg_sub, 1)
            act.activation(sc[:].rearrange("p i h e -> p h i e"), lg[:].rearrange("p (h i) e -> p h i e", h=2),
                           ACT.Exp).then_inc(s_lg_exp, 1)
            def split_hidden(p):
                act.wait_ge(s_hw_ready, p + 1)
                if p >= HS:
                    act.wait_ge(s_y_psum, p - HS + 1)
                act.activation(h_parts[:, p % HS, 0], hw[p % 3], ACT.Copy).then_inc(s_hhi_ready, 1)

            for u in range(WU):
                if u:
                    split_weights(u + AHEAD)
                p = u // 2
                if u == WU - 2:
                    for q in range(HEAD):
                        split_hidden(q)
                act.wait_ge(s_ug_psum, u + 1)
                if p >= 2:
                    act.wait_ge(s_hh_ready, p - 1)
                bank = 4 + 2 * (u % 2)
                if u % 2 == 0:
                    act.activation(uu[:, p % 2].rearrange("p (h n) -> p h n", h=2), ps[:, bank:bank + 2, 0:HALF],
                                   ACT.Silu, bias=bup[:, p:p + 1]).then_inc(s_ug_ready, 1)
                else:
                    act.activation(vv[:, p % 2].rearrange("p (h n) -> p h n", h=2), ps[:, bank:bank + 2, 0:HALF],
                                   ACT.Identity, bias=bgate[:, p:p + 1]).then_inc(s_ug_ready, 1)
            for p in range(XP):
                if p >= HEAD:
                    split_hidden(p)
                if AHEAD <= p + 1 < XP:
                    split_weights(WU + p + 1)
            act.preload_act_table(ACT.Sqrt)
            act.wait_ge(s_ag_ready, TTN)
            act.activation(sdf[:], ag[:, :, 1], ACT.Sqrt, bias=C("eps", TT)).then_inc(s_sdn_ready, 1)
            act.wait_ge(s_rsf_ready, 2)
            for i in ACT_TILES:
                act.activation(ofin[:, i], ps[0:TT, 4 + i // 2, (i % 2) * E:(i % 2 + 1) * E], ACT.Identity,
                               bias=nmr[:, i:i + 1], scale=rsf[:, i:i + 1]).then_inc(s_out_act_ready, 1)

        @block.gpsimd
        def _(pool):
            for j in range(2):
                pool.memset(psb[:, j, HEADS:NTRI * TRI, :], 0.0).then_inc(s_pool_n, 1)
            pool.wait_ge(s_ld_cst, 16)
            for layer in range(2):
                vt = values_of(layer)
                for i in range(PAIRS):
                    if layer and i == 1:
                        def blocks(x, half):
                            return x[:, :, hs_(half)].rearrange("p c (b t) -> p c b t", t=SEQ)

                        cosb = C("cos").unsqueeze(1).unsqueeze(1).to_broadcast([P, EC, B // 2, SEQ])
                        sinb = C("sin").unsqueeze(1).unsqueeze(1).to_broadcast([P, EC, B // 2, SEQ])
                        pool.wait_ge(s_qswap_ready, 1)
                        pool.tensor_tensor(blocks(xc, 0), blocks(xc, 0), sinb, ALU.mult).then_inc(s_rope_n, 1)
                        pool.tensor_tensor(blocks(cx, 1), blocks(cx, 1), cosb, ALU.mult).then_inc(s_rope_n, 1)
                        pool.wait_ge(s_rope_n, 2)
                        pool.tensor_tensor(qt[:, :, hs_(1)], cx[:, :, hs_(1)], xc[:, :, hs_(0)], ALU.add)\
                            .then_inc(s_q_ready, 1)
                    if i == 1 + layer and POOL_HEADS[layer]:
                        pool.wait_ge(s_khat_ready, 2 * layer + 2)
                        for h in range(HPC - POOL_HEADS[layer], HPC):
                            for c in range(EC):
                                if layer == 0:
                                    ins = pool.tensor_scalar(kb[:, c, h, hs_(1)], kc[:, c, hs_(1)], scal[:, 0, h:h + 1],
                                                             scal[:, 1, h:h + 1], ALU.mult, ALU.add)
                                else:
                                    ins = pool.tensor_scalar(kb[:, c, h, hs_(1)], kc[:, c, hs_(1)],
                                                             C("head_of")[:, h:h + 1], None, ALU.mult)
                        ins.then_inc(s_kb2_ready, 1)
                    if layer or i:
                        pool.wait_ge(s_v_psum, PAIRS * layer + i)
                    pool.wait_ge(s_vt_ready, 2 * layer + 1 + i // (PAIRS // 2))
                    for j in range(2):
                        b = 2 * i + j
                        rep = vt[:, :, b * SEQ:(b + 1) * SEQ].unsqueeze(2).to_broadcast([P, EC, TRI, SEQ])
                        own = C("v_mask").rearrange("p (k r) -> p k r", r=TRI).unsqueeze(3).to_broadcast([P, EC, TRI, SEQ])
                        pool.tensor_tensor(xr[:, j].rearrange("p k (r t) -> p k r t", r=TRI), rep, own, ALU.mult)\
                            .then_inc(s_xr_ready, 1)
            pool.wait_ge(s_ld_cst, 16)
            def split_weights(u):
                pool.wait_ge(s_whi_ready, u + 1)
                w_ = w_in[:, u].rearrange("p c n -> p (c n)") if u < WU else wdown[:, u - WU]
                pool.tensor_tensor(w_parts[:, u % WS, 1], w_, w_parts[:, u % WS, 0].bitcast(F32), ALU.subtract)\
                    .then_inc(s_wlo_ready, 1)

            for u in range(AHEAD):
                split_weights(u)
            pool.wait_ge(s_xhi_ready, 1)
            pool.tensor_tensor(x_lo[:, :, hs_(0)], ha[:, :, hs_(0)], x_hi[:, :, hs_(0)].bitcast(F32), ALU.subtract)\
                .then_inc(s_xlo_ready, 1)
            pool.wait_ge(s_x_ready, 6)
            pool.memset(sel[:], 0.0).then_inc(s_pool_n, 1)
            for i, (rows, first) in enumerate(((slice(0, NX), 0), (slice(NX, P), NG - NGH))):
                at = NT - NX + NX * first
                pool.wait_ge(s_pool_n, 3 + 3 * i)
                pool.memset(before[rows, 0:at], 1.0).then_inc(s_pool_n, 1)
                pool.tensor_copy(before[rows, at:at + NX], C("before")[rows, :]).then_inc(s_pool_n, 1)
                pool.memset(before[rows, at + NX:2 * NT - NX], 0.0).then_inc(s_pool_n, 1)
            pool.wait_ge(s_pool_n, 9)

            for u in range(WU):
                split_weights(u + AHEAD)
                if u % 2:
                    p = u // 2
                    pool.wait_ge(s_ug_ready, u + 1)
                    pool.tensor_tensor(hh[:, p], uu[:, p % 2], vv[:, p % 2], ALU.mult).then_inc(s_hh_ready, 1)
            for p in range(XP - AHEAD):
                split_weights(WU + p + AHEAD)

        @block.vector
        def _(v):
            marked = [0]

            def mark(ins):
                marked[0] += 1
                return ins.then_inc(s_dve_n, 1)

            def chain(ins):
                mark(ins)
                v.wait_ge(s_dve_n, marked[0])

            v.wait_ge(s_ld_par, 16)
            v.wait_ge(s_ld_pos, 16)
            v.wait_ge(s_pool_n, 2)
            chain(v.tensor_scalar(gco[:, 0:1], par_col("cn_b4"), 0.5, None, ALU.mult))
            v.tensor_scalar(gco[:, 1:2], par_col("gc_b3"), 0.5, None, ALU.mult).then_inc(s_pool_ready, 1)
            for c in range(EC):
                mark(v.tensor_scalar(posb[:, c], posb[:, c], par_col("b_proj1" if c else "b_proj"), None, ALU.add))
            v.wait_ge(s_dve_n, marked[0])
            v.wait_ge(s_tok_psum, 1)
            for c in range(EC):
                for half in range(2):
                    v.tensor_tensor(split(ha[:, c, hs_(half)]), split(ps[:, 2 * c + half, 0:HALF]),
                                    posb[:, c].unsqueeze(1).to_broadcast([P, B // 2, SEQ]), ALU.add)\
                     .then_inc(s_h0_ready, 1)

            def halves(x):
                return x[:, :, 0:NT].rearrange("p c (h n) -> p c h n", h=2)

            def center(n, half):
                v.wait_ge(s_mean_psum, 2 * n + half + 1)
                v.wait_ge(s_r_ready, 2 * n + half + 1)
                v.tensor_tensor(xc[:, :, hs_(half)], res[:, :, hs_(half)],
                                ps[:, 6 + half, 0:HALF].unsqueeze(1).to_broadcast([P, EC, HALF]), ALU.subtract)\
                 .then_inc(s_xc_ready, 1)

            def rescale(n, half, dst):
                v.wait_ge(s_sdn_ready, 2 * n + half + 1)
                chain(v.reciprocal(rs[:, 0, hs_(half)], sd[:, 0, hs_(half)]))
                v.wait_ge(s_xc_ready, 2 * n + half + 1)
                v.tensor_tensor(dst[:, :, hs_(half)], xc[:, :, hs_(half)],
                                rs[:, 0, hs_(half)].unsqueeze(1).to_broadcast([P, EC, HALF]), ALU.mult)\
                 .then_inc(s_x_ready, 1)

            def attention(layer):
                def keep_values_t(half):
                    v.wait_ge(s_vt_psum, 2 * layer + half + 1)
                    for c in range(EC):
                        ins = v.tensor_copy(values_of(layer)[:, c, hs_(half)],
                                            ps[:, 2 + 4 * half + c if layer == 0 else 4 + half + 2 * c, 0:HALF])
                    ins.then_inc(s_vt_ready, 1)

                if layer == 0:
                    v.wait_ge(s_ld_cst, 16)
                    for j, col in enumerate(("kln_w", "kln_b")):
                        ins = v.tensor_scalar(scal[:, j], C("head_of"), par_col(col), None, ALU.mult)
                    ins.then_inc(s_scal_ready, 1)
                    v.wait_ge(s_kraw, 1)
                    for c in range(EC):
                        for half in range(2):
                            ins = v.tensor_copy(kc[:, c, hs_(half)], ps[:, 2 * c + half, 0:HALF])
                    ins.then_inc(s_kcopy, 1)
                    v.wait_ge(s_qraw, 1)
                    for c in range(EC):
                        for half in range(2):
                            ins = v.tensor_copy(cx[:, c, hs_(half)], ps[:, 4 + 2 * c + half, 0:HALF])
                    ins.then_inc(s_kcopy, 1)
                    v.wait_ge(s_kcopy, 2)
                    keep_values_t(0)
                    for m in range(2):
                        v.wait_ge(s_hsd_ready, m + 1)
                        v.reciprocal(hrs[:, m], hsd[:, m]).then_inc(s_hrs_ready, 1)
                    keep_values_t(1)

                    def over_deviation(m, x_, done):
                        for half in range(2):
                            v.wait_ge(s_back_psum, 2 * m + half + 1)
                            v.tensor_tensor(x_[:, :, hs_(half)], x_[:, :, hs_(half)],
                                            ps[:, 4 * m + 2 * half:4 * m + 2 * half + 2, 0:HALF], ALU.mult)\
                             .then_inc(done, 1)

                    def spread_keys(first, last):
                        for h in range(first, last):
                            for c in range(EC):
                                ins = v.tensor_scalar(kb[:, c, h, hs_(0)], kc[:, c, hs_(0)], scal[:, 0, h:h + 1],
                                                      scal[:, 1, h:h + 1], ALU.mult, ALU.add)
                        return ins

                    over_deviation(0, kc, s_khat_ready)
                    v.wait_ge(s_scal_ready, 1)
                    v.wait_ge(s_khat_ready, 1)
                    spread_keys(0, 2)
                    over_deviation(1, cx, s_qhat_ready)
                    spread_keys(2, DVE_HEADS).then_inc(s_kb_ready, 1)
                else:
                    cosb = C("cos").unsqueeze(1).unsqueeze(1).to_broadcast([P, EC, B // 2, SEQ])
                    sinb = C("sin").unsqueeze(1).unsqueeze(1).to_broadcast([P, EC, B // 2, SEQ])

                    def blocks(x, half):
                        return x[:, :, hs_(half)].rearrange("p c (b t) -> p c b t", t=SEQ)

                    v.wait_ge(s_qb_ready, 1)
                    mark(v.stream_shuffle(xc[:, :, hs_(0)], kc[:, :, hs_(0)], SHUFFLE))
                    v.wait_ge(s_qb_ready, 2)
                    mark(v.stream_shuffle(sq[:, :, hs_(0)], cx[:, :, hs_(0)], SHUFFLE))
                    v.wait_ge(s_dve_n, marked[0] - 1)
                    mark(v.tensor_tensor(blocks(xc, 0), blocks(xc, 0), sinb, ALU.mult))
                    v.wait_ge(s_dve_n, marked[0] - 1)
                    mark(v.tensor_tensor(blocks(sq, 0), blocks(sq, 0), sinb, ALU.mult))
                    mark(v.tensor_tensor(blocks(kc, 0), blocks(kc, 0), cosb, ALU.mult))
                    mark(v.tensor_tensor(blocks(cx, 0), blocks(cx, 0), cosb, ALU.mult))
                    v.wait_ge(s_dve_n, marked[0] - 1)
                    v.tensor_tensor(kc[:, :, hs_(0)], kc[:, :, hs_(0)], xc[:, :, hs_(0)], ALU.add)\
                     .then_inc(s_khat_ready, 1)
                    v.wait_ge(s_dve_n, marked[0])
                    v.tensor_tensor(qt[:, :, hs_(0)], cx[:, :, hs_(0)], sq[:, :, hs_(0)], ALU.add)\
                     .then_inc(s_q_ready, 1)
                    keep_values_t(0)
                    v.wait_ge(s_khat_ready, 3)
                    v.wait_ge(s_qb_ready, 4)
                    v.stream_shuffle(xc[:, :, hs_(0)], cx[:, :, hs_(1)], SHUFFLE).then_inc(s_qswap_ready, 1)
                    for h in range(DVE_HEADS):
                        for c in range(EC):
                            ins = v.tensor_scalar(kb[:, c, h, hs_(0)], kc[:, c, hs_(0)],
                                                  C("head_of")[:, h:h + 1], None, ALU.mult)
                    ins.then_inc(s_kb_ready, 1)

                    def second_half():
                        v.wait_ge(s_qb_ready, 4)
                        mark(v.stream_shuffle(xc[:, :, hs_(1)], kc[:, :, hs_(1)], SHUFFLE))
                        v.wait_ge(s_dve_n, marked[0])
                        mark(v.tensor_tensor(blocks(xc, 1), blocks(xc, 1), sinb, ALU.mult))
                        chain(v.tensor_tensor(blocks(kc, 1), blocks(kc, 1), cosb, ALU.mult))
                        v.tensor_tensor(kc[:, :, hs_(1)], kc[:, :, hs_(1)], xc[:, :, hs_(1)], ALU.add)\
                         .then_inc(s_khat_ready, 1)

                n0 = PAIRS * layer

                def spread(a):
                    return a.unsqueeze(2).to_broadcast([P, HEADS, SEQ])

                def shift(n, i):
                    a = n % 2
                    pss = ps[:, 2 * a:2 * a + 2, 0:HPC * SEQ].rearrange("p c (h t) -> p c h t", t=SEQ)
                    sh = ssb[:, a].rearrange("p (c h) t -> p c h t", c=EC)
                    mv = mx[:, a].rearrange("p (c h) -> p c h", c=EC)
                    v.wait_ge(s_s_psum, n + 1)
                    if n >= 2:
                        v.wait_ge(s_p_ready, n - 1)
                    if layer == 0:
                        causal = C("causal").unsqueeze(1).unsqueeze(1).to_broadcast([P, EC, HPC, SEQ])
                        v.tensor_tensor(sh, pss, causal, ALU.add).then_inc(s_s_read, 1)
                    else:
                        mark(v.tensor_reduce(mv, pss, AX.X, ALU.max))
                    if layer == 0:
                        v.wait_ge(s_s_read, n + 1)
                        chain(v.tensor_reduce(mx[:, a], ssb[:, a], AX.X, ALU.max))
                        v.tensor_tensor(ssb[:, a], ssb[:, a], spread(mx[:, a]), ALU.subtract).then_inc(s_sub_ready, 1)
                    else:
                        v.wait_ge(s_dve_n, marked[0])
                        v.tensor_tensor(sh, pss, mv.unsqueeze(3).to_broadcast([P, EC, HPC, SEQ]), ALU.subtract)\
                         .then_inc(s_sub_ready, 1)

                def sums(n):
                    a = n % 2
                    v.wait_ge(s_p_ready, n + 1)
                    v.tensor_reduce(sm[:, a], psb[:, a, 0:HEADS, :], AX.X, ALU.add).then_inc(s_rs_done, 1)
                    v.wait_ge(s_rs_done, n + 1)
                    chain(v.reciprocal(rc[:, a], sm[:, a]))

                def keep_weighed(n):
                    a = n % 2
                    v.wait_ge(s_o_psum, n + 1)
                    if n >= 2:
                        v.wait_ge(s_turn_psum, n + layer + 1)
                    v.tensor_tensor(osb[:, a].rearrange("p (h d) -> p h d", d=HD),
                                    ps[:, 7, 0:E].rearrange("p (h d) -> p h d", d=HD),
                                    rc[:, a].unsqueeze(2).to_broadcast([P, HEADS, HD]), ALU.mult)\
                     .then_inc(s_o_ready, 1)

                def residual(half):
                    x = layer_in(layer)
                    v.wait_ge(s_u_psum, 2 * layer + half + 1)
                    for c in range(EC):
                        if layer == 0:
                            ins = v.tensor_tensor(res[:, c, hs_(half)], ps[:, 2 * half + c, 0:HALF], x[:, c, hs_(half)],
                                                  ALU.add)
                        else:
                            ins = v.scalar_tensor_tensor(res[:, c, hs_(half)], ps[:, 2 * half + c, 0:HALF],
                                                         par_col("bo1" if c else "bo"), x[:, c, hs_(half)],
                                                         ALU.add, ALU.add)
                    ins.then_inc(s_r_ready, 1)

                shift(n0, 0)
                if layer == 1:
                    keep_values_t(1)
                for i in range(PAIRS + 1):
                    if i >= 1:
                        sums(n0 + i - 1)
                    if i + 1 < PAIRS:
                        shift(n0 + i + 1, i + 1)
                    if i == 0 and layer == 1:
                        second_half()
                    if i == PAIRS:
                        residual(0)
                    if i >= 1:
                        keep_weighed(n0 + i - 1)
                center(2 * layer, 0)
                residual(1)
                center(2 * layer, 1)
                for half in range(2):
                    rescale(2 * layer, half, hb if layer == 0 else ha)

            attention(0)
            v.wait_ge(s_x_ready, 2)
            for c in range(EC):
                ins = v.tensor_reduce(gsum[:, c], split(hb[:, c, :]), AX.X, ALU.add)
            ins.then_inc(s_gsum_ready, 1)
            v.wait_ge(s_g3r, 1)
            chain(v.tensor_scalar(cg[:], gth[:], par_col("ar"), 0.7, ALU.mult, ALU.mult))
            mark(v.tensor_scalar(cg[:], cg[:], 0.1, None, ALU.add))
            chain(v.tensor_scalar(scal[:, 0, 0:1], par_col("ar"), 0.3, None, ALU.mult))
            for cy in range(CYCLES):
                xin, xout = pass_io(cy)
                for half in range(2):
                    u = 2 * cy + half
                    t_ = hs_(half)
                    v.wait_ge(s_th_ready, u + 1)
                    if cy > 0:
                        v.wait_ge(s_f_ready, EC * (u - 1))
                    cgb = cg[:, half * B // 2:(half + 1) * B // 2].unsqueeze(2).to_broadcast([P, B // 2, SEQ])
                    chain(v.scalar_tensor_tensor(split(co[:, t_]), split(th[:, t_]), scal[:, 0, 0:1], cgb,
                                                 ALU.mult, ALU.add))
                    for c, sign in enumerate(("sign", "minus_sign")):
                        mark(v.scalar_tensor_tensor(g1[:, c, t_], xin[:, 1 - c, t_], C(sign), co[:, t_],
                                                    ALU.mult, ALU.mult))
                    for c in range(EC):
                        v.wait_ge(s_dve_n, marked[0] - 1 + c)
                        v.tensor_tensor(xout[:, c, t_], xin[:, c, t_], g1[:, c, t_], ALU.add).then_inc(s_f_ready, 1)
                    if cy == CYCLES - 1:
                        v.wait_ge(s_f_ready, EC * (u + 1))
                        v.tensor_tensor(res[:, :, t_], res[:, :, t_], hb[:, :, t_], ALU.add).then_inc(s_r_ready, 1)
            for half in range(2):
                center(1, half)
            for half in range(2):
                rescale(1, half, hb)
            attention(1)

            v.wait_ge(s_xhi_ready, 2)
            v.wait_ge(s_xlo_ready, 1)
            v.tensor_tensor(x_lo[:, :, hs_(1)], ha[:, :, hs_(1)], x_hi[:, :, hs_(1)].bitcast(F32), ALU.subtract)\
             .then_inc(s_xlo_ready, 1)

            v.wait_ge(s_lg_psum, 2)
            v.wait_ge(s_ld_wr, 32)
            chain(v.tensor_tensor(lg[:], ps[0:TT, 2, 0:TTN * NX].rearrange("p (i e) -> p i e", e=NX),
                                  br[:].unsqueeze(1).to_broadcast([TT, TTN, NX]), ALU.add))
            chain(v.tensor_reduce(lm[:], lg[:], AX.X, ALU.max))
            v.tensor_tensor(lg[:], lg[:], lm[:].unsqueeze(2).to_broadcast([TT, TTN, NX]), ALU.subtract)\
             .then_inc(s_lg_sub, 1)
            v.wait_ge(s_lg_exp, 1)
            chain(v.tensor_reduce(ls[:].rearrange("p (i h) -> p i h", h=2), sc[:], AX.X, ALU.add))
            chain(v.reciprocal(lr[:], ls[:]))
            flat = sc[:].rearrange("p i h e -> p (i h) e")
            v.tensor_tensor(flat, flat, lr[:].unsqueeze(2).to_broadcast([TT, TTN, NX]), ALU.mult)\
             .then_inc(s_sc_ready, 1)
            v.wait_ge(s_tr_psum, 1)
            mark(v.tensor_copy(wk[:], ps[:, 3, 0:HALF]))
            v.tensor_copy(se[:], ps[:, 3, 0:HALF]).then_inc(s_se_ready, 1)
            v.wait_ge(s_dve_n, marked[0])
            quarter = HALF // 2
            up_, down_ = wk[:, 0:quarter], wk[:, quarter:HALF]
            back = srt[:, ::-1]
            for k in range(quarter // 8):
                for q_, s_ in ((up_, srt), (down_, back)):
                    v.wait_ge(s_dve_n, marked[0] - 1)
                    mark(v.max(s_[:, 8 * k:8 * k + 8], q_))
                if k < quarter // 8 - 1:
                    for q_, s_ in ((up_, srt), (down_, back)):
                        v.wait_ge(s_dve_n, marked[0] - 1)
                        mark(v.match_replace(q_, s_[:, 8 * k:8 * k + 8], q_, -1.0))
            v.wait_ge(s_dve_n, marked[0])
            far = 256
            near = HALF - far
            mark(v.tensor_tensor(alt[:, far:HALF], srt[:, 0:near], srt[:, far:HALF], ALU.max))
            chain(v.tensor_tensor(srt[:, 0:near], srt[:, 0:near], srt[:, far:HALF], ALU.min))
            src, dst = srt, alt
            for m in (128, 64, 32, 16, 8, 4, 2, 1):
                n = far if m >= near else HALF
                a = src[:, 0:n].rearrange("p (n two m) -> p n two m", two=2, m=m)
                b_ = dst[:, 0:n].rearrange("p (n two m) -> p n two m", two=2, m=m)
                mark(v.tensor_tensor(b_[:, :, 0, :], a[:, :, 0, :], a[:, :, 1, :], ALU.min))
                ins = v.tensor_tensor(b_[:, :, 1, :], a[:, :, 0, :], a[:, :, 1, :], ALU.max)
                if m == 1:
                    ins.then_inc(s_srt_ready, 1)
                    v.wait_ge(s_srt_ready, 1)
                    v.wait_ge(s_dve_n, marked[0])
                else:
                    chain(ins)
                src, dst = dst, src
            mark(v.tensor_copy(ma[:, 0:HALF][:, ::-1], srt[0:NX, :]))
            v.wait_ge(s_sh_psum, 1)
            ins = v.tensor_copy(ma[:, HALF:NT], ps[0:NX, 2, 0:HALF])
            ins.then_inc(s_m_ready, 1)
            v.wait_ge(s_m_ready, 1)
            v.wait_ge(s_dve_n, marked[0])
            top = NT - GROUP
            mark(v.tensor_tensor(mb[:, top:NT], ma[:, 0:GROUP], ma[:, top:NT], ALU.max))
            chain(v.tensor_tensor(ma[:, 0:GROUP], ma[:, 0:GROUP], ma[:, top:NT], ALU.min))
            src, dst = ma, mb
            for m in (256, 128, 64):
                a = src[:, 0:512].rearrange("p (n two m) -> p n two m", two=2, m=m)
                b_ = dst[:, 0:512].rearrange("p (n two m) -> p n two m", two=2, m=m)
                mark(v.tensor_tensor(b_[:, :, 0, :], a[:, :, 0, :], a[:, :, 1, :], ALU.min))
                chain(v.tensor_tensor(b_[:, :, 1, :], a[:, :, 0, :], a[:, :, 1, :], ALU.max))
                src, dst = dst, src
            blocks_ = src[:].rearrange("p (g n) -> p g n", n=GROUP)
            mark(v.tensor_reduce(st[:, 0:NG][:, ::-1], blocks_, AX.X, ALU.add))
            ins = v.tensor_reduce(st[:, NG:2 * NG][:, ::-1], blocks_, AX.X, ALU.min)
            ins.then_inc(s_st_ready, 1)
            v.wait_ge(s_dve_n, marked[0])
            v.tensor_tensor(dg[:], ident[0:NX, 0:NX].unsqueeze(1).to_broadcast([NX, NG, NX]),
                            st[:, 0:NG].unsqueeze(2).to_broadcast([NX, NG, NX]), ALU.mult).then_inc(s_dg_ready, 1)
            v.wait_ge(s_st_psum, 1)
            mark(v.tensor_copy(st2[:], ps[:, 1, 0:2 * NG]))
            mark(v.tensor_copy(st3[0:NX, :], ps[0:NX, 1, 0:NGH]))
            mark(v.tensor_copy(st3[NX:P, :], ps[NX:P, 1, NG - NGH:NG]))
            v.wait_ge(s_dve_n, marked[0])
            v.wait_ge(s_g_psum, 2)
            v.wait_ge(s_pool_n, 9)
            gall = ps[:, 0:3:2, 0:HALF]
            for g in range(NGH):
                v.tensor_scalar(junk[:].rearrange("p (j n) -> p j n", j=2), gall, st3[:, g:g + 1], None,
                                ALU.is_gt, ALU.add, accum_out=rank[:, g:g + 1]).then_inc(s_rank_ready, 1)
                at = NT - NX - NX * g
                earlier = before[:, at:at + NT].rearrange("p (j n) -> p j n", j=2)
                if g:
                    v.wait_ge(s_dve_n, marked[0])
                mark(v.scalar_tensor_tensor(junk2[:].rearrange("p (j n) -> p j n", j=2), gall, st3[:, g:g + 1], earlier,
                                            ALU.is_equal, ALU.mult, accum_out=rank[:, NGH + g:NGH + g + 1]))
                v.wait_ge(s_rank_ready, g + 1)
            v.wait_ge(s_dve_n, marked[0])
            chain(v.tensor_tensor(rank[:, 0:NGH], rank[:, 0:NGH], rank[:, NGH:2 * NGH], ALU.add))
            v.tensor_scalar(sel[0:NX, 0:NGH], rank[0:NX, 0:NGH], float(BUDGET), None, ALU.is_lt).then_inc(s_d_ready, 1)
            v.tensor_scalar(sel[NX:P, NGH:NG], rank[NX:P, 2 * NGH - NG:NGH], float(BUDGET), None, ALU.is_lt)\
             .then_inc(s_d_ready, 1)
            for k in range(nk):
                mark(v.tensor_scalar(gt[:, k], se[:], st2[:, NG + k:NG + k + 1], None, ALU.is_gt, ALU.add,
                                         accum_out=cnt[:, k:k + 1]))
                v.tensor_scalar(eq[:, k], se[:], st2[:, NG + k:NG + k + 1], None, ALU.is_equal, ALU.add,
                                accum_out=cnt[:, nk + k:nk + k + 1]).then_inc(s_cnt_ready, 1)
            v.wait_ge(s_d_psum, 1)
            mark(v.tensor_copy(sel2[:], ps[:, 1, 0:NG]))
            v.wait_ge(s_cnt_psum, 1)
            mark(v.tensor_copy(base[:], ps[:, 2, 0:nk]))
            v.wait_ge(s_dve_n, marked[0])
            mark(v.tensor_tensor(dsel[:, 0:nk], sel2[:, 0:nk], sel2[:, 1:NG], ALU.subtract))
            mark(v.tensor_scalar(mask[:], se[:], 0.0, sel2[:, nk:NG], ALU.mult, ALU.add))
            mark(v.tensor_scalar(mask2[:], se[:], 0.0, None, ALU.mult))
            v.wait_ge(s_dve_n, marked[0])
            for k in range(nk + 1):
                if k < nk:
                    v.wait_ge(s_dve_n, marked[0] - 1)
                    mark(v.tensor_tensor_scan(cum[:, k % 2], eq[:, k], C("ones")[:, 0:1].to_broadcast([P, HALF]),
                                              base[:, k:k + 1], ALU.add, ALU.mult))
                if k >= 1:
                    v.wait_ge(s_dve_n, marked[0] - (1 if k < nk else 0))
                    mark(v.scalar_tensor_tensor(mask2[:], ine[:, (k - 1) % 2], dsel[:, k - 1:k], mask2[:], ALU.mult, ALU.add))
                if k < nk:
                    v.wait_ge(s_dve_n, marked[0] - 1)
                    mark(v.scalar_tensor_tensor(mask[:], gt[:, k], dsel[:, k:k + 1], mask[:], ALU.mult, ALU.add))
                    v.wait_ge(s_dve_n, marked[0] - 1)
                    mark(v.scalar_tensor_tensor(ine[:, k % 2], cum[:, k % 2], float(GROUP * (k + 1)), eq[:, k],
                                                ALU.is_le, ALU.mult))
            v.wait_ge(s_dve_n, marked[0])
            chain(v.tensor_tensor(mask[:], mask[:], mask2[:], ALU.add))
            v.tensor_tensor(msc[:], mask[:], se[:], ALU.mult).then_inc(s_mk_ready, 1)
            v.wait_ge(s_sum_psum, 1)
            chain(v.tensor_scalar(rden[:], ps[:, 3, 0:HALF], 1e-6, None, ALU.add))
            chain(v.reciprocal(rden[:], rden[:]))
            v.wait_ge(s_mk_ready, 1)
            v.tensor_tensor(fst[:], msc[:], rden[:], ALU.mult).then_inc(s_fs_ready, 1)

            for p in range(XP + LAG):
                if p < XP:
                    v.wait_ge(s_hh_ready, p + 1)
                    v.wait_ge(s_fb_ld[p // FP % FB], 32 * (p // FP // FB + 1))
                    if p >= 3:
                        v.wait_ge(s_hlo_ready, p - 2)
                    v.tensor_tensor(hw[p % 3], hh[:, p], fb[:, p // FP % FB, p % FP], ALU.mult).then_inc(s_hw_ready, 1)
                if p >= LAG:
                    q = p - LAG
                    v.wait_ge(s_hhi_ready, q + 1)
                    v.tensor_tensor(h_parts[:, q % HS, 1], hw[q % 3], h_parts[:, q % HS, 0].bitcast(F32), ALU.subtract)\
                     .then_inc(s_hlo_ready, 1)
            for half in range(2):
                v.wait_ge(s_y_done, half + 1)
                v.tensor_tensor(res[:, :, hs_(half)], ps[:, 2 * half:2 * half + 2, 0:HALF], ha[:, :, hs_(half)], ALU.add)\
                 .then_inc(s_y_ready, 1)
            for i in range(TTN + 1):
                if i < TTN:
                    v.wait_ge(s_yt_psum, i // 2 + 1)
                    v.bn_stats(bn[:, i], ps[0:TT, 4 + i // 2, (i % 2) * E:(i % 2 + 1) * E]).then_inc(s_bn_ready, 1)
                if i >= 1:
                    v.wait_ge(s_bn_ready, i)
                    v.bn_aggr(ag[:, i - 1], bn[:, i - 1]).then_inc(s_ag_ready, 1)
            v.wait_ge(s_sdn_ready, 7)
            v.reciprocal(rsf[:], sdf[:]).then_inc(s_rsf_ready, 1)
            v.wait_ge(s_rsf_ready, 1)
            v.wait_ge(s_ag_ready, TTN)
            v.scalar_tensor_tensor(nmr[:], ag[:, :, 0], -1.0, rsf[:], ALU.mult, ALU.mult).then_inc(s_rsf_ready, 1)
            for i in DVE_TILES:
                v.tensor_scalar(ofin[:, i], ps[0:TT, 4 + i // 2, (i % 2) * E:(i % 2 + 1) * E], ag[:, i, 0:1],
                                rsf[:, i:i + 1], ALU.subtract, ALU.mult).then_inc(s_out_ready, 1)


def _layout(a):
    def chunks(w):
        return np.ascontiguousarray(w.reshape(-1, P, w.shape[1]).transpose(1, 0, 2))

    x = a["x"].reshape(B, 6, 16, 6, 16, 3).transpose(2, 4, 5, 0, 1, 3).reshape(768, NT)
    cols = {
        "kln_w": np.tile(a["L0_attn_kln_w"], HPC), "kln_b": np.tile(a["L0_attn_kln_b"], HPC),
        "qln_w": np.tile(a["L0_attn_qln_w"], HPC), "qln_b": np.tile(a["L0_attn_qln_b"], HPC),
        "b_proj": a["L0_tok_b_proj"], "cn_b1": a["L0_ffn_cn_b1"], "cn_b2": a["L0_ffn_cn_b2"],
        "cn_b3": a["L0_ffn_cn_b3"], "cn_b4": np.tile(a["L0_ffn_cn_b4"], P), "gc_b1": a["L0_ffn_gc_b1"],
        "gc_b2": a["L0_ffn_gc_b2"], "gc_b3": np.tile(a["L0_ffn_gc_b3"], P), "ar": np.tile(a["L0_ffn_adaptive_range"], P),
        "bq": a["L1_attn_bq"], "bk": a["L1_attn_bk"], "bv": a["L1_attn_bv"], "bo": a["L1_attn_bo"],
    }
    par = np.zeros((P, NPAR), np.float32)
    for name, v in cols.items():
        for c in range(-(-len(v) // P)):
            part = v[c * P:(c + 1) * P]
            par[:len(part), PCOL[name + ("1" if c else "")]] = part

    def top(w, rows=P):
        full = np.zeros((rows, w.shape[1]), np.float32)
        full[:w.shape[0]] = w
        return full

    cw = np.concatenate([chunks(a["L0_ffn_cn_w1"]).reshape(P, -1), chunks(a["L0_ffn_cn_w2"]).reshape(P, -1),
                         a["L0_ffn_cn_w3"], top(np.tile(a["L0_ffn_cn_w4"], (1, P)))], axis=1)
    gw = np.concatenate([chunks(a["L0_ffn_gc_w1"]).reshape(P, -1), a["L0_ffn_gc_w2"],
                         top(np.tile(a["L0_ffn_gc_w3"], (1, P)))], axis=1)

    def experts_in(w):
        return w.reshape(XP, 2, EC, P, XH).transpose(3, 0, 2, 1, 4).reshape(P, XP, E)

    return {
        "cst": CONST, "par": par, "patches": chunks(x), "w_proj": chunks(a["L0_tok_W_proj"].T),
        "pos": chunks(a["L0_tok_pos_emb"].T),
        "wa0": np.stack([chunks(a["L0_attn_Wk"]), chunks(a["L0_attn_Wq"]), chunks(a["L0_attn_Wv"].T),
                         chunks(a["L0_attn_Wu"].T)], axis=1),
        "wa1": np.stack([chunks(a["L1_attn_" + n]) for n in ("Wq", "Wk", "Wv", "Wo")], axis=1),
        "cw": cw, "gw": gw, "wr": chunks(a["L1_ffn_Wr"]), "br": np.tile(a["L1_ffn_br"][None, :], (TT, 1)),
        "bdown": np.tile(a["L1_ffn_bdown"], (2, 1)), "bup": a["L1_ffn_bup"].reshape(XP, P).T,
        "bgate": a["L1_ffn_bgate"].reshape(XP, P).T,
        "w_in": np.stack([experts_in(a["L1_ffn_Wup"]), experts_in(a["L1_ffn_Wgate"])], axis=2).reshape(P, WU * E),
        "wdown": a["L1_ffn_Wdown"].reshape(XP, P, E).transpose(1, 0, 2),
    }


def kernel(**inputs):
    import concourse.bacc as _bacc
    from concourse.bass_utils import run_bass_kernel_spmd as _run

    arrays = {k: np.ascontiguousarray(v) for k, v in _layout({k: np.asarray(v) for k, v in inputs.items()}).items()}
    nc = _bacc.Bacc("TRN2", target_bir_lowering=False, num_devices=1)
    d = {k: nc.dram_tensor(k + "_in", v.shape, F32, kind="ExternalInput").ap() for k, v in arrays.items()}
    out = nc.dram_tensor("out", (NT, E), F32, kind="ExternalOutput").ap()
    build(nc, d, out)
    r = _run(nc, [{k + "_in": v for k, v in arrays.items()}], core_ids=[0])
    return r.results[0]["out"].reshape(B, SEQ, E)
```
